# Optimizing a Trainium2 kernel written in Bass

```python
import numpy as np
import jax
import jax.numpy as jnp

def _softmax(x, axis=-1):
    return jax.nn.softmax(x, axis=axis)

def _gelu(x):
    return jax.nn.gelu(x, approximate=True)

def _silu(x):
    return jax.nn.silu(x)

def _sigmoid(x):
    return jax.nn.sigmoid(x)

def _layernorm(x, axis=-1, eps=1e-05):
    m = jnp.mean(x, axis=axis, keepdims=True)
    v = jnp.var(x, axis=axis, keepdims=True)
    return (x - m) / jnp.sqrt(v + eps)

def _scatter_add(tgt, idx, src, axis=0):
    return tgt.at[idx].add(src)

def _segment_sum(src, seg, n):
    return jax.ops.segment_sum(src, seg, n)
kernel_name = 'mk_decoder_postln_d4_seqx_r8_8fa359'

def setup_inputs(seed: int=0):
    np.random.seed(seed)
    _w = jnp.asarray

    def _rec_inputs():
        import jax
        import jax.numpy as jnp
        _rk = jax.random.key(seed)
        x = 7.22e-05 + 1 * jax.random.normal(jax.random.fold_in(_rk, 1), (8, 100, 128), jnp.float32)
        _lenS = 100 - jax.random.randint(jax.random.fold_in(_rk, 7), (8,), 0, max(1, 100 // 4) + 1, jnp.int32)
        _lenS2 = 1444 - jax.random.randint(jax.random.fold_in(_rk, 8), (8,), 0, max(1, 1444 // 4) + 1, jnp.int32)
        _ctx_1024P = jax.random.normal(jax.random.fold_in(_rk, 11), (8, 16, 128), jnp.float32)
        _ctx_1024c = jax.random.dirichlet(jax.random.fold_in(_rk, 511), 0.3 * jnp.ones((16,), jnp.float32), (8, 1444))
        _ctx_1024t = jnp.einsum('bsk,bkd->bsd', _ctx_1024c, _ctx_1024P)
        _ctx_1024t = _ctx_1024t * jax.lax.rsqrt(jnp.mean(jnp.square(_ctx_1024t)) + 1e-12) * 0.953939
        ctx_1024 = 4.13588e-05 + 0.999923 * (_ctx_1024t + 0.3 * jax.random.normal(jax.random.fold_in(_rk, 611), (8, 1444, 128), jnp.float32))
        _validS = jnp.arange(100)[None, :] < _lenS[:, None]
        _validS2 = jnp.arange(1444)[None, :] < _lenS2[:, None]
        _causal = jnp.tril(jnp.ones((100, 100), dtype=bool))
        mask_Bx1x1xS2_if1 = jnp.where(jnp.ones((8, 1, 1, 1444), dtype=bool), 1, 0).astype(jnp.int32)
        mask_BxS2_bf1 = jnp.ones((8, 1444), dtype=bool)
        return (x, ctx_1024, mask_Bx1x1xS2_if1, mask_BxS2_bf1)
    x, ctx_1024, mask_Bx1x1xS2_if1, mask_BxS2_bf1 = _rec_inputs()

    def _L0_attn_setup():
        import jax, jax.numpy as jnp
        import numpy as np
        N_HEADS = 16
        WINDOW = 32
        GLOBAL_IDX = np.array([0])

        def _global_local_mask(seq_len):
            i = jnp.arange(seq_len)[:, None]
            j = jnp.arange(seq_len)[None, :]
            g = jnp.asarray(GLOBAL_IDX)
            row_global = jnp.isin(jnp.arange(seq_len), g)
            allowed = (jnp.abs(i - j) <= WINDOW) | row_global[:, None] | row_global[None, :]
            return allowed
        key = jax.random.key(seed)
        ks = jax.random.split(key, 9)
        B, S, D = (1, 256, 128)
        w = 0.02
        return {'x': jax.random.normal(ks[0], (B, S, D), jnp.float32), 'Wq': jax.random.normal(ks[1], (D, D), jnp.float32) * w, 'bq': jnp.zeros((D,), jnp.float32), 'Wk': jax.random.normal(ks[2], (D, D), jnp.float32) * w, 'bk': jnp.zeros((D,), jnp.float32), 'Wv': jax.random.normal(ks[3], (D, D), jnp.float32) * w, 'bv': jnp.zeros((D,), jnp.float32), 'Wo': jax.random.normal(ks[4], (D, D), jnp.float32) * w, 'bo': jnp.zeros((D,), jnp.float32)}
    _L0_attn_all = _L0_attn_setup()
    _L0_attn_in = {k: v for k, v in _L0_attn_all.items() if k in ('Wq', 'bq', 'Wk', 'bk', 'Wv', 'bv', 'Wo', 'bo')}
    del _L0_attn_all

    def _L0_xattn_setup():
        import jax, jax.numpy as jnp
        import numpy as np
        HIDDEN = 128
        NUM_HEAD = 16
        HEAD_DIM = HIDDEN // NUM_HEAD

        def _split_heads(x):
            bs, seq, _ = x.shape
            return x.reshape(bs, seq, NUM_HEAD, HEAD_DIM).transpose(0, 2, 1, 3)
        key = jax.random.key(seed)
        ks = jax.random.split(key, 12)
        bs, seq = (4, 256)
        inp = {'srcQ': jax.random.normal(ks[0], (bs, seq, HIDDEN), jnp.float32), 'srcK': jax.random.normal(ks[1], (bs, seq, HIDDEN), jnp.float32), 'srcV': jax.random.normal(ks[2], (bs, seq, HIDDEN), jnp.float32), 'mask': jnp.ones((bs, 1, 1, seq), jnp.int32), 'Wq': jax.random.normal(ks[3], (HIDDEN, HIDDEN), jnp.float32) * 0.02, 'bq': jnp.zeros((HIDDEN,), jnp.float32), 'Wk': jax.random.normal(ks[4], (HIDDEN, HIDDEN), jnp.float32) * 0.02, 'bk': jnp.zeros((HIDDEN,), jnp.float32), 'Wv': jax.random.normal(ks[5], (HIDDEN, HIDDEN), jnp.float32) * 0.02, 'bv': jnp.zeros((HIDDEN,), jnp.float32), 'Wo': jax.random.normal(ks[6], (HIDDEN, HIDDEN), jnp.float32) * 0.02, 'bo': jnp.zeros((HIDDEN,), jnp.float32)}
        return inp
    _L0_xattn_all = _L0_xattn_setup()
    _L0_xattn_in = {k: v for k, v in _L0_xattn_all.items() if k in ('Wq', 'bq', 'Wk', 'bk', 'Wv', 'bv', 'Wo', 'bo')}
    del _L0_xattn_all

    def _L0_ffn_setup():
        import jax, jax.numpy as jnp
        import numpy as np
        E = 8
        D = 128
        H = 128
        K = 2
        key = jax.random.key(seed)
        k1, k2, k3, k4, k5, k6 = jax.random.split(key, 6)
        x = jax.random.normal(k1, (4, 128, D), dtype=jnp.float32)
        w1 = jax.random.uniform(k2, (E, D, H), jnp.float32, -1.0 / D, 1.0 / D)
        b1 = jax.random.uniform(k3, (E, H), jnp.float32, -1.0 / np.sqrt(D), 1.0 / np.sqrt(D))
        w2 = jax.random.uniform(k4, (E, H, D), jnp.float32, -1.0 / H, 1.0 / H)
        b2 = jax.random.uniform(k5, (E, D), jnp.float32, -1.0 / np.sqrt(H), 1.0 / np.sqrt(H))
        wg = jax.random.normal(k6, (D, E), dtype=jnp.float32) * 0.02
        return {'x': x, 'w1': w1, 'b1': b1, 'w2': w2, 'b2': b2, 'wg': wg}
    _L0_ffn_all = _L0_ffn_setup()
    _L0_ffn_in = {k: v for k, v in _L0_ffn_all.items() if k in ('w1', 'b1', 'w2', 'b2', 'wg')}
    del _L0_ffn_all

    def _L1_attn_setup():
        import jax, jax.numpy as jnp
        import numpy as np
        D_MODEL = 128
        D_INNER = 2 * D_MODEL
        D_STATE = 16
        D_CONV = 4
        DT_RANK = D_MODEL // 16
        D_FF = 2 * D_MODEL
        B, L = (4, 256)

        def layer_norm(x, w, b, eps=1e-05):
            mu = jnp.mean(x, axis=-1, keepdims=True)
            var = jnp.mean(jnp.square(x - mu), axis=-1, keepdims=True)
            return (x - mu) * jax.lax.rsqrt(var + eps) * w + b

        def mamba(x, in_proj_w, conv_w, conv_b, x_proj_w, dt_proj_w, dt_proj_b, A_log, Dp, out_proj_w):
            xz = jnp.einsum('bld,ed->ble', x, in_proj_w)
            xc, z = jnp.split(xz, 2, axis=-1)
            xp = jnp.pad(xc, ((0, 0), (D_CONV - 1, 0), (0, 0)))
            conv = conv_b
            for k in range(D_CONV):
                conv = conv + xp[:, k:k + xc.shape[1], :] * conv_w[:, k]
            xc = jax.nn.silu(conv)
            dbc = jnp.einsum('bld,ed->ble', xc, x_proj_w)
            dt_raw = dbc[..., :DT_RANK]
            Bm = dbc[..., DT_RANK:DT_RANK + D_STATE]
            Cm = dbc[..., DT_RANK + D_STATE:]
            dt = jax.nn.softplus(jnp.einsum('blr,dr->bld', dt_raw, dt_proj_w) + dt_proj_b)
            A = -jnp.exp(A_log)
            dA = jnp.exp(dt[..., None] * A)
            dBx = dt[..., None] * Bm[:, :, None, :] * xc[..., None]
            dA_t = jnp.moveaxis(dA, 1, 0)
            dBx_t = jnp.moveaxis(dBx, 1, 0)
            Cm_t = jnp.moveaxis(Cm, 1, 0)

            def step(h, inputs):
                dA_i, dBx_i, C_i = inputs
                h = dA_i * h + dBx_i
                y = jnp.einsum('bdn,bn->bd', h, C_i)
                return (h, y)
            h0 = jnp.zeros((xc.shape[0], D_INNER, D_STATE), xc.dtype)
            _, ys = jax.lax.scan(step, h0, (dA_t, dBx_t, Cm_t))
            y = jnp.moveaxis(ys, 0, 1) + xc * Dp
            y = y * jax.nn.silu(z)
            return jnp.einsum('ble,de->bld', y, out_proj_w)
        key = jax.random.key(seed)
        ks = jax.random.split(key, 16)
        s = 0.02
        inp = {'x': jax.random.normal(ks[0], (B, L, D_MODEL), jnp.float32), 'ln1_w': jnp.ones((D_MODEL,), jnp.float32), 'ln1_b': jnp.zeros((D_MODEL,), jnp.float32), 'in_proj_w': jax.random.normal(ks[1], (2 * D_INNER, D_MODEL), jnp.float32) * s, 'conv_w': jax.random.normal(ks[2], (D_INNER, D_CONV), jnp.float32) * 0.1, 'conv_b': jnp.zeros((D_INNER,), jnp.float32), 'x_proj_w': jax.random.normal(ks[3], (DT_RANK + 2 * D_STATE, D_INNER), jnp.float32) * s, 'dt_proj_w': jax.random.normal(ks[4], (D_INNER, DT_RANK), jnp.float32) * s, 'dt_proj_b': jax.random.uniform(ks[5], (D_INNER,), jnp.float32, -4.0, -2.0), 'A_log': jnp.log(jnp.broadcast_to(jnp.arange(1, D_STATE + 1, dtype=jnp.float32), (D_INNER, D_STATE))), 'D': jnp.ones((D_INNER,), jnp.float32), 'out_proj_w': jax.random.normal(ks[6], (D_MODEL, D_INNER), jnp.float32) * s, 'ln2_w': jnp.ones((D_MODEL,), jnp.float32), 'ln2_b': jnp.zeros((D_MODEL,), jnp.float32), 'ffn_w1': jax.random.normal(ks[7], (D_FF, D_MODEL), jnp.float32) * s, 'ffn_b1': jnp.zeros((D_FF,), jnp.float32), 'ffn_w2': jax.random.normal(ks[8], (D_MODEL, D_FF), jnp.float32) * s, 'ffn_b2': jnp.zeros((D_MODEL,), jnp.float32)}
        return inp
    _L1_attn_all = _L1_attn_setup()
    _L1_attn_in = {k: v for k, v in _L1_attn_all.items() if k in ('ln1_w', 'ln1_b', 'in_proj_w', 'conv_w', 'conv_b', 'x_proj_w', 'dt_proj_w', 'dt_proj_b', 'A_log', 'D', 'out_proj_w', 'ln2_w', 'ln2_b', 'ffn_w1', 'ffn_b1', 'ffn_w2', 'ffn_b2')}
    del _L1_attn_all

    def _L1_xattn_setup():
        import jax, jax.numpy as jnp
        import numpy as np
        key = jax.random.key(seed)
        ks = jax.random.split(key, 6)
        B, S, DK = (4, 256, 128)
        scale = 1.0 / np.sqrt(DK)
        return {'q': jax.random.normal(ks[0], (B, S, DK), jnp.float32), 'k': jax.random.normal(ks[1], (B, S, DK), jnp.float32), 'v': jax.random.normal(ks[2], (B, S, DK), jnp.float32), 'wq': jax.random.normal(ks[3], (DK, DK), jnp.float32) * scale, 'wk': jax.random.normal(ks[4], (DK, DK), jnp.float32) * scale, 'wv': jax.random.normal(ks[5], (DK, DK), jnp.float32) * scale}
    _L1_xattn_all = _L1_xattn_setup()
    _L1_xattn_in = {k: v for k, v in _L1_xattn_all.items() if k in ('wq', 'wk', 'wv')}
    del _L1_xattn_all

    def _L1_ffn_setup():
        import jax, jax.numpy as jnp
        import numpy as np
        DIM = 128

        def _reference_tuple_inner(x, W_r, W_k, W_v, mu_r, mu_k):
            B, T, C = x.shape
            x_prev = jnp.concatenate([jnp.zeros((B, 1, C), x.dtype), x[:, :-1, :]], axis=1)
            xr = mu_r * x + (1.0 - mu_r) * x_prev
            xk = mu_k * x + (1.0 - mu_k) * x_prev
            r = jax.nn.sigmoid(jnp.einsum('btc,dc->btd', xr, W_r))
            k = jnp.einsum('btc,dc->btd', xk, W_k)
            k_act = jnp.square(jax.nn.relu(k))
            out = r * jnp.einsum('btc,dc->btd', k_act, W_v)
            new_state = x[:, -1, :]
            return (out, new_state)
        key = jax.random.key(seed)
        ks = jax.random.split(key, 6)
        B, T, C = (8, 256, DIM)
        x = jax.random.normal(ks[0], (B, T, C), dtype=jnp.float32)
        s = 1.0 / np.sqrt(C)
        W_r = jax.random.uniform(ks[1], (C, C), jnp.float32, -s, s)
        W_k = jax.random.uniform(ks[2], (C, C), jnp.float32, -s, s)
        W_v = jax.random.uniform(ks[3], (C, C), jnp.float32, -s, s)
        mu_r = jax.random.uniform(ks[4], (C,), jnp.float32)
        mu_k = jax.random.uniform(ks[5], (C,), jnp.float32)
        return {'x': x, 'W_r': W_r, 'W_k': W_k, 'W_v': W_v, 'mu_r': mu_r, 'mu_k': mu_k}
    _L1_ffn_all = _L1_ffn_setup()
    _L1_ffn_in = {k: v for k, v in _L1_ffn_all.items() if k in ('W_r', 'W_k', 'W_v', 'mu_r', 'mu_k')}
    del _L1_ffn_all

    def _L2_attn_setup():
        import jax, jax.numpy as jnp
        import numpy as np
        NUM_HEADS = 16
        HIDDEN = 128
        HEAD_DIM = HIDDEN // NUM_HEADS

        def _rope_cos_sin(S, head_dim):
            inv = 1.0 / 10000.0 ** (jnp.arange(0, head_dim, 2, dtype=jnp.float32) / head_dim)
            t = jnp.arange(S, dtype=jnp.float32)
            ang = jnp.outer(t, inv)
            return (jnp.cos(ang), jnp.sin(ang))

        def _apply_rope(x, cos, sin):
            B, S, nh, hd = x.shape
            xr = x[..., 0::2]
            xi = x[..., 1::2]
            c = cos[None, :, None, :]
            s = sin[None, :, None, :]
            or_ = xr * c - xi * s
            oi_ = xr * s + xi * c
            return jnp.stack([or_, oi_], axis=-1).reshape(B, S, nh, hd)
        key = jax.random.key(seed)
        k1, k2, k3, k4, k5 = jax.random.split(key, 5)
        std = 1.0 / np.sqrt(HIDDEN)
        return {'x': jax.random.normal(k1, (2, 256, HIDDEN), dtype=jnp.float32), 'wq': jax.random.normal(k2, (HIDDEN, HIDDEN), dtype=jnp.float32) * std, 'wk': jax.random.normal(k3, (HIDDEN, HIDDEN), dtype=jnp.float32) * std, 'wv': jax.random.normal(k4, (HIDDEN, HIDDEN), dtype=jnp.float32) * std, 'wo': jax.random.normal(k5, (HIDDEN, HIDDEN), dtype=jnp.float32) * std}
    _L2_attn_all = _L2_attn_setup()
    _L2_attn_in = {k: v for k, v in _L2_attn_all.items() if k in ('wq', 'wk', 'wv', 'wo')}
    del _L2_attn_all

    def _L2_xattn_setup():
        import jax, jax.numpy as jnp
        import numpy as np
        DIM = 128
        DIM_LATENT = 128
        DIM_HEAD = 64
        HEADS = 16
        INNER = HEADS * DIM_HEAD

        def layernorm(x, g, b, eps=1e-05):
            m = jnp.mean(x, axis=-1, keepdims=True)
            v = jnp.mean((x - m) ** 2, axis=-1, keepdims=True)
            return (x - m) / jnp.sqrt(v + eps) * g + b

        def rmsnorm(x, gamma, eps=1e-08):
            n = jnp.linalg.norm(x, axis=-1, keepdims=True) * x.shape[-1] ** (-0.5)
            return x / jnp.maximum(n, eps) * gamma
        key = jax.random.key(seed)
        ks = jax.random.split(key, 8)
        b, n, m = (4, 512, 64)
        x = jax.random.normal(ks[0], (b, n, DIM), dtype=jnp.float32)
        latents = jax.random.normal(ks[1], (b, m, DIM_LATENT), dtype=jnp.float32)
        mask = jnp.ones((b, n), dtype=bool)
        s = 0.02
        return {'x': x, 'latents': latents, 'mask': mask, 'ln_x_g': jnp.ones((DIM,), jnp.float32), 'ln_x_b': jnp.zeros((DIM,), jnp.float32), 'ln_l_g': jnp.ones((DIM_LATENT,), jnp.float32), 'ln_l_b': jnp.zeros((DIM_LATENT,), jnp.float32), 'qn_g': jnp.ones((DIM_HEAD,), jnp.float32), 'kn_g': jnp.ones((DIM_HEAD,), jnp.float32), 'Wq': jax.random.normal(ks[2], (DIM_LATENT, INNER), jnp.float32) * s, 'Wkv': jax.random.normal(ks[3], (DIM, 2 * INNER), jnp.float32) * s, 'Wout': jax.random.normal(ks[4], (INNER, DIM_LATENT), jnp.float32) * s, 'bout': jnp.zeros((DIM_LATENT,), jnp.float32)}
    _L2_xattn_all = _L2_xattn_setup()
    _L2_xattn_in = {k: v for k, v in _L2_xattn_all.items() if k in ('ln_x_g', 'ln_x_b', 'ln_l_g', 'ln_l_b', 'qn_g', 'kn_g', 'Wq', 'Wkv', 'Wout', 'bout')}
    del _L2_xattn_all

    def _L2_ffn_setup():
        import jax, jax.numpy as jnp
        import numpy as np
        D_MODEL = 128
        EXPANSION = 4
        D_HIDDEN = D_MODEL * EXPANSION
        NUM_STAGES = int(np.log2(D_HIDDEN))

        def butterfly(y, weights, dim):
            lead = y.shape[:-1]
            for stage in range(weights.shape[0]):
                s = 2 ** stage
                nb = dim // (2 * s)
                yr = y.reshape(*lead, nb, 2, s)
                a = yr[..., 0, :]
                b = yr[..., 1, :]
                w = weights[stage].reshape(nb, s, 2, 2)
                na = w[..., 0, 0] * a + w[..., 0, 1] * b
                nb2 = w[..., 1, 0] * a + w[..., 1, 1] * b
                y = jnp.stack([na, nb2], axis=-2).reshape(*lead, dim)
            return y
        key = jax.random.key(seed)
        ks = jax.random.split(key, 6)
        B, S = (4, 256)
        x = jax.random.normal(ks[0], (B, S, D_MODEL), jnp.float32)
        W_exp = jax.random.normal(ks[1], (D_MODEL, D_HIDDEN), jnp.float32) * 0.02
        b_exp = jnp.zeros((D_HIDDEN,), jnp.float32)
        up_weights = jax.random.normal(ks[2], (NUM_STAGES, D_HIDDEN // 2, 2, 2), jnp.float32) * 0.02
        up_bias = jnp.zeros((D_HIDDEN,), jnp.float32)
        down_weights = jax.random.normal(ks[3], (NUM_STAGES, D_HIDDEN // 2, 2, 2), jnp.float32) * 0.02
        W_con = jax.random.normal(ks[4], (D_HIDDEN, D_MODEL), jnp.float32) * 0.02
        b_con = jnp.zeros((D_MODEL,), jnp.float32)
        down_bias = jnp.zeros((D_MODEL,), jnp.float32)
        return dict(x=x, W_exp=W_exp, b_exp=b_exp, up_weights=up_weights, up_bias=up_bias, down_weights=down_weights, W_con=W_con, b_con=b_con, down_bias=down_bias)
    _L2_ffn_all = _L2_ffn_setup()
    _L2_ffn_in = {k: v for k, v in _L2_ffn_all.items() if k in ('W_exp', 'b_exp', 'up_weights', 'up_bias', 'down_weights', 'W_con', 'b_con', 'down_bias')}
    del _L2_ffn_all

    def _L3_attn_setup():
        import jax, jax.numpy as jnp
        import numpy as np
        B, S, HID = (2, 256, 128)
        H = 16
        D = HID // H
        SPARSITY = 0.9

        def _sparse_attn(x, Wq, bq, Wk, bk, Wv, bv, Wo, bo):
            b, s, hid = x.shape
            d = hid // H

            def heads(y):
                return y.reshape(b, s, H, d).transpose(0, 2, 1, 3)
            Q = heads(x @ Wq + bq)
            K = heads(x @ Wk + bk)
            V = heads(x @ Wv + bv)
            scores = jnp.einsum('bhqd,bhkd->bhqk', Q, K) / np.sqrt(d)
            k_keep = int(s * (1.0 - SPARSITY))
            vals, idx = jax.lax.top_k(scores, k_keep)
            n = b * H * s
            rows = jnp.arange(n)[:, None]
            sparse = jnp.zeros((n, s), scores.dtype).at[rows, idx.reshape(n, k_keep)].set(vals.reshape(n, k_keep)).reshape(b, H, s, s)
            attn = jax.nn.softmax(sparse, axis=-1)
            out = jnp.einsum('bhqk,bhkd->bhqd', attn, V)
            out = out.transpose(0, 2, 1, 3).reshape(b, s, hid)
            return out @ Wo + bo
        key = jax.random.key(seed)
        ks = jax.random.split(key, 5)
        sc = 1.0 / np.sqrt(HID)
        inp = {'x': jax.random.normal(ks[0], (B, S, HID), jnp.float32)}
        for i, name in enumerate(['q', 'k', 'v', 'o']):
            inp[f'W{name}'] = jax.random.normal(ks[i + 1], (HID, HID), jnp.float32) * sc
            inp[f'b{name}'] = jnp.zeros((HID,), jnp.float32)
        return inp
    _L3_attn_all = _L3_attn_setup()
    _L3_attn_in = {k: v for k, v in _L3_attn_all.items() if k in ('Wq', 'bq', 'Wk', 'bk', 'Wv', 'bv', 'Wo', 'bo')}
    del _L3_attn_all

    def _L3_xattn_setup():
        import jax, jax.numpy as jnp
        import numpy as np
        DIM = 128
        HEADS = 16
        HEAD_DIM = DIM // HEADS
        SCALE = HEAD_DIM ** (-0.5)

        def _split_heads(t):
            b, n, _ = t.shape
            return t.reshape(b, n, HEADS, HEAD_DIM).transpose(0, 2, 1, 3)
        key = jax.random.key(seed)
        ks = jax.random.split(key, 7)
        B, N, M = (2, 256, 256)
        x = jax.random.normal(ks[0], (B, N, DIM), dtype=jnp.float32)
        y = jax.random.normal(ks[1], (B, M, DIM), dtype=jnp.float32)
        s = DIM ** (-0.5)
        Wq = jax.random.normal(ks[2], (DIM, DIM), dtype=jnp.float32) * s
        Wk = jax.random.normal(ks[3], (DIM, DIM), dtype=jnp.float32) * s
        Wv = jax.random.normal(ks[4], (DIM, DIM), dtype=jnp.float32) * s
        Wp = jax.random.normal(ks[5], (DIM, DIM), dtype=jnp.float32) * s
        bp = jax.random.normal(ks[6], (DIM,), dtype=jnp.float32) * 0.01
        return {'x': x, 'y': y, 'Wq': Wq, 'Wk': Wk, 'Wv': Wv, 'Wp': Wp, 'bp': bp}
    _L3_xattn_all = _L3_xattn_setup()
    _L3_xattn_in = {k: v for k, v in _L3_xattn_all.items() if k in ('Wq', 'Wk', 'Wv', 'Wp', 'bp')}
    del _L3_xattn_all

    def _L3_ffn_setup():
        import jax, jax.numpy as jnp
        import numpy as np
        ALPHA = 1.702
        LIMIT = 7.0
        EPS = 1e-05
        E = 16
        K = 4

        def _swiglu(h):
            x_glu = jnp.minimum(h[..., ::2], LIMIT)
            x_lin = jnp.clip(h[..., 1::2], LIMIT, LIMIT)
            return x_glu * jax.nn.sigmoid(ALPHA * x_glu) * (x_lin + 1.0)
        key = jax.random.key(seed)
        ks = jax.random.split(key, 7)
        B, T, H, I = (1, 256, 128, 128)
        x = jax.random.normal(ks[0], (B, T, H), jnp.float32)
        scale = jnp.ones((H,), jnp.float32)
        gate_w = jax.random.normal(ks[1], (E, H), jnp.float32) * 0.02
        gate_b = jnp.zeros((E,), jnp.float32)
        mlp1_w = jax.random.normal(ks[2], (E, 2 * I, H), jnp.float32) * 0.02
        mlp1_b = jax.random.normal(ks[3], (E, 2 * I), jnp.float32) * 0.02
        mlp2_w = jax.random.normal(ks[4], (E, H, I), jnp.float32) * 0.02
        mlp2_b = jax.random.normal(ks[5], (E, H), jnp.float32) * 0.02
        return dict(x=x, scale=scale, gate_w=gate_w, gate_b=gate_b, mlp1_w=mlp1_w, mlp1_b=mlp1_b, mlp2_w=mlp2_w, mlp2_b=mlp2_b)
    _L3_ffn_all = _L3_ffn_setup()
    _L3_ffn_in = {k: v for k, v in _L3_ffn_all.items() if k in ('scale', 'gate_w', 'gate_b', 'mlp1_w', 'mlp1_b', 'mlp2_w', 'mlp2_b')}
    del _L3_ffn_all
    return {'x': x, 'ctx_1024': ctx_1024, 'mask_Bx1x1xS2_if1': mask_Bx1x1xS2_if1, 'mask_BxS2_bf1': mask_BxS2_bf1, 'L0_attn_Wq': _L0_attn_in['Wq'], 'L0_attn_bq': _L0_attn_in['bq'], 'L0_attn_Wk': _L0_attn_in['Wk'], 'L0_attn_bk': _L0_attn_in['bk'], 'L0_attn_Wv': _L0_attn_in['Wv'], 'L0_attn_bv': _L0_attn_in['bv'], 'L0_attn_Wo': _L0_attn_in['Wo'], 'L0_attn_bo': _L0_attn_in['bo'], 'L0_xattn_Wq': _L0_xattn_in['Wq'], 'L0_xattn_bq': _L0_xattn_in['bq'], 'L0_xattn_Wk': _L0_xattn_in['Wk'], 'L0_xattn_bk': _L0_xattn_in['bk'], 'L0_xattn_Wv': _L0_xattn_in['Wv'], 'L0_xattn_bv': _L0_xattn_in['bv'], 'L0_xattn_Wo': _L0_xattn_in['Wo'], 'L0_xattn_bo': _L0_xattn_in['bo'], 'L0_ffn_w1': _L0_ffn_in['w1'], 'L0_ffn_b1': _L0_ffn_in['b1'], 'L0_ffn_w2': _L0_ffn_in['w2'], 'L0_ffn_b2': _L0_ffn_in['b2'], 'L0_ffn_wg': _L0_ffn_in['wg'], 'L1_attn_ln1_w': _L1_attn_in['ln1_w'], 'L1_attn_ln1_b': _L1_attn_in['ln1_b'], 'L1_attn_in_proj_w': _L1_attn_in['in_proj_w'], 'L1_attn_conv_w': _L1_attn_in['conv_w'], 'L1_attn_conv_b': _L1_attn_in['conv_b'], 'L1_attn_x_proj_w': _L1_attn_in['x_proj_w'], 'L1_attn_dt_proj_w': _L1_attn_in['dt_proj_w'], 'L1_attn_dt_proj_b': _L1_attn_in['dt_proj_b'], 'L1_attn_A_log': _L1_attn_in['A_log'], 'L1_attn_D': _L1_attn_in['D'], 'L1_attn_out_proj_w': _L1_attn_in['out_proj_w'], 'L1_attn_ln2_w': _L1_attn_in['ln2_w'], 'L1_attn_ln2_b': _L1_attn_in['ln2_b'], 'L1_attn_ffn_w1': _L1_attn_in['ffn_w1'], 'L1_attn_ffn_b1': _L1_attn_in['ffn_b1'], 'L1_attn_ffn_w2': _L1_attn_in['ffn_w2'], 'L1_attn_ffn_b2': _L1_attn_in['ffn_b2'], 'L1_xattn_wq': _L1_xattn_in['wq'], 'L1_xattn_wk': _L1_xattn_in['wk'], 'L1_xattn_wv': _L1_xattn_in['wv'], 'L1_ffn_W_r': _L1_ffn_in['W_r'], 'L1_ffn_W_k': _L1_ffn_in['W_k'], 'L1_ffn_W_v': _L1_ffn_in['W_v'], 'L1_ffn_mu_r': _L1_ffn_in['mu_r'], 'L1_ffn_mu_k': _L1_ffn_in['mu_k'], 'L2_attn_wq': _L2_attn_in['wq'], 'L2_attn_wk': _L2_attn_in['wk'], 'L2_attn_wv': _L2_attn_in['wv'], 'L2_attn_wo': _L2_attn_in['wo'], 'L2_xattn_ln_x_g': _L2_xattn_in['ln_x_g'], 'L2_xattn_ln_x_b': _L2_xattn_in['ln_x_b'], 'L2_xattn_ln_l_g': _L2_xattn_in['ln_l_g'], 'L2_xattn_ln_l_b': _L2_xattn_in['ln_l_b'], 'L2_xattn_qn_g': _L2_xattn_in['qn_g'], 'L2_xattn_kn_g': _L2_xattn_in['kn_g'], 'L2_xattn_Wq': _L2_xattn_in['Wq'], 'L2_xattn_Wkv': _L2_xattn_in['Wkv'], 'L2_xattn_Wout': _L2_xattn_in['Wout'], 'L2_xattn_bout': _L2_xattn_in['bout'], 'L2_ffn_W_exp': _L2_ffn_in['W_exp'], 'L2_ffn_b_exp': _L2_ffn_in['b_exp'], 'L2_ffn_up_weights': _L2_ffn_in['up_weights'], 'L2_ffn_up_bias': _L2_ffn_in['up_bias'], 'L2_ffn_down_weights': _L2_ffn_in['down_weights'], 'L2_ffn_W_con': _L2_ffn_in['W_con'], 'L2_ffn_b_con': _L2_ffn_in['b_con'], 'L2_ffn_down_bias': _L2_ffn_in['down_bias'], 'L3_attn_Wq': _L3_attn_in['Wq'], 'L3_attn_bq': _L3_attn_in['bq'], 'L3_attn_Wk': _L3_attn_in['Wk'], 'L3_attn_bk': _L3_attn_in['bk'], 'L3_attn_Wv': _L3_attn_in['Wv'], 'L3_attn_bv': _L3_attn_in['bv'], 'L3_attn_Wo': _L3_attn_in['Wo'], 'L3_attn_bo': _L3_attn_in['bo'], 'L3_xattn_Wq': _L3_xattn_in['Wq'], 'L3_xattn_Wk': _L3_xattn_in['Wk'], 'L3_xattn_Wv': _L3_xattn_in['Wv'], 'L3_xattn_Wp': _L3_xattn_in['Wp'], 'L3_xattn_bp': _L3_xattn_in['bp'], 'L3_ffn_scale': _L3_ffn_in['scale'], 'L3_ffn_gate_w': _L3_ffn_in['gate_w'], 'L3_ffn_gate_b': _L3_ffn_in['gate_b'], 'L3_ffn_mlp1_w': _L3_ffn_in['mlp1_w'], 'L3_ffn_mlp1_b': _L3_ffn_in['mlp1_b'], 'L3_ffn_mlp2_w': _L3_ffn_in['mlp2_w'], 'L3_ffn_mlp2_b': _L3_ffn_in['mlp2_b']}

def reference(x, ctx_1024, mask_Bx1x1xS2_if1, mask_BxS2_bf1, L0_attn_Wq, L0_attn_bq, L0_attn_Wk, L0_attn_bk, L0_attn_Wv, L0_attn_bv, L0_attn_Wo, L0_attn_bo, L0_xattn_Wq, L0_xattn_bq, L0_xattn_Wk, L0_xattn_bk, L0_xattn_Wv, L0_xattn_bv, L0_xattn_Wo, L0_xattn_bo, L0_ffn_w1, L0_ffn_b1, L0_ffn_w2, L0_ffn_b2, L0_ffn_wg, L1_attn_ln1_w, L1_attn_ln1_b, L1_attn_in_proj_w, L1_attn_conv_w, L1_attn_conv_b, L1_attn_x_proj_w, L1_attn_dt_proj_w, L1_attn_dt_proj_b, L1_attn_A_log, L1_attn_D, L1_attn_out_proj_w, L1_attn_ln2_w, L1_attn_ln2_b, L1_attn_ffn_w1, L1_attn_ffn_b1, L1_attn_ffn_w2, L1_attn_ffn_b2, L1_xattn_wq, L1_xattn_wk, L1_xattn_wv, L1_ffn_W_r, L1_ffn_W_k, L1_ffn_W_v, L1_ffn_mu_r, L1_ffn_mu_k, L2_attn_wq, L2_attn_wk, L2_attn_wv, L2_attn_wo, L2_xattn_ln_x_g, L2_xattn_ln_x_b, L2_xattn_ln_l_g, L2_xattn_ln_l_b, L2_xattn_qn_g, L2_xattn_kn_g, L2_xattn_Wq, L2_xattn_Wkv, L2_xattn_Wout, L2_xattn_bout, L2_ffn_W_exp, L2_ffn_b_exp, L2_ffn_up_weights, L2_ffn_up_bias, L2_ffn_down_weights, L2_ffn_W_con, L2_ffn_b_con, L2_ffn_down_bias, L3_attn_Wq, L3_attn_bq, L3_attn_Wk, L3_attn_bk, L3_attn_Wv, L3_attn_bv, L3_attn_Wo, L3_attn_bo, L3_xattn_Wq, L3_xattn_Wk, L3_xattn_Wv, L3_xattn_Wp, L3_xattn_bp, L3_ffn_scale, L3_ffn_gate_w, L3_ffn_gate_b, L3_ffn_mlp1_w, L3_ffn_mlp1_b, L3_ffn_mlp2_w, L3_ffn_mlp2_b):
    import jax
    import jax.numpy as jnp

    def _L0_attn_ref(x, Wq, bq, Wk, bk, Wv, bv, Wo, bo):
        import jax, jax.numpy as jnp
        import numpy as np
        N_HEADS = 16
        WINDOW = 32
        GLOBAL_IDX = np.array([0])

        def _global_local_mask(seq_len):
            i = jnp.arange(seq_len)[:, None]
            j = jnp.arange(seq_len)[None, :]
            g = jnp.asarray(GLOBAL_IDX)
            row_global = jnp.isin(jnp.arange(seq_len), g)
            allowed = (jnp.abs(i - j) <= WINDOW) | row_global[:, None] | row_global[None, :]
            return allowed
        B, S, D = x.shape
        H = N_HEADS
        Dh = D // H
        scale = Dh ** (-0.5)
        q = (x @ Wq + bq).reshape(B, S, H, Dh)
        k = (x @ Wk + bk).reshape(B, S, H, Dh)
        v = (x @ Wv + bv).reshape(B, S, H, Dh)
        scores = jnp.einsum('bqhd,bkhd->bhqk', q, k) * scale
        allowed = _global_local_mask(S)
        scores = jnp.where(allowed[None, None], scores, -jnp.inf)
        attn = jax.nn.softmax(scores, axis=-1)
        out = jnp.einsum('bhqk,bkhd->bqhd', attn, v).reshape(B, S, D)
        return out @ Wo + bo

    def _L0_xattn_ref(srcQ, srcK, srcV, mask, Wq, bq, Wk, bk, Wv, bv, Wo, bo):
        import jax, jax.numpy as jnp
        import numpy as np
        HIDDEN = 128
        NUM_HEAD = 16
        HEAD_DIM = HIDDEN // NUM_HEAD

        def _split_heads(x):
            bs, seq, _ = x.shape
            return x.reshape(bs, seq, NUM_HEAD, HEAD_DIM).transpose(0, 2, 1, 3)
        Q = _split_heads(srcQ @ Wq + bq)
        K = _split_heads(srcK @ Wk + bk)
        V = _split_heads(srcV @ Wv + bv)
        scores = jnp.einsum('bhqd,bhkd->bhqk', Q, K)
        scores = jnp.where(mask == 0, jnp.float32(-10000.0), scores)
        attn = jax.nn.softmax(scores, axis=-1)
        out = jnp.einsum('bhqk,bhkd->bhqd', attn, V)
        bs, _, seq, _ = out.shape
        out = out.transpose(0, 2, 1, 3).reshape(bs, seq, HIDDEN)
        return out @ Wo + bo

    def _L0_ffn_ref(x, w1, b1, w2, b2, wg):
        import jax, jax.numpy as jnp
        import numpy as np
        E = 8
        D = 128
        H = 128
        K = 2
        bsz, length, d = x.shape
        xf = x.reshape(-1, d)
        logits = xf @ wg
        probs = jax.nn.softmax(logits, axis=-1)
        top_v, top_i = jax.lax.top_k(probs, K)
        top_v = top_v / (jnp.sum(top_v, axis=-1, keepdims=True) + 1e-06)
        gates = jnp.sum(jax.nn.one_hot(top_i, E, dtype=xf.dtype) * top_v[..., None], axis=1)
        h = jnp.einsum('td,edh->teh', xf, w1) + b1[None]
        a = jax.nn.gelu(h, approximate=False)
        o = jnp.einsum('teh,ehd->ted', a, w2) + b2[None]
        y = jnp.einsum('te,ted->td', gates, o)
        return y.reshape(bsz, length, d)

    def _L1_attn_ref(x, ln1_w, ln1_b, in_proj_w, conv_w, conv_b, x_proj_w, dt_proj_w, dt_proj_b, A_log, D, out_proj_w, ln2_w, ln2_b, ffn_w1, ffn_b1, ffn_w2, ffn_b2):
        import jax, jax.numpy as jnp
        import numpy as np
        D_MODEL = 128
        D_INNER = 2 * D_MODEL
        D_STATE = 16
        D_CONV = 4
        DT_RANK = D_MODEL // 16
        D_FF = 2 * D_MODEL
        B, L = (4, 256)

        def layer_norm(x, w, b, eps=1e-05):
            mu = jnp.mean(x, axis=-1, keepdims=True)
            var = jnp.mean(jnp.square(x - mu), axis=-1, keepdims=True)
            return (x - mu) * jax.lax.rsqrt(var + eps) * w + b

        def mamba(x, in_proj_w, conv_w, conv_b, x_proj_w, dt_proj_w, dt_proj_b, A_log, Dp, out_proj_w):
            xz = jnp.einsum('bld,ed->ble', x, in_proj_w)
            xc, z = jnp.split(xz, 2, axis=-1)
            xp = jnp.pad(xc, ((0, 0), (D_CONV - 1, 0), (0, 0)))
            conv = conv_b
            for k in range(D_CONV):
                conv = conv + xp[:, k:k + xc.shape[1], :] * conv_w[:, k]
            xc = jax.nn.silu(conv)
            dbc = jnp.einsum('bld,ed->ble', xc, x_proj_w)
            dt_raw = dbc[..., :DT_RANK]
            Bm = dbc[..., DT_RANK:DT_RANK + D_STATE]
            Cm = dbc[..., DT_RANK + D_STATE:]
            dt = jax.nn.softplus(jnp.einsum('blr,dr->bld', dt_raw, dt_proj_w) + dt_proj_b)
            A = -jnp.exp(A_log)
            dA = jnp.exp(dt[..., None] * A)
            dBx = dt[..., None] * Bm[:, :, None, :] * xc[..., None]
            dA_t = jnp.moveaxis(dA, 1, 0)
            dBx_t = jnp.moveaxis(dBx, 1, 0)
            Cm_t = jnp.moveaxis(Cm, 1, 0)

            def step(h, inputs):
                dA_i, dBx_i, C_i = inputs
                h = dA_i * h + dBx_i
                y = jnp.einsum('bdn,bn->bd', h, C_i)
                return (h, y)
            h0 = jnp.zeros((xc.shape[0], D_INNER, D_STATE), xc.dtype)
            _, ys = jax.lax.scan(step, h0, (dA_t, dBx_t, Cm_t))
            y = jnp.moveaxis(ys, 0, 1) + xc * Dp
            y = y * jax.nn.silu(z)
            return jnp.einsum('ble,de->bld', y, out_proj_w)
        x = x + mamba(layer_norm(x, ln1_w, ln1_b), in_proj_w, conv_w, conv_b, x_proj_w, dt_proj_w, dt_proj_b, A_log, D, out_proj_w)
        h = layer_norm(x, ln2_w, ln2_b)
        h = jax.nn.gelu(jnp.einsum('bld,fd->blf', h, ffn_w1) + ffn_b1, approximate=False)
        h = jnp.einsum('blf,df->bld', h, ffn_w2) + ffn_b2
        return x + h

    def _L1_xattn_ref(q, k, v, wq, wk, wv):
        import jax, jax.numpy as jnp
        import numpy as np
        dk = q.shape[-1]
        qp = jnp.einsum('bsd,ed->bse', q, wq)
        kp = jnp.einsum('bsd,ed->bse', k, wk)
        vp = jnp.einsum('bsd,ed->bse', v, wv)
        norm = 1.0 / jnp.sqrt(jnp.asarray(dk, qp.dtype))
        s = jnp.einsum('bqd,bkd->bqk', qp, kp) * norm
        e = jnp.exp(s)
        attention = e / jnp.sum(e, axis=-1, keepdims=True)
        return jnp.einsum('bqk,bkd->bqd', attention, vp)

    def _L1_ffn_ref(x, W_r, W_k, W_v, mu_r, mu_k):
        import jax, jax.numpy as jnp
        import numpy as np
        DIM = 128

        def _reference_tuple_inner(x, W_r, W_k, W_v, mu_r, mu_k):
            B, T, C = x.shape
            x_prev = jnp.concatenate([jnp.zeros((B, 1, C), x.dtype), x[:, :-1, :]], axis=1)
            xr = mu_r * x + (1.0 - mu_r) * x_prev
            xk = mu_k * x + (1.0 - mu_k) * x_prev
            r = jax.nn.sigmoid(jnp.einsum('btc,dc->btd', xr, W_r))
            k = jnp.einsum('btc,dc->btd', xk, W_k)
            k_act = jnp.square(jax.nn.relu(k))
            out = r * jnp.einsum('btc,dc->btd', k_act, W_v)
            new_state = x[:, -1, :]
            return (out, new_state)
        return _reference_tuple_inner(x, W_r, W_k, W_v, mu_r, mu_k)[0]

    def _L2_attn_ref(x, wq, wk, wv, wo):
        import jax, jax.numpy as jnp
        import numpy as np
        NUM_HEADS = 16
        HIDDEN = 128
        HEAD_DIM = HIDDEN // NUM_HEADS

        def _rope_cos_sin(S, head_dim):
            inv = 1.0 / 10000.0 ** (jnp.arange(0, head_dim, 2, dtype=jnp.float32) / head_dim)
            t = jnp.arange(S, dtype=jnp.float32)
            ang = jnp.outer(t, inv)
            return (jnp.cos(ang), jnp.sin(ang))

        def _apply_rope(x, cos, sin):
            B, S, nh, hd = x.shape
            xr = x[..., 0::2]
            xi = x[..., 1::2]
            c = cos[None, :, None, :]
            s = sin[None, :, None, :]
            or_ = xr * c - xi * s
            oi_ = xr * s + xi * c
            return jnp.stack([or_, oi_], axis=-1).reshape(B, S, nh, hd)
        B, S, H = x.shape
        nh, hd = (NUM_HEADS, HEAD_DIM)
        xq = jnp.einsum('bsh,oh->bso', x, wq).reshape(B, S, nh, hd)
        xk = jnp.einsum('bsh,oh->bso', x, wk).reshape(B, S, nh, hd)
        xv = jnp.einsum('bsh,oh->bso', x, wv).reshape(B, S, nh, hd)
        cos, sin = _rope_cos_sin(S, hd)
        xq = _apply_rope(xq.astype(jnp.float32), cos, sin).astype(x.dtype)
        xk = _apply_rope(xk.astype(jnp.float32), cos, sin).astype(x.dtype)
        scores = jnp.einsum('bqhd,bkhd->bhqk', xq, xk) / np.sqrt(hd)
        probs = jax.nn.softmax(scores.astype(jnp.float32), axis=-1).astype(xq.dtype)
        out = jnp.einsum('bhqk,bkhd->bqhd', probs, xv).reshape(B, S, nh * hd)
        return jnp.einsum('bso,ho->bsh', out, wo)

    def _L2_xattn_ref(x, latents, mask, ln_x_g, ln_x_b, ln_l_g, ln_l_b, qn_g, kn_g, Wq, Wkv, Wout, bout):
        import jax, jax.numpy as jnp
        import numpy as np
        DIM = 128
        DIM_LATENT = 128
        DIM_HEAD = 64
        HEADS = 16
        INNER = HEADS * DIM_HEAD

        def layernorm(x, g, b, eps=1e-05):
            m = jnp.mean(x, axis=-1, keepdims=True)
            v = jnp.mean((x - m) ** 2, axis=-1, keepdims=True)
            return (x - m) / jnp.sqrt(v + eps) * g + b

        def rmsnorm(x, gamma, eps=1e-08):
            n = jnp.linalg.norm(x, axis=-1, keepdims=True) * x.shape[-1] ** (-0.5)
            return x / jnp.maximum(n, eps) * gamma
        b, n, _ = x.shape
        m = latents.shape[1]
        h, d = (HEADS, DIM_HEAD)
        scale = d ** (-0.5)
        xn = layernorm(x, ln_x_g, ln_x_b)
        ln = layernorm(latents, ln_l_g, ln_l_b)
        q = (ln @ Wq).reshape(b, m, h, d).transpose(0, 2, 1, 3)
        kv = jnp.concatenate([xn @ Wkv, ln @ Wkv], axis=1)
        kv = kv.reshape(b, n + m, 2, h, d)
        k = kv[:, :, 0].transpose(0, 2, 1, 3)
        v = kv[:, :, 1].transpose(0, 2, 1, 3)
        qn = rmsnorm(q, qn_g) * scale
        kn = rmsnorm(k, kn_g)
        sim = jnp.einsum('bhid,bhjd->bhij', qn, kn)
        max_neg = -jnp.finfo(sim.dtype).max
        padded_mask = jnp.concatenate([mask, jnp.ones((b, m), bool)], axis=1)
        sim = jnp.where(padded_mask[:, None, None, :], sim, max_neg)
        attn = jax.nn.softmax(sim.astype(jnp.float32), axis=-1).astype(sim.dtype)
        out = jnp.einsum('bhij,bhjd->bhid', attn, v)
        out = out.transpose(0, 2, 1, 3).reshape(b, m, h * d)
        return out @ Wout + bout

    def _L2_ffn_ref(x, W_exp, b_exp, up_weights, up_bias, down_weights, W_con, b_con, down_bias):
        import jax, jax.numpy as jnp
        import numpy as np
        D_MODEL = 128
        EXPANSION = 4
        D_HIDDEN = D_MODEL * EXPANSION
        NUM_STAGES = int(np.log2(D_HIDDEN))

        def butterfly(y, weights, dim):
            lead = y.shape[:-1]
            for stage in range(weights.shape[0]):
                s = 2 ** stage
                nb = dim // (2 * s)
                yr = y.reshape(*lead, nb, 2, s)
                a = yr[..., 0, :]
                b = yr[..., 1, :]
                w = weights[stage].reshape(nb, s, 2, 2)
                na = w[..., 0, 0] * a + w[..., 0, 1] * b
                nb2 = w[..., 1, 0] * a + w[..., 1, 1] * b
                y = jnp.stack([na, nb2], axis=-2).reshape(*lead, dim)
            return y
        h = jnp.einsum('bsd,dh->bsh', x, W_exp) + b_exp
        h = butterfly(h, up_weights, D_HIDDEN)
        h = jax.nn.gelu(h + up_bias, approximate=False)
        h = butterfly(h, down_weights, D_HIDDEN)
        y = jnp.einsum('bsh,hd->bsd', h, W_con) + b_con
        return y + down_bias

    def _L3_attn_ref(x, Wq, bq, Wk, bk, Wv, bv, Wo, bo):
        import jax, jax.numpy as jnp
        import numpy as np
        B, S, HID = (2, 256, 128)
        H = 16
        D = HID // H
        SPARSITY = 0.9

        def _sparse_attn(x, Wq, bq, Wk, bk, Wv, bv, Wo, bo):
            b, s, hid = x.shape
            d = hid // H

            def heads(y):
                return y.reshape(b, s, H, d).transpose(0, 2, 1, 3)
            Q = heads(x @ Wq + bq)
            K = heads(x @ Wk + bk)
            V = heads(x @ Wv + bv)
            scores = jnp.einsum('bhqd,bhkd->bhqk', Q, K) / np.sqrt(d)
            k_keep = int(s * (1.0 - SPARSITY))
            vals, idx = jax.lax.top_k(scores, k_keep)
            n = b * H * s
            rows = jnp.arange(n)[:, None]
            sparse = jnp.zeros((n, s), scores.dtype).at[rows, idx.reshape(n, k_keep)].set(vals.reshape(n, k_keep)).reshape(b, H, s, s)
            attn = jax.nn.softmax(sparse, axis=-1)
            out = jnp.einsum('bhqk,bhkd->bhqd', attn, V)
            out = out.transpose(0, 2, 1, 3).reshape(b, s, hid)
            return out @ Wo + bo
        return _sparse_attn(x, Wq, bq, Wk, bk, Wv, bv, Wo, bo)

    def _L3_xattn_ref(x, y, Wq, Wk, Wv, Wp, bp):
        import jax, jax.numpy as jnp
        import numpy as np
        DIM = 128
        HEADS = 16
        HEAD_DIM = DIM // HEADS
        SCALE = HEAD_DIM ** (-0.5)

        def _split_heads(t):
            b, n, _ = t.shape
            return t.reshape(b, n, HEADS, HEAD_DIM).transpose(0, 2, 1, 3)
        q = _split_heads(x @ Wq)
        k = _split_heads(y @ Wk)
        v = _split_heads(y @ Wv)
        attn = jnp.einsum('bhid,bhjd->bhij', q, k) * SCALE
        attn = jax.nn.softmax(attn, axis=-1)
        out = jnp.einsum('bhij,bhjd->bhid', attn, v)
        b, h, n, d = out.shape
        out = out.transpose(0, 2, 1, 3).reshape(b, n, h * d)
        return out @ Wp + bp

    def _L3_ffn_ref(x, scale, gate_w, gate_b, mlp1_w, mlp1_b, mlp2_w, mlp2_b):
        import jax, jax.numpy as jnp
        import numpy as np
        ALPHA = 1.702
        LIMIT = 7.0
        EPS = 1e-05
        E = 16
        K = 4

        def _swiglu(h):
            x_glu = jnp.minimum(h[..., ::2], LIMIT)
            x_lin = jnp.clip(h[..., 1::2], LIMIT, LIMIT)
            return x_glu * jax.nn.sigmoid(ALPHA * x_glu) * (x_lin + 1.0)
        t = x * jax.lax.rsqrt(jnp.mean(x * x, axis=-1, keepdims=True) + EPS) * scale
        g = jnp.einsum('bth,eh->bte', t, gate_w) + gate_b
        vals, idx = jax.lax.top_k(g, K)
        w = jax.nn.softmax(vals, axis=-1)
        route = jnp.sum(jax.nn.one_hot(idx, E, dtype=t.dtype) * w[..., None], axis=-2)
        route_e = jnp.moveaxis(route, -1, 0)

        def step(acc, p):
            w1, b1, w2, b2, r = p
            h = jnp.einsum('bth,ih->bti', t, w1) + b1
            s = _swiglu(h)
            y = jnp.einsum('bti,hi->bth', s, w2) + b2
            return (acc + r[..., None] * y, None)
        acc, _ = jax.lax.scan(step, jnp.zeros_like(x), (mlp1_w, mlp1_b, mlp2_w, mlp2_b, route_e))
        return x + acc
    x = _layernorm(x + _L0_attn_ref(x, L0_attn_Wq, L0_attn_bq, L0_attn_Wk, L0_attn_bk, L0_attn_Wv, L0_attn_bv, L0_attn_Wo, L0_attn_bo), axis=-1)
    x = _layernorm(x + _L0_xattn_ref(x, ctx_1024, ctx_1024, mask_Bx1x1xS2_if1, L0_xattn_Wq, L0_xattn_bq, L0_xattn_Wk, L0_xattn_bk, L0_xattn_Wv, L0_xattn_bv, L0_xattn_Wo, L0_xattn_bo), axis=-1)
    x = _layernorm(x + _L0_ffn_ref(x, L0_ffn_w1, L0_ffn_b1, L0_ffn_w2, L0_ffn_b2, L0_ffn_wg), axis=-1)
    x = _layernorm(x + _L1_attn_ref(x, L1_attn_ln1_w, L1_attn_ln1_b, L1_attn_in_proj_w, L1_attn_conv_w, L1_attn_conv_b, L1_attn_x_proj_w, L1_attn_dt_proj_w, L1_attn_dt_proj_b, L1_attn_A_log, L1_attn_D, L1_attn_out_proj_w, L1_attn_ln2_w, L1_attn_ln2_b, L1_attn_ffn_w1, L1_attn_ffn_b1, L1_attn_ffn_w2, L1_attn_ffn_b2), axis=-1)
    x = _layernorm(x + _L1_xattn_ref(x, ctx_1024, ctx_1024, L1_xattn_wq, L1_xattn_wk, L1_xattn_wv), axis=-1)
    x = _layernorm(x + _L1_ffn_ref(x, L1_ffn_W_r, L1_ffn_W_k, L1_ffn_W_v, L1_ffn_mu_r, L1_ffn_mu_k), axis=-1)
    x = _layernorm(x + _L2_attn_ref(x, L2_attn_wq, L2_attn_wk, L2_attn_wv, L2_attn_wo), axis=-1)
    x = _layernorm(x + _L2_xattn_ref(ctx_1024, x, mask_BxS2_bf1, L2_xattn_ln_x_g, L2_xattn_ln_x_b, L2_xattn_ln_l_g, L2_xattn_ln_l_b, L2_xattn_qn_g, L2_xattn_kn_g, L2_xattn_Wq, L2_xattn_Wkv, L2_xattn_Wout, L2_xattn_bout), axis=-1)
    x = _layernorm(x + _L2_ffn_ref(x, L2_ffn_W_exp, L2_ffn_b_exp, L2_ffn_up_weights, L2_ffn_up_bias, L2_ffn_down_weights, L2_ffn_W_con, L2_ffn_b_con, L2_ffn_down_bias), axis=-1)
    x = _layernorm(x + _L3_attn_ref(x, L3_attn_Wq, L3_attn_bq, L3_attn_Wk, L3_attn_bk, L3_attn_Wv, L3_attn_bv, L3_attn_Wo, L3_attn_bo), axis=-1)
    x = _layernorm(x + _L3_xattn_ref(x, ctx_1024, L3_xattn_Wq, L3_xattn_Wk, L3_xattn_Wv, L3_xattn_Wp, L3_xattn_bp), axis=-1)
    x = _layernorm(x + _L3_ffn_ref(x, L3_ffn_scale, L3_ffn_gate_w, L3_ffn_gate_b, L3_ffn_mlp1_w, L3_ffn_mlp1_b, L3_ffn_mlp2_w, L3_ffn_mlp2_b), axis=-1)
    return x

_drawn_inputs = setup_inputs


def setup_inputs(seed=0):
    import zlib

    import numpy as np

    out = dict(_drawn_inputs(seed))
    spreads = {'L0_attn_bq': (0.0, 0.8),
     'L0_attn_bk': (0.0, 2.0),
     'L0_attn_bv': (0.0, 0.1),
     'L0_attn_bo': (0.0, 0.1),
     'L0_xattn_bq': (0.0, 0.8),
     'L0_xattn_bk': (0.0, 2.0),
     'L0_xattn_bv': (0.0, 0.305),
     'L0_xattn_bo': (0.0, 0.1),
     'L1_attn_ln1_w': (1.0, 0.6),
     'L1_attn_ln1_b': (0.0, 0.8),
     'L1_attn_conv_b': (0.0, 0.8),
     'L1_attn_D': (1.0, 0.6),
     'L1_attn_ln2_w': (1.0, 0.6),
     'L1_attn_ln2_b': (0.0, 2.0),
     'L1_attn_ffn_b1': (0.0, 2.0),
     'L1_attn_ffn_b2': (0.0, 0.8),
     'L2_xattn_ln_x_g': (1.0, 0.6),
     'L2_xattn_ln_x_b': (0.0, 0.5),
     'L2_xattn_ln_l_g': (1.0, 0.6),
     'L2_xattn_ln_l_b': (0.0, 0.8),
     'L2_xattn_qn_g': (1.0, 0.6),
     'L2_xattn_kn_g': (1.0, 0.6),
     'L2_xattn_bout': (0.0, 0.1),
     'L2_ffn_b_exp': (0.0, 0.1),
     'L2_ffn_up_bias': (0.0, 0.1),
     'L2_ffn_b_con': (0.0, 0.1),
     'L2_ffn_down_bias': (0.0, 0.1),
     'L3_attn_bq': (0.0, 0.462),
     'L3_attn_bk': (0.0, 0.8),
     'L3_attn_bv': (0.0, 0.1),
     'L3_attn_bo': (0.0, 0.1),
     'L3_ffn_scale': (1.0, 0.6),
     'L3_ffn_gate_b': (0.0, 0.1)}
    factors = {'L0_attn_Wq': 8.0,
     'L0_attn_Wk': 8.0,
     'L0_attn_Wv': 6.731,
     'L0_xattn_Wq': 8.0,
     'L0_xattn_Wk': 8.0,
     'L0_ffn_w1': 8.0,
     'L0_ffn_b1': 8.0,
     'L0_ffn_w2': 8.0,
     'L1_attn_in_proj_w': 8.0,
     'L1_attn_conv_w': 8.0,
     'L1_attn_x_proj_w': 8.0,
     'L1_attn_dt_proj_w': 8.0,
     'L1_attn_dt_proj_b': 8.0,
     'L1_attn_A_log': 8.0,
     'L1_attn_out_proj_w': 8.0,
     'L1_attn_ffn_w1': 3.738,
     'L1_attn_ffn_w2': 2.846,
     'L1_ffn_W_r': 3.069,
     'L1_ffn_mu_r': 6.778,
     'L3_xattn_bp': 5.456,
     'L3_ffn_mlp1_b': 8.0,
     'L3_ffn_mlp2_b': 8.0}
    for name, (base, spread) in spreads.items():
        noise = np.random.default_rng([zlib.crc32(name.encode()), seed]).standard_normal(out[name].shape)
        drawn = base * np.exp(spread * noise) if base else spread * noise
        out[name] = jnp.asarray(drawn.astype(out[name].dtype))
    for name, factor in factors.items():
        out[name] = (out[name] * factor).astype(out[name].dtype)
    return out
```

```python
from contextlib import ExitStack

import numpy as np
import concourse.bass as bass
from concourse import mybir

ALU = mybir.AluOpType
ACT = mybir.ActivationFunctionType
AX = mybir.AxisListType.X
F32 = mybir.dt.float32
BF16 = mybir.dt.bfloat16
I32 = mybir.dt.int32
U8 = mybir.dt.uint8

D = 128
NB, S = 8, 100
T = NB * S
HALF = T // 2
CTX = 1444
H, DH = 16, 8
SLOT = 32
BIG = 1e30
LN_EPS = 1e-5
CHUNK = 512
KT_TILES = [(t * 128, min(128, CTX - t * 128)) for t in range(-(-CTX // 128))]
E0, K0 = 8, 2
E3, K3 = 16, 4
TOP = int(S * (1.0 - 0.9))

STAGES = 9
F0_CHAIN = 13

PIECES = [
    ("ident", 128), ("headmask", H), ("selx", 128), ("parity", 2), ("window", S), ("blockdiag", 128), ("sel64", 8 * 128),
    ("cosq", S), ("sinq", S), ("cosk", S), ("sink", S), ("maskab", 2),
    ("a0_wq", 128), ("a0_wk", 128), ("a0_wv", 128), ("a0_wo", 512), ("a0_bv", 128), ("a0_b", 3),
    ("x0_wq", 128), ("x0_wk", 128), ("x0_wv", 128), ("x0_wo", 512), ("x0_bv", 128), ("x0_b", 3),
    ("f0_wg", E0), ("f0_b2", 128),
    ("m_ln1", 2), ("m_ln2", 2), ("m_in", 512), ("m_conv", 2 * 5), ("m_xp", 2 * 40), ("m_dtw", 256), ("m_dtb", 2),
    ("m_alog", 32), ("m_d", 2), ("m_out", 256), ("m_w1", 256), ("m_b1", 2), ("m_w2", 256), ("m_b2", 1),
    ("m_sel", 16 * 256),
    ("x1_wq", 128), ("x1_wk", 128), ("x1_wv", 128),
    ("f1_wr", 128), ("f1_wk", 128), ("f1_wv", 128), ("f1_mu", 2),
    ("a2_wq", 128), ("a2_wk", 128), ("a2_wqs", 128), ("a2_wks", 128), ("a2_wv", 128), ("a2_wo", 512),
    ("x2_ln", 4), ("x2_g", 2), ("x2_wq", 1024), ("x2_wk", 1024), ("x2_wv", 1024), ("x2_wo", 1024), ("x2_b", 1),
    ("f2_we", 512), ("f2_wc", 512), ("f2_be", 512), ("f2_ub", 4), ("f2_b", 2),
    ("a3_wq", 128), ("a3_wk", 128), ("a3_wv", 128), ("a3_wo", 512), ("a3_bv", 128), ("a3_b", 3),
    ("x3_wq", 128), ("x3_wk", 128), ("x3_wv", 128), ("x3_wo", 512), ("x3_b", 1),
    ("f3_scale", 1), ("f3_wg", E3), ("f3_bg", E3), ("f3_b2", 128),
]
AT, _n = {}, 0
for _name, _w in PIECES:
    AT[_name] = (_n, _w)
    _n += _w
PACKED = _n
LOADS = ["ident", "x0_wq", "m_ln1", "x2_ln"]
EXPERT0 = 128 * 3 + 1
EXPERT3 = 128 * 4 + 2


def build(nc, x_in, ctx_in, mask0_in, mask2_in, packed_in, expert0_in, expert3_in, stages_in, out):
    with ExitStack() as scope:
        sems = {}

        def sem(name):
            if name not in sems:
                sems[name] = scope.enter_context(nc.semaphore(name))
            return sems[name]

        BEFORE, PIECES_OF_STEP = 10, 8

        LEFT = {}
        for kind, called, totals in (
            ("self", ("a0", "a2", "a3"), lambda L: dict(
                qk=2, qf=2, kf=2, scores=2 + NB, pv=2 + NB, staged=2 * NB, sub=1 + NB, v=NB, probs=NB, pt=1 + 2 * NB,
                t=2 * NB, vp=NB, oa=1 + NB, zero=2, exp=NB, chain=NB * {"a0": 5, "a2": 3, "a3": 10}[L], win=3 * NB, y=2)),
            ("cross", ("x0", "x1", "x2", "x3"), lambda L: {
                "x1": dict(ctx=16 * NB, ctx_used=1 + NB, exp=1 + 4 * NB, k=3 * NB, kf=3 * NB, pv=NB, vzero=1, q=2, qf=2, rd=NB,
                           scores=3 * NB, v=3 * NB, vp=4 * NB, o=1 + NB),
                "x2": dict(ctx=16 * NB, ctx_used=1 + NB, exp=1 + NB * H, k=32 * NB, kf=64 * NB, nm=NB * H, o=1 + 2 * NB,
                           pt_act=2 * H * NB, pt_dve=2 * H * NB, pv=2 + NB * H, q=NB, op0=2 * NB, rd=NB, rdt=NB, rdtf=NB, bc=NB,
                           normed=NB, scores=1 + NB * H, t=4 * H * NB, v=32 * NB, vp=32 * NB, y=NB, vzero=4),
            }.get(L) or dict(
                q=2, qf=3, qlink=8, qw=16, scores=NB * H, nm=NB * H, pv=2 + NB * H, exp=4 * NB * H, t=3 * NB * H, ctx=16 * NB,
                k=BEFORE + 6 * PIECES_OF_STEP + 6, kf=BEFORE + 6 * PIECES_OF_STEP + 6, split=3 * NB, split_act=3 * NB, kw=16 * NB, o=1 + NB, bc=8,
                rd=8, normed=8, y=2, vzero=2, ones=32, mxs=2 * NB, mlink=8 * NB, mx0=48 * NB, mx1=48 * NB,
                op0=16 * 13 * NB, op1=16 * 13 * NB, mask=16 * NB, mrow=NB, m01=NB, mneg=NB)),
            ("ffn", ("f0", "f1", "f2", "f3"), lambda L: {
                "f1": dict(x=2, h=4, sig=2, relu=2, act=2, y=2, rv=2, each=5),
                "f2": dict(made=12 * STAGES, gt=1, gtc=3, h=8, act=8, y=2),
            }.get(L) or dict(
                y_done=3 + 2 * E0, w0=8 * E0, w1=8 * E0, h=2 * E0, act=2 + 2 * E0, bc=2 * E0, up=2 + 2 * E0, gates=1, gt=1,
                gtc=1, logits=1, y=1, sub=1, exp=1, chain=F0_CHAIN, each=2 * (NB - 1))),
        ):
            before = {}
            for L in called:
                LEFT[L] = (kind, dict(before))
                for name, n in totals(L).items():
                    before[name] = before.get(name, 0) + n

        def of(L, name):
            return sem(f"{LEFT[L][0]}_{name}")

        def at(L, name, value):
            return of(L, name), value + LEFT[L][1].get(name, 0)

        W = scope.enter_context(nc.sbuf_tensor("weights", [128, PACKED], F32))
        PS = scope.enter_context(nc.psum_tensor("ps", [128, 8, CHUNK], F32))
        PSF = PS[:, :, :].rearrange("p b c -> p (b c)")
        X = scope.enter_context(nc.sbuf_tensor("x", [128, T], F32))
        R = scope.enter_context(nc.sbuf_tensor("residual", [128, T], F32))
        SQ = scope.enter_context(nc.sbuf_tensor("squares", [128, T], F32))
        mean_w = scope.enter_context(nc.sbuf_tensor("mean_w", [128, 128], F32))
        epsc = scope.enter_context(nc.sbuf_tensor("eps_column", [128, 1], F32))
        room = (212900 - 4 * (PACKED + 3 * T + 129 + 570)) // 4
        ARENA = scope.enter_context(nc.sbuf_tensor("arena", [128, room], F32))

        class Layout:

            def __init__(self, start=0):
                self.at = start

            def take(self, *shape):
                n = int(np.prod(shape))
                a = ARENA[:, self.at:self.at + n]
                self.at += n
                assert self.at <= room, (self.at, room)
                if len(shape) == 2:
                    a = a.rearrange("p (a b) -> p a b", a=shape[0])
                if len(shape) == 3:
                    a = a.rearrange("p (a b c) -> p a b c", a=shape[0], b=shape[1])
                return a

            def take_bf16(self, n):
                a = ARENA[:, self.at:self.at + (n + 1) // 2].bitcast(BF16)
                self.at += (n + 1) // 2
                return a

        def w(name, rows=128):
            a, n = AT[name]
            return W[0:rows, a:a + n]

        def wcol(name, j=0):
            a, _ = AT[name]
            return W[:, a + j:a + j + 1]

        def pool_wait(pool, s, value):
            pool.wait_ge(s, value)
            pool.sem_inc(sem("pool_passed"), 1)

        def sync_wait(sp, s, value):
            sp.wait_ge(s, value)
            sp.sem_inc(sem("sync_passed"), 1)

        ident = w("ident")

        def half(a, h):
            return a[:, h * HALF:(h + 1) * HALF]

        def loaded(eng, name):
            n = max(i for i, first in enumerate(LOADS) if AT[first][0] <= AT[name][0])
            eng.wait_ge(sem(f"w_loaded{n}"), 16)

        def x_ready(eng, c, h):
            if c < 0:
                eng.wait_ge(sem("x_loaded"), 16)
            else:
                eng.wait_ge(sem("ln_out"), 2 * c + h + 1)

        def norm_pe(pe, c):
            for h in range(2):
                pe.wait_ge(sem("ln_row"), 2 * c + h + 1)
                if c == 0 and h == 0:
                    pe.wait_ge(sem("consts"), 2)
                pe.matmul(PS[:, 6 + h, 0:HALF], mean_w[:, :], half(R, h), start=True, stop=True) \
                    .then_inc(sem("ln_mean"), 1)
            for h in range(2):
                pe.wait_ge(sem("ln_square"), 2 * c + h + 1)
                pe.matmul(PS[:, 6 + h, 0:HALF], mean_w[:, :], half(SQ, h), start=True, stop=True) \
                    .then_inc(sem("ln_var"), 1)

        def norm_act(act, c):
            for h in range(2):
                act.wait_ge(sem("ln_centred"), 2 * c + h + 1)
                act.activation(half(SQ, h), half(R, h), ACT.Square).then_inc(sem("ln_square"), 1)
            for h in range(2):
                act.wait_ge(sem("ln_var"), 2 * c + h + 1)
                act.activation(half(SQ, h), PS[:, 6 + h, 0:HALF], ACT.Sqrt, bias=epsc[:, :]) \
                    .then_inc(sem("ln_std"), 1)

        def norm_dve(dve, c, rows, dst=None, affine=None):
            dst = X if dst is None else dst
            for h in range(2):
                rows(h).then_inc(sem("ln_row"), 1)
            for h in range(2):
                dve.wait_ge(sem("ln_mean"), 2 * c + h + 1)
                dve.tensor_tensor(half(R, h), half(R, h), PS[:, 6 + h, 0:HALF], ALU.subtract) \
                    .then_inc(sem("ln_centred"), 1)
            for h in range(2):
                dve.wait_ge(sem("ln_std"), 2 * c + h + 1)
                dve.reciprocal(half(SQ, h), half(SQ, h)).then_inc(sem("ln_recip"), 1)
            for h in range(2):
                dve.wait_ge(sem("ln_recip"), 2 * c + h + 1)
                if affine is None:
                    dve.tensor_tensor(half(dst, h), half(R, h), half(SQ, h), ALU.mult).then_inc(sem("ln_out"), 1)
                else:
                    gain, shift = affine
                    dve.scalar_tensor_tensor(half(dst, h), half(R, h), gain, half(SQ, h), ALU.mult, ALU.mult) \
                        .then_inc(sem("ln_scaled"), 1)
                    dve.wait_ge(sem("ln_scaled"), 2 * (0 if c == C_M1 else 1) + h + 1)
                    dve.tensor_scalar(half(dst, h), half(dst, h), shift, None, ALU.add).then_inc(sem("ln_out"), 1)

        def residual(dve, c, ready, y, bias=None):
            def rows(h):
                ready(h)
                if bias is None:
                    return dve.tensor_tensor(half(R, h), y(h), half(X, h), ALU.add)
                return dve.scalar_tensor_tensor(half(R, h), y(h), bias, half(X, h), ALU.add, ALU.add)
            norm_dve(dve, c, rows)

        def bank(b, n=HALF):
            return PS[:, b, 0:n]

        C_A0, C_X0, C_F0, C_M1, C_M2, C_M, C_X1, C_F1, C_A2, C_X2, C_F2, C_A3, C_X3, C_F3 = range(14)

        def self_buffers():
            lay = Layout()
            return dict(
                q=lay.take(T), k=lay.take(T), ta=lay.take(T), tb=lay.take(T), o=lay.take(4, T),
                xb=[lay.take(S) for _ in range(2)], qbd=[lay.take(H, S) for _ in range(2)],
                v=[lay.take(H, SLOT) for _ in range(2)], p=[lay.take(H, S) for _ in range(2)],
                pt=[lay.take(H, S) for _ in range(2)], s2=lay.take(H, S), s3=lay.take(H, S),
                best=[lay.take(H, 8) for _ in range(2)], mx=[lay.take(H) for _ in range(2)],
                den=[lay.take(H) for _ in range(2)])

        SB = self_buffers()
        SPRE = {"window": "a0", "rope": "a2", "top": "a3"}

        def self_pe(pe, kind, c):
            L = SPRE[kind]
            names = ["wq", "wk"] + (["wqs", "wks"] if kind == "rope" else [])
            loaded(pe, f"{L}_wq")
            for h in range(2):
                x_ready(pe, c, h)
                for j, name in enumerate(names):
                    mm = pe.matmul(bank(2 * j + h), w(f"{L}_{name}"), half(X, h), start=True, stop=True)
                mm.then_inc(of(L, "qk"), 1)
            pe.wait_ge(*at(L, "qf", 2))
            pe.wait_ge(*at(L, "kf", 2))
            pe.sem_inc(of(L, "scores"), 2)
            pe.sem_inc(of(L, "pv"), 2)
            with pe.Fori(0, NB // 2) as i:
                for k in range(2):
                    b0 = i * (2 * S) + k * S
                    pe.wait_ge(*at(L, "staged", i * 4 + (2 * k + 2)))
                    pe.wait_ge(*at(L, "sub", i * 2 + (k + 1)))
                    pe.matmul(PS[0:S, 6, k * 128:k * 128 + D], SB["xb"][k], w(f"{L}_wv"), start=True, stop=True) \
                        .then_inc(of(L, "v"), 1)
                    for hd in range(H):
                        mm = pe.matmul(PS[0:S, hd // 4, (hd % 4) * S:(hd % 4 + 1) * S], SB["qbd"][k][:, hd, :],
                                       SB["k"][:, bass.ds(b0, S)], start=True, stop=True)
                    mm.then_inc(of(L, "scores"), 1)
                for k in range(2):
                    pe.wait_ge(*at(L, "probs", i * 2 + (k + 1)))
                    for j in range(2):
                        pe.wait_ge(*at(L, "pt", i * 4 + (2 * k + j + 1)))
                        for q in range(8):
                            mm = pe.transpose(PS[0:S, 4 + q // 4, (q % 4) * S:(q % 4 + 1) * S],
                                              SB["p"][k][0:S, 8 * j + q, :], ident[0:S, 0:S])
                        mm.then_inc(of(L, "t"), 1)
                    pe.wait_ge(*at(L, "pt", i * 4 + (2 * k + 3)))
                    pe.wait_ge(*at(L, "vp", i * 2 + (k + 1)))
                    pe.wait_ge(*at(L, "oa", i * 2 + (k + 1)))
                    for hd in range(H):
                        q = hd % 4
                        mm = pe.matmul(PS[SLOT * q:SLOT * (q + 1), 7, (hd // 4) * S:(hd // 4 + 1) * S],
                                       SB["v"][k][0:S, hd, :], SB["pt"][k][0:S, hd, :], start=True, stop=True)
                    mm.then_inc(of(L, "pv"), 1)
            pe.wait_ge(*at(L, "oa", 1 + NB))
            project_out_pe(pe, L, SB["o"])
            norm_pe(pe, c + 1)

        def project_out_pe(pe, L, o):
            wo = w(f"{L}_wo").rearrange("p (g n) -> p g n", g=4)
            for h in range(2):
                for g in range(4):
                    mm = pe.matmul(bank(h), wo[:, g, :], o[:, g, h * HALF:(h + 1) * HALF],
                                   start=(g == 0), stop=(g == 3))
                mm.then_inc(of(L, "y"), 1)

        def self_pool(pool, kind, c):
            L = SPRE[kind]
            x_ready(pool, c, 1)
            for k in range(2):
                pool.memset(SB["v"][k], 0.0).then_inc(of(L, "zero"), 1)
            pool.wait_ge(*at(L, "qf", 2))
            loaded(pool, "headmask")
            hm = w("headmask").unsqueeze(2).to_broadcast([128, H, S])
            with pool.Fori(0, NB // 2) as i:
                for k in range(2):
                    b0 = i * (2 * S) + k * S
                    pool.wait_ge(*at(L, "scores", i * 2 + (k + 1)))
                    pool.tensor_copy(SB["xb"][k], X[:, bass.ds(b0, S)]).then_inc(of(L, "staged"), 1)
                    pool.tensor_tensor(SB["qbd"][k], SB["q"][:, bass.ds(b0, S)].unsqueeze(1).to_broadcast([128, H, S]),
                                       hm, ALU.mult).then_inc(of(L, "staged"), 1)

        def self_act(act, kind, c):
            L = SPRE[kind]
            if kind != "rope":
                for h in range(2):
                    act.wait_ge(*at(L, "qk", h + 1))
                    act.activation(half(SB["k"], h), bank(2 + h), ACT.Identity, bias=wcol(f"{L}_b", 1)) \
                        .then_inc(of(L, "kf"), 1)
            act.sem_inc(of(L, "pt"), 1)
            act.sem_inc(of(L, "oa"), 1)
            with act.Fori(0, NB // 2) as i:
                for k in range(2):
                    act.wait_ge(*at(L, "sub", i * 2 + (k + 2)))
                    act.activation(SB["p"][k][0:S], SB["p"][k][0:S], ACT.Exp).then_inc(of(L, "exp"), 1)
                for k in range(2):
                    act.wait_ge(*at(L, "pv", i * 2 + (k + 1)))
                    for j in range(2):
                        act.wait_ge(*at(L, "t", i * 4 + (2 * k + j + 1)))
                        act.activation(SB["pt"][k][0:S, 8 * j:8 * j + 8, :].rearrange("p (a b) s -> p a (b s)", a=2),
                                       PS[0:S, 4:6, 0:4 * S], ACT.Copy).then_inc(of(L, "pt"), 1)
                    act.wait_ge(*at(L, "pv", i * 2 + (k + 3)))
                    act.activation(SB["o"][:, :, bass.ds(i * (2 * S) + k * S, S)],
                                   PS[:, 7, 0:4 * S].rearrange("p (g s) -> p g s", g=4), ACT.Copy) \
                        .then_inc(of(L, "oa"), 1)
            norm_act(act, c + 1)

        def self_dve(dve, kind, c):
            L = SPRE[kind]
            scale = DH ** -0.5
            loaded(dve, f"{L}_wq")
            for h in range(2):
                dve.wait_ge(*at(L, "qk", h + 1))
                if kind == "rope":
                    for n, (name, dst) in enumerate((("q", SB["q"]), ("k", SB["k"]))):
                        base = 8 * h + 4 * n
                        tabs = [w(t + name).unsqueeze(1).to_broadcast([128, 4, S]) for t in ("cos", "sin")]
                        for j, tmp in enumerate((SB["ta"], SB["tb"])):
                            dve.tensor_tensor(half(tmp, h).rearrange("p (b s) -> p b s", b=4),
                                              bank(n * 2 + h + 4 * j).rearrange("p (b s) -> p b s", b=4),
                                              tabs[j], ALU.mult).then_inc(sem("rope"), 1)
                        dve.wait_ge(sem("rope"), 4 * h + 2 * n + 2)
                        dve.tensor_tensor(half(dst, h), half(SB["ta"], h), half(SB["tb"], h), ALU.add) \
                            .then_inc(of(L, f"{name}f"), 1)
                        dve.wait_ge(*at(L, f"{name}f", h + 1))
                else:
                    dve.tensor_scalar(half(SB["q"], h), bank(h), wcol(f"{L}_b", 0), scale, ALU.add, ALU.mult) \
                        .then_inc(of(L, "qf"), 1)
            dve.wait_ge(*at(L, "zero", 2))
            dve.sem_inc(of(L, "sub"), 1)
            steps = {"window": 5, "rope": 3, "top": 10}[kind]
            chain = of(L, "chain")
            with dve.Fori(0, NB // 2) as i:
                for k in range(2):
                    P, MX = SB["p"][k], SB["mx"][k]
                    dve.wait_ge(*at(L, "pv", i * 2 + (k + 1)))
                    dve.wait_ge(*at(L, "v", i * 2 + (k + 1)))
                    vps = PS[0:S, 6, k * 128:k * 128 + D].rearrange("p (h d) -> p h d", h=H)
                    if kind == "rope":
                        dve.tensor_copy(SB["v"][k][0:S, :, 0:DH], vps).then_inc(of(L, "vp"), 1)
                    else:
                        dve.tensor_tensor(SB["v"][k][0:S, :, 0:DH], vps,
                                          w(f"{L}_bv", S).rearrange("p (h d) -> p h d", h=H), ALU.add) \
                            .then_inc(of(L, "vp"), 1)
                    dve.wait_ge(*at(L, "scores", i * 2 + (k + 3)))
                    sps = PS[0:S, 0:4, 0:4 * S].rearrange("p a (b s) -> p a b s", b=4)
                    n = [0]

                    def link(ins):
                        n[0] += 1
                        ins.then_inc(chain, 1)
                        dve.wait_ge(*at(L, "chain", i * (2 * steps) + (k * (steps - 2) + n[0])))

                    four = lambda a: a[0:S].rearrange("p (a b) s -> p a b s", a=4)
                    wide = lambda a: a[0:S].rearrange("p (a b) -> p a b", a=4).unsqueeze(3).to_broadcast([S, 4, 4, S])
                    if kind == "window":
                        win = w("window", S).unsqueeze(1).to_broadcast([S, 4, S])
                        for a in range(4):
                            ins = dve.tensor_tensor(SB["s2"][0:S, 4 * a:4 * a + 4, :],
                                                    PS[0:S, a, 0:4 * S].rearrange("p (b s) -> p b s", b=4), win, ALU.add)
                            if a < 3:
                                ins.then_inc(of(L, "win"), 1)
                        link(ins)
                        dve.wait_ge(*at(L, "win", i * 6 + (3 * k + 3)))
                        link(dve.tensor_reduce(MX[0:S], SB["s2"][0:S], AX, ALU.max))
                        link(dve.tensor_tensor(P[0:S], SB["s2"][0:S], MX[0:S].unsqueeze(2).to_broadcast([S, H, S]), ALU.subtract))
                    elif kind == "rope":
                        link(dve.tensor_reduce(MX[0:S], sps, AX, ALU.max))
                        for a in range(4):
                            ins = dve.tensor_tensor(P[0:S, 4 * a:4 * a + 4, :],
                                                    PS[0:S, a, 0:4 * S].rearrange("p (b s) -> p b s", b=4),
                                                    MX[0:S, 4 * a:4 * a + 4].unsqueeze(2).to_broadcast([S, 4, S]), ALU.subtract)
                            if a < 3:
                                ins.then_inc(of(L, "win"), 1)
                        dve.wait_ge(*at(L, "win", i * 6 + (3 * k + 3)))
                    else:
                        S0, S2, S3, B8, B9 = P, SB["s2"], SB["s3"], SB["best"][0], SB["best"][1]
                        link(dve.tensor_copy(four(S0), sps))
                        dve.sem_inc(sem("dve_passed"), 1)
                        for hd in range(H):
                            ins = dve.max(B8[0:S, hd, :], S0[0:S, hd, :])
                            if hd < H - 1:
                                ins.then_inc(of(L, "each"), 1)
                        link(ins)
                        dve.wait_ge(*at(L, "each", i * (2 * 3 * (H - 1)) + (k * 3 + 1) * (H - 1)))
                        dve.sem_inc(sem("dve_passed"), 1)
                        for hd in range(H):
                            ins = dve.match_replace(S2[0:S, hd, :], B8[0:S, hd, :], S0[0:S, hd, :], -BIG)
                            if hd < H - 1:
                                ins.then_inc(of(L, "each"), 1)
                        link(ins)
                        dve.wait_ge(*at(L, "each", i * (2 * 3 * (H - 1)) + (k * 3 + 2) * (H - 1)))
                        dve.sem_inc(sem("dve_passed"), 1)
                        for hd in range(H):
                            ins = dve.max(B9[0:S, hd, :], S2[0:S, hd, :])
                            if hd < H - 1:
                                ins.then_inc(of(L, "each"), 1)
                        link(ins)
                        dve.wait_ge(*at(L, "each", i * (2 * 3 * (H - 1)) + (k * 3 + 3) * (H - 1)))
                        link(dve.memset(B9[0:S, :, TOP - 8:8], -BIG))
                        dve.sem_inc(sem("dve_passed"), 1)
                        for hd in range(H):
                            ins = dve.match_replace(S3[0:S, hd, :], B9[0:S, hd, :], S2[0:S, hd, :], -BIG)
                            if hd < H - 1:
                                ins.then_inc(of(L, "last"), 1)
                        link(ins)
                        dve.wait_ge(*at(L, "last", i * (2 * (H - 1)) + (k + 1) * (H - 1)))
                        dve.scalar_tensor_tensor(P[0:S], S3[0:S], -BIG, S0[0:S], ALU.is_le, ALU.mult) \
                            .then_inc(of(L, "each2"), 1)
                        dve.wait_ge(*at(L, "each2", i * 2 + (k + 1)))
                        link(dve.tensor_scalar(MX[0:S], B8[0:S, :, 0], 0.0, None, ALU.max))
                        link(dve.tensor_tensor(P[0:S], P[0:S], MX[0:S].unsqueeze(2).to_broadcast([S, H, S]), ALU.subtract))
                    assert n[0] == steps - 2, (kind, n, steps)
                    if kind == "rope":
                        ins.then_inc(of(L, "sub"), 1)
                    else:
                        dve.sem_inc(of(L, "sub"), 1)
                for k in range(2):
                    P, DEN = SB["p"][k], SB["den"][k]
                    dve.wait_ge(*at(L, "exp", i * 2 + (k + 1)))
                    m = i * (2 * steps) + (2 * (steps - 2) + 2 * k)
                    dve.tensor_reduce(DEN[0:S], P[0:S], AX, ALU.add).then_inc(chain, 1)
                    dve.wait_ge(*at(L, "chain", m + 1))
                    dve.reciprocal(DEN[0:S], DEN[0:S]).then_inc(chain, 1)
                    dve.wait_ge(*at(L, "chain", m + 2))
                    dve.tensor_tensor(P[0:S], P[0:S], DEN[0:S].unsqueeze(2).to_broadcast([S, H, S]), ALU.mult) \
                        .then_inc(of(L, "probs"), 1)
            residual(dve, c + 1, lambda h: dve.wait_ge(*at(L, "y", h + 1)), bank,
                     None if kind == "rope" else wcol(f"{L}_b", 2))

        NT = len(KT_TILES)
        KEY_CHUNKS = [(0, 512), (512, 512), (1024, CTX - 1024)]
        KPART, QPART = (0, 0, 0, 1, 1, 2), (0, 1, 2, 0, 1, 0)
        MASK_ROW, MAX_ROW, ROWS = 96, 98, 101
        PAIR, VW = H // 2, DH + 1

        class Step:

            def __init__(self, k, i=None):
                self.k, self.i = k, i

            def n(self, times, plus=0):
                if self.i is None:
                    return self.k * times + plus
                return self.i * (2 * times) + (self.k * times + plus)

            def buf(self, ahead=0):
                return (self.k + ahead) % 2

            def piece(self, j):
                if self.i is not None:
                    return self.n(PIECES_OF_STEP, BEFORE + j)
                return BEFORE + 6 * PIECES_OF_STEP + (5 + j if self.k == 7 else j if j == 0 else j - 3)

        def cross_buffers():
            lay = Layout()
            two = range(2)
            d = dict(
                o=lay.take(4, T), ctx=[lay.take(CTX) for _ in two], kf=lay.take(CTX),
                v=[lay.take(NT, H, VW) for _ in two], pt=lay.take(2, NT, S),
                mx=[lay.take(H) for _ in two], neg=lay.take(S))
            bf = lay.take_bf16
            d["kp"] = bf(3 * CTX).rearrange("p (c n) -> p c n", c=3)
            d["kk"] = [bf(PAIR * CTX).rearrange("p (a n) -> p a n", a=PAIR) for _ in two]
            d["qq"] = [bf(H * S).rearrange("p (a n) -> p a n", a=PAIR) for _ in two]
            d["mc"] = [bf(3 * S).rearrange("p (c n) -> p c n", c=3) for _ in two]
            d["mask"] = d["m01"] = lay.take(CTX)
            d["q"] = d["kf"][:, 0:T]
            d["mrow"] = [a[:, 0:CTX // 2].bitcast(BF16) for a in (R, SQ)]
            d["ones"] = SQ[0:ROWS - MASK_ROW, 0:CTX // 2].bitcast(BF16)
            d["qp"] = d["pt"].rearrange("p k t s -> p (k t s)").bitcast(BF16).rearrange("p (c b e n) -> p c b e n", c=3, b=NB, e=2)
            d["pt"] = [d["pt"][:, k] for k in two]
            return d

        CB = cross_buffers()
        k_parts = nc.dram_tensor("k_parts", (2, 3, 128, CTX), BF16, kind="Internal").ap()
        q_parts = nc.dram_tensor("q_parts", (3, 128, NB * 2 * S), BF16, kind="Internal").ap()
        RUN = [Step(6), Step(7)]

        def steps(eng, body):
            with eng.Fori(0, (NB - 2) // 2) as i:
                for k in range(2):
                    body(Step(k, i), True, True)
            body(RUN[0], True, False)
            body(RUN[1], False, False)

        def cross_sync(sp, L, c, masked):
            def keys_in(b, ahead):
                k = b.buf(ahead)
                sync_wait(sp, *at(L, "split", b.n(3, 3 * ahead + 3)))
                sp.dma_start(k_parts[k].rearrange("c p n -> p c n"), CB["kp"]).then_inc(of(L, "kw"), 16)
                sync_wait(sp, *at(L, "kw", b.n(16, 16 * ahead + 16)))

            def operand(b, ahead, half_):
                k, done = b.buf(ahead), of(L, f"op{half_}")
                pairs = slice(4 * half_, 4 * half_ + 4)
                for j in range(6):
                    rows = slice(16 * j, 16 * j + 16)
                    sp.dma_start(CB["kk"][k][rows, pairs, :],
                                 k_parts[k, KPART[j]].rearrange("(a r) n -> r a n", a=PAIR)[:, pairs, :]).then_inc(done, 16)
                    sp.dma_start(CB["qq"][k][rows, pairs, :],
                                 q_parts[QPART[j]].rearrange("(a r) n -> r a n", a=PAIR)[:, pairs, bass.ds(b.n(2 * S, 2 * S * ahead), 2 * S)]) \
                        .then_inc(done, 16)
                if masked:
                    sync_wait(sp, *at(L, "mrow", b.n(1, ahead + 1)))
                    sp.dma_start(CB["kk"][k][MASK_ROW:MASK_ROW + 2, pairs, :],
                                 CB["mrow"][k][0:2].unsqueeze(1).to_broadcast([2, 4, CTX])).then_inc(done, 16)

            def maxima(b, ahead, half_):
                sync_wait(sp, *at(L, "mxs", b.n(2, 2 * ahead + half_ + 1)))
                k = b.buf(ahead)
                for part in range(3):
                    sp.dma_start(CB["qq"][k][MAX_ROW + part:MAX_ROW + part + 1, 4 * half_:4 * half_ + 4, :]
                                 .rearrange("c a (e n) -> c (a e) n", e=2), CB["mc"][half_][0:8, part, :]) \
                        .then_inc(of(L, f"mx{half_}"), 16)

            def context(b, ahead):
                k = b.buf(ahead)
                sp.dma_start(CB["ctx"][k], ctx_in[:, bass.ds(b.n(CTX, CTX * ahead), CTX)]).then_inc(of(L, "ctx"), 16)

            def mask(b, ahead):
                if masked:
                    if ahead == 3:
                        sync_wait(sp, *at(L, "kf", b.n(PIECES_OF_STEP, BEFORE + PIECES_OF_STEP)))
                    elif ahead:
                        sync_wait(sp, *at(L, "kf", 3 * ahead))
                    sp.dma_start(CB["mask"].bitcast(I32), mask0_in[bass.ds(b.n(1, ahead), 1), :].partition_broadcast(128)) \
                        .then_inc(of(L, "mask"), 16)

            zero = Step(0)
            x_ready(sp, c, 1)
            context(zero, 0)
            sp.wait_ge(*at(L, "vzero", 1))
            for k in range(2):
                sp.dma_start(CB["kk"][k][MASK_ROW:ROWS], CB["ones"].unsqueeze(1).to_broadcast([ROWS - MASK_ROW, PAIR, CTX])) \
                    .then_inc(of(L, "ones"), 16)
            context(zero, 1)
            mask(zero, 0)
            sp.wait_ge(*at(L, "qf", 3))
            sp.dma_start(q_parts.rearrange("c p n -> p c n"), CB["qp"].rearrange("p c b e n -> p c (b e n)")).then_inc(of(L, "qw"), 16)
            sp.wait_ge(*at(L, "qw", 16))
            sp.wait_ge(*at(L, "ones", 32))
            for ahead in range(2):
                if ahead:
                    mask(zero, 1)
                keys_in(zero, ahead)
                for half_ in range(2):
                    if ahead:
                        sp.wait_ge(*at(L, "scores", 8 * half_ + 1))
                    operand(zero, ahead, half_)
            sp.wait_ge(*at(L, "k", 9))
            context(zero, 2)
            mask(zero, 2)
            maxima(zero, 0, 0)

            def body(b):
                n = 0 if b.i is not None else b.k
                maxima(b, 0, 1)
                if n + 2 < NB:
                    keys_in(b, 2)
                if n + 1 < NB:
                    maxima(b, 1, 0)
                if n + 2 < NB:
                    sync_wait(sp, *at(L, "pv", b.n(H, 2 + 8)))
                    operand(b, 2, 0)
                if n + 3 < NB:
                    sync_wait(sp, *at(L, "k", b.n(PIECES_OF_STEP, BEFORE + PIECES_OF_STEP)))
                    context(b, 3)
                    mask(b, 3)
                if n + 2 < NB:
                    sync_wait(sp, *at(L, "pv", b.n(H, 2 + H)))
                    operand(b, 2, 1)

            with sp.Fori(0, 2) as i:
                for k in range(2):
                    body(Step(k, i))
            for k in range(4, NB):
                body(Step(k))

        def cross_pe(pe, L, c, masked):
            phase1 = MAX_ROW if masked else MASK_ROW
            ops = 16 * (13 if masked else 12)

            def piece(n, mms):
                if not isinstance(n, int) or n:
                    pe.wait_ge(*at(L, "kf", n))
                for dst, lhs, rhs in mms:
                    mm = pe.matmul(dst, lhs, rhs, start=True, stop=True)
                mm.then_inc(of(L, "k"), 1)

            def keys(b, ahead, n, j):
                if j == 0:
                    pe.wait_ge(*at(L, "ctx", b.n(16, 16 * ahead + 16) if b.i is not None or ahead > 1 else 32))
                c0, m = KEY_CHUNKS[j]
                piece(n, [(PS[:, 6, 0:m], w(f"{L}_wk"), CB["ctx"][b.buf(ahead)][:, c0:c0 + m])])

            def values(b, ahead, n, j):
                ctx = CB["ctx"][b.buf(ahead)]
                piece(n, [(PS[0:m, 6, (t % 4) * 128:(t % 4) * 128 + 128], ctx[:, t0:t0 + m], w(f"{L}_wv"))
                                for t, (t0, m) in list(enumerate(KT_TILES))[4 * j:4 * j + 4]])

            def turn_maxima(b, ahead, n, j):
                pe.wait_ge(*at(L, "nm", b.n(H, H * ahead + 8 * j + 8)))
                pe.wait_ge(*at(L, "kf", n))
                pe.transpose(PS[0:8, 6, 0:S], CB["mx"][b.buf(ahead)][0:S, 8 * j:8 * j + 8], ident[0:S, 0:S]) \
                    .then_inc(of(L, "k"), 1)

            def rows_of_queries(b, ahead, h):
                if h % 8 == 0:
                    pe.wait_ge(*at(L, f"op{h // 8}", b.n(ops, ops * (ahead + 1))))
                if b.i is not None or ahead or h:
                    pe.wait_ge(*at(L, "nm", b.n(H, H * ahead + h)))
                k = b.buf(ahead)
                for c0, m in KEY_CHUNKS:
                    mm = pe.matmul(PSF[0:S, c0:c0 + m], CB["qq"][k][0:phase1, h // 2, (h % 2) * S:(h % 2 + 1) * S],
                                   CB["kk"][k][0:phase1, h // 2, c0:c0 + m], start=True, stop=True)
                mm.then_inc(of(L, "scores"), 1)

            def rows_of_keys(b, ahead, h):
                if h % 8 == 0:
                    pe.wait_ge(*at(L, f"mx{h // 8}", b.n(48, 48 * (ahead + 1))))
                k = b.buf(ahead)
                for g in range(3):
                    if b.i is not None or ahead or h:
                        pe.wait_ge(*at(L, "exp", b.n(4 * H, 4 * (H * ahead + h - 1) + (1, 2, 4)[g])))
                    for t in range(4 * g, 4 * g + 4):
                        t0, m = KT_TILES[t]
                        mm = pe.matmul(PS[0:m, 3 + g, (t % 4) * S:(t % 4 + 1) * S], CB["kk"][k][0:ROWS, h // 2, t0:t0 + m],
                                       CB["qq"][k][0:ROWS, h // 2, (h % 2) * S:(h % 2 + 1) * S], start=True, stop=True)
                    mm.then_inc(of(L, "t"), 1)

            def product(b, h):
                pe.wait_ge(*at(L, "exp", b.n(4 * H, 4 * (h + 1))))
                if h == 0:
                    pe.wait_ge(*at(L, "o", b.n(1, 1)))
                q = h % 4
                for t, (t0, m) in enumerate(KT_TILES):
                    mm = pe.matmul(PS[SLOT * q:SLOT * q + VW, 7, (h // 4) * S:(h // 4 + 1) * S],
                                   CB["v"][b.buf()][0:m, t, h, :], CB["pt"][h % 2][0:m, t, :], start=(t == 0), stop=(t == NT - 1))
                mm.then_inc(of(L, "pv"), 1)

            loaded(pe, f"{L}_wq")
            for h in range(2):
                x_ready(pe, c, h)
                pe.matmul(bank(h), w(f"{L}_wq"), half(X, h), start=True, stop=True).then_inc(of(L, "q"), 1)
            zero = Step(0)
            for ahead in range(2):
                for j in range(3):
                    keys(zero, ahead, 3 * ahead + j, j)
            for j in range(3):
                values(zero, 0, 6 + j, j)
            pe.sem_inc(of(L, "pv"), 2)
            for h in range(H):
                rows_of_queries(zero, 0, h)
                if h == 9:
                    turn_maxima(zero, 0, 9, 0)
            pe.wait_ge(*at(L, "ones", 32))
            rows_of_keys(zero, 0, 0)

            def body(b, following, more):
                n = b.piece
                for h in range(H):
                    if following:
                        rows_of_queries(b, 1, h)
                    if h < H - 1:
                        rows_of_keys(b, 0, h + 1)
                    elif following:
                        rows_of_keys(b, 1, 0)
                    if h == 1:
                        turn_maxima(b, 0, n(0), 1)
                    if more and 2 <= h <= 4:
                        keys(b, 2, n(h - 1), h - 2)
                    if following:
                        if h == 9:
                            turn_maxima(b, 1, n(4), 0)
                        if 10 <= h <= 12:
                            values(b, 1, n(h - 5), h - 10)
                    product(b, h)

            steps(pe, body)
            pe.wait_ge(*at(L, "o", 1 + NB))
            selx = w("selx")
            for g in range(4):
                for h in range(2):
                    if 2 * g + h >= 6:
                        pe.wait_ge(*at(L, "normed", 2 * g + h - 5))
                    pe.matmul(bank((2 * g + h) % 6), selx, CB["o"][:, g, h * HALF:(h + 1) * HALF], start=True, stop=True) \
                        .then_inc(of(L, "bc"), 1)
            pe.wait_ge(*at(L, "normed", 8))
            project_out_pe(pe, L, CB["o"])
            norm_pe(pe, c + 1)

        def cross_pool(pool, L, c, masked):
            zero = Step(0)

            def split(b, ahead):
                n = lambda j: b.n(3, 3 * ahead + j)
                pool.wait_ge(*at(L, "split_act", b.n(3, 3 * ahead + 3)))
                pool.tensor_tensor(CB["kf"], CB["kf"], CB["kp"][:, 0, :], ALU.subtract).then_inc(of(L, "split"), 1)
                pool_wait(pool, *at(L, "split", n(1)))
                pool.tensor_copy(CB["kp"][:, 1, :], CB["kf"]).then_inc(of(L, "split"), 1)
                pool.wait_ge(*at(L, "split", n(2)))
                pool.tensor_tensor(CB["kp"][:, 2, :], CB["kf"], CB["kp"][:, 1, :], ALU.subtract).then_inc(of(L, "split"), 1)

            loaded(pool, "headmask")
            x_ready(pool, c, 1)
            for ahead in range(2):
                split(zero, ahead)

            def body(b, following, more):
                if more:
                    split(b, 2)

            with pool.Fori(0, (NB - 2) // 2) as i:
                for k in range(2):
                    body(Step(k, i), True, True)

        def cross_act(act, L, c, masked):
            last = KT_TILES[-1][1]

            def first_part(b, ahead, n, j):
                act.wait_ge(*at(L, "kf", n + 1))
                if j == 0 and (b.i is not None or ahead):
                    act.wait_ge(*at(L, "kw", b.n(16, 16 * ahead)))
                c0, m = KEY_CHUNKS[j]
                act.activation(CB["kp"][:, 0, c0:c0 + m], CB["kf"][:, c0:c0 + m], ACT.Copy).then_inc(of(L, "split_act"), 1)

            for ahead in range(2):
                for j in range(3):
                    first_part(Step(0), ahead, 3 * ahead + j, j)

            def body(b, following, more):
                for h in range(H):
                    if more and 3 <= h <= 5:
                        first_part(b, 2, b.piece(h - 2), h - 3)
                    pt = CB["pt"][h % 2]
                    act.wait_ge(*at(L, "pv", b.n(H, h + 1)))
                    for g in range(3):
                        act.wait_ge(*at(L, "t", b.n(3 * H, 3 * h + g + 1)))
                        for t, m, rows in ((4 * g, 4, 128),) if g < 2 else ((8, 3, 128), (11, 1, last)):
                            act.activation(pt[0:rows, t:t + m, :].rearrange("p t s -> p (t s)"),
                                           PS[0:rows, 3 + g, (t % 4) * S:(t % 4 + m) * S], ACT.Exp).then_inc(of(L, "exp"), 1)

            steps(act, body)
            norm_act(act, c + 1)

        def cross_dve(dve, L, c, masked):
            has_bias = L == "x0"
            scale = 1.0 if L == "x0" else DH ** -0.5
            chain, links = of(L, "mlink"), 4

            def mask(b, ahead):
                k = b.buf(ahead)
                dve.wait_ge(*at(L, "mask", b.n(16, 16 * ahead + 16)))
                dve.tensor_scalar(CB["m01"], CB["mask"].bitcast(I32), 0.0, 0.0, ALU.is_equal, ALU.is_equal).then_inc(of(L, "m01"), 1)
                if b.i is not None:
                    dve.wait_ge(*at(L, "op1", b.n(208, 208 * (ahead - 1))))
                elif ahead:
                    dve.wait_ge(*at(L, "ones", 32))
                dve.wait_ge(*at(L, "m01", b.n(1, ahead + 1)))
                dve.tensor_scalar(CB["mrow"][k][0:2], CB["m01"][0:2], 0.0, wcol("maskab", 0)[0:2], ALU.is_equal, ALU.mult) \
                    .then_inc(of(L, "mrow"), 1)

            def key_piece(b, ahead, n, j):
                c0, m = KEY_CHUNKS[j]
                if j == 0:
                    if b.i is not None or ahead:
                        dve.wait_ge(*at(L, "split", b.n(3, 3 * ahead)))
                dve.wait_ge(*at(L, "k", n + 1))
                src, dst = PS[:, 6, 0:m], CB["kf"][:, c0:c0 + m]
                if masked:
                    ins = dve.scalar_tensor_tensor(dst, src, wcol(f"{L}_b", 1), CB["m01"][:, c0:c0 + m], ALU.add, ALU.mult)
                else:
                    ins = dve.tensor_copy(dst, src)
                ins.then_inc(of(L, "kf"), 1)

            def value_piece(b, ahead, n, j):
                dve.wait_ge(*at(L, "k", n + 1))
                for t, m, rows in ((4 * j, 4, 128),) if j < 2 else ((8, 3, 128), (11, 1, KT_TILES[-1][1])):
                    src = PS[0:rows, 6, (t % 4) * 128:(t % 4 + m) * 128].rearrange("p (t h d) -> p t h d", t=m, h=H)
                    dst = CB["v"][b.buf(ahead)][0:rows, t:t + m, :, 0:DH]
                    if has_bias:
                        bv = w(f"{L}_bv", rows).rearrange("p (h d) -> p h d", h=H).unsqueeze(1).to_broadcast([rows, m, H, DH])
                        ins = dve.tensor_tensor(dst, src, bv, ALU.add)
                    else:
                        ins = dve.tensor_copy(dst, src)
                ins.then_inc(of(L, "kf"), 1)

            def split_maxima(b, ahead, n, j):
                dve.wait_ge(*at(L, "k", n + 1))
                mc, neg, src = CB["mc"][j][0:8], CB["neg"][0:8], PS[0:8, 6, 0:S]
                base = 2 * ahead + j
                done = lambda m: dve.wait_ge(*at(L, "mlink", b.n(2 * links, base * links + m)))
                dve.tensor_copy(mc[:, 0, :], src).then_inc(chain, 1)
                done(1)
                dve.tensor_tensor(neg, src, mc[:, 0, :], ALU.subtract).then_inc(chain, 1)
                done(2)
                dve.sem_inc(of(L, "kf"), 1)
                dve.tensor_copy(mc[:, 1, :], neg).then_inc(chain, 1)
                done(3)
                dve.tensor_tensor(mc[:, 2, :], neg, mc[:, 1, :], ALU.subtract).then_inc(chain, 1)
                done(4)
                dve.sem_inc(of(L, "mxs"), 1)

            def maximum(b, ahead, h):
                dve.wait_ge(*at(L, "scores", b.n(H, H * ahead + h + 1)))
                dve.tensor_reduce(CB["mx"][b.buf(ahead)][0:S, h:h + 1], PSF[0:S, 0:CTX], AX, ALU.max, negate=True) \
                    .then_inc(of(L, "nm"), 1)

            x_ready(dve, c, 1)
            dve.memset(CB["ones"], 1.0).then_inc(of(L, "vzero"), 1)
            for k in range(2):
                dve.memset(CB["qq"][k][MASK_ROW:128], 1.0 if masked else 0.0)
                dve.memset(CB["v"][k][:, :, :, DH:VW].rearrange("p t h d -> p (t h) d"), 1.0)
            dve.memset(PS[:, 7, 0:4 * S], 0.0).then_inc(of(L, "vzero"), 1)
            loaded(dve, f"{L}_wq")
            for h in range(2):
                dve.wait_ge(*at(L, "q", h + 1))
                dve.tensor_scalar(half(CB["q"], h), bank(h), wcol(f"{L}_b", 0) if has_bias else 0.0, scale,
                                  ALU.add, ALU.mult).then_inc(of(L, "qlink"), 1)
            loaded(dve, "parity")
            by_batch = lambda a: a.rearrange("p (b n) -> p b n", b=NB)
            part = CB["kp"][:, 0, 0:T]
            for j in range(3):
                dve.wait_ge(*at(L, "qlink", 2 + 2 * j))
                dve.tensor_copy(part, CB["q"]).then_inc(of(L, "qlink"), 1)
                dve.wait_ge(*at(L, "qlink", 3 + 2 * j))
                for e in range(2):
                    ins = dve.tensor_scalar(CB["qp"][:, j, :, e, :], by_batch(part), wcol("parity", e), None, ALU.mult)
                ins.then_inc(of(L, "qf"), 1)
                dve.wait_ge(*at(L, "qf", j + 1))
                dve.tensor_tensor(CB["q"], CB["q"], part, ALU.subtract).then_inc(of(L, "qlink"), 1)
            dve.sem_inc(of(L, "o"), 1)
            dve.wait_ge(*at(L, "qlink", 8))
            zero = Step(0)
            for ahead in range(2):
                if masked:
                    mask(zero, ahead)
                for j in range(3):
                    key_piece(zero, ahead, 3 * ahead + j, j)
            for j in range(3):
                value_piece(zero, 0, 6 + j, j)
            for h in range(H):
                maximum(zero, 0, h)
                if h == 9:
                    split_maxima(zero, 0, 9, 0)

            def body(b, following, more):
                n = b.piece
                for h in range(H):
                    if following:
                        maximum(b, 1, h)
                    if h == 1:
                        split_maxima(b, 0, n(0), 1)
                        if more and masked:
                            mask(b, 2)
                    if more and 2 <= h <= 4:
                        key_piece(b, 2, n(h - 1), h - 2)
                    if following:
                        if h == 9:
                            split_maxima(b, 1, n(4), 0)
                        if 10 <= h <= 12:
                            value_piece(b, 1, n(h - 5), h - 10)
                dve.wait_ge(*at(L, "pv", b.n(H, H + 2)))
                dve.tensor_copy(CB["o"][:, :, bass.ds(b.n(S), S)], PS[:, 7, 0:4 * S].rearrange("p (g s) -> p g s", g=4)) \
                    .then_inc(of(L, "o"), 1)

            steps(dve, body)
            for g in range(4):
                for h in range(2):
                    n, rd = 2 * g + h, CB["kf"][:, (h % 2) * HALF:(h % 2 + 1) * HALF]
                    dve.wait_ge(*at(L, "bc", n + 1))
                    if n >= 2:
                        dve.wait_ge(*at(L, "normed", n - 1))
                    dve.reciprocal(rd, bank(n % 6)).then_inc(of(L, "rd"), 1)
                    dve.wait_ge(*at(L, "rd", n + 1))
                    o = CB["o"][:, g, h * HALF:(h + 1) * HALF]
                    dve.tensor_tensor(o, o, rd, ALU.mult).then_inc(of(L, "normed"), 1)
            residual(dve, c + 1, lambda h: dve.wait_ge(*at(L, "y", h + 1)), bank,
                     wcol(f"{L}_b", 2 if has_bias else 0))

        OTHER_SYNC, OTHER_POOL, OTHER_ACT, OTHER_DVE, OTHER_PE = {}, {}, {}, {}, {}

        def moe_buffers(E, width):
            lay = Layout()
            return dict(
                x=lay.take(T), lg=lay.take(NB, 2 * E if E > 8 else E + 8), tmp=lay.take(NB, E), pr=lay.take(NB, E),
                best=lay.take(NB, 8), mv=lay.take(NB, 8), rep=lay.take(NB, 2 * E if E > 8 else E + 8),
                den=lay.take(NB), rd=lay.take(NB), gt=lay.take(T),
                a=[lay.take(HALF) for _ in range(2)], s=[lay.take(HALF) for _ in range(2)],
                lin=[lay.take(HALF) for _ in range(2)], w=[lay.take(width) for _ in range(2)])

        MOE = {"f0": (E0, K0, EXPERT0, moe_buffers(E0, EXPERT0)), "f3": (E3, K3, EXPERT3, moe_buffers(E3, EXPERT3))}

        def moe_sync(sp, L, c):
            E, _, width, B = MOE[L]
            x_ready(sp, c, 1)
            src = expert0_in if L == "f0" else expert3_in
            with sp.Fori(0, E // 2) as i:
                for k in range(2):
                    sp.wait_ge(*at(L, "y_done", i * 4 + (2 * k + 1)))
                    sp.dma_start(B["w"][k], src[:, bass.ds(i * (2 * width) + k * width, width)]) \
                        .then_inc(of(L, f"w{k}"), 16)

        def moe_pe(pe, L, c):
            E, _, width, B = MOE[L]
            w2 = 128 if L == "f0" else 256
            loaded(pe, f"{L}_wg")
            x = X if L == "f0" else B["x"]
            if L == "f3":
                for h in range(2):
                    pe.wait_ge(*at(L, "sq", h + 1))
                    pe.matmul(bank(6 + h), mean_w[:, :], half(SQ, h), start=True, stop=True).then_inc(of(L, "ms"), 1)
                pe.wait_ge(*at(L, "x", 2))
            else:
                x_ready(pe, c, 0)
                x_ready(pe, c, 1)
            for b in range(NB):
                mm = pe.matmul(PS[0:S, 0, b * E:(b + 1) * E], x[:, b * S:(b + 1) * S], w(f"{L}_wg"), start=True, stop=True)
            mm.then_inc(of(L, "logits"), 1)
            pe.wait_ge(*at(L, "gates", 1))
            for b in range(NB):
                mm = pe.transpose(PS[0:E, 2 + b // 4, (b % 4) * S:(b % 4 + 1) * S], B["pr"][0:S, b, :], ident[0:S, 0:S])
            mm.then_inc(of(L, "gt"), 1)
            pe.wait_ge(*at(L, "gtc", 1))
            for h in range(2):
                pe.matmul(bank(h), w(f"{L}_b2", E), half(B["gt"][0:E], h), start=True, stop=False, skip_group_check=True)
            pe.sem_inc(of(L, "y_done"), 3)
            with pe.Fori(0, E // 2) as i:
                def second(j):
                    pe.wait_ge(*at(L, "act", i * 4 + (j + 3)))
                    pe.matmul(bank(j % 2), B["w"][j // 2][:, w2:w2 + 128], B["a"][j % 2], start=False, stop=False, skip_group_check=True) \
                        .then_inc(of(L, "y_done"), 1)

                for j in range(4):
                    wk = B["w"][j // 2]
                    if j % 2 == 0:
                        pe.wait_ge(*at(L, f"w{j // 2}", i * 16 + 16))
                    pe.wait_ge(*at(L, "up", i * 4 + (j + 1)))
                    if L == "f3":
                        pe.matmul(bank(6 + j % 2), wk[:, 128:256], half(x, j % 2), start=True, stop=True)
                    pe.matmul(bank(2 + j % 2), wk[:, 0:128], half(x, j % 2), start=True, stop=True) \
                        .then_inc(of(L, "h"), 1)
                    pe.wait_ge(*at(L, "act", i * 4 + (j + 1)))
                    sel = wk[0:E, w2 + 128:w2 + 256]
                    pe.matmul(bank(4 + j % 2), sel, half(B["gt"][0:E], j % 2), start=True, stop=True) \
                        .then_inc(of(L, "bc"), 1)
                    if j:
                        second(j - 1)
                second(3)
            pe.wait_ge(*at(L, "y_done", 3 + 2 * E))
            pe.sem_inc(of(L, "y"), 1)
            norm_pe(pe, c + 1)

        def moe_pool(pool, L, c):
            E, _, width, B = MOE[L]
            if L == "f3":
                with pool.Fori(0, E // 2) as i:
                    for j in range(4):
                        pool_wait(pool, *at(L, "lin", i * 4 + (j + 1)))
                        pool.tensor_scalar(B["lin"][j % 2], B["lin"][j % 2], 7.0, 1.0, ALU.min, ALU.add) \
                            .then_inc(of(L, "lin1"), 1)
                        pool.wait_ge(*at(L, "sig", i * 4 + (j + 1)))
                        pool.tensor_tensor(B["s"][j % 2], B["s"][j % 2], B["a"][j % 2], ALU.mult).then_inc(of(L, "glu"), 1)
                        pool.wait_ge(*at(L, "lin1", i * 4 + (j + 1)))
                        pool.wait_ge(*at(L, "glu", i * 4 + (j + 1)))
                        pool.tensor_tensor(B["a"][j % 2], B["s"][j % 2], B["lin"][j % 2], ALU.mult) \
                            .then_inc(of(L, "swiglu"), 1)

        def moe_act(act, L, c):
            E, _, width, B = MOE[L]
            if L == "f3":
                for h in range(2):
                    x_ready(act, c, h)
                    act.activation(half(SQ, h), half(X, h), ACT.Square).then_inc(of(L, "sq"), 1)
                for h in range(2):
                    act.wait_ge(*at(L, "ms", h + 1))
                    act.activation(half(SQ, h), bank(6 + h), ACT.Sqrt, bias=epsc[:, :]).then_inc(of(L, "rms"), 1)
            act.wait_ge(*at(L, "sub", 1))
            act.activation(B["tmp"][0:S], B["tmp"][0:S], ACT.Exp).then_inc(of(L, "exp"), 1)
            if L == "f0":
                act.sem_inc(of(L, "up"), 2)
            with act.Fori(0, E // 2) as i:
                for j in range(4):
                    if L == "f0":
                        act.wait_ge(*at(L, "h", i * 4 + (j + 1)))
                        act.wait_ge(*at(L, "y_done", i * 4 + (j + 2)))
                        act.activation(B["a"][j % 2], bank(2 + j % 2), ACT.Gelu, bias=B["w"][j // 2][:, width - 1:width]) \
                            .then_inc(of(L, "up"), 1)
                    else:
                        act.wait_ge(*at(L, "glu_in", i * 4 + (j + 1)))
                        act.activation(B["s"][j % 2], B["a"][j % 2], ACT.Sigmoid, scale=1.702).then_inc(of(L, "sig"), 1)
            norm_act(act, c + 1)

        def moe_dve(dve, L, c):
            E, K, width, B = MOE[L]
            chain, n = of(L, "chain"), [0]

            def link(ins):
                n[0] += 1
                ins.then_inc(chain, 1)
                dve.wait_ge(*at(L, "chain", n[0]))

            x_ready(dve, c, 1)
            if L == "f3":
                for h in range(2):
                    dve.wait_ge(*at(L, "rms", h + 1))
                    link(dve.reciprocal(half(SQ, h), half(SQ, h)))
                    dve.scalar_tensor_tensor(half(B["x"], h), half(X, h), wcol("f3_scale"), half(SQ, h), ALU.mult, ALU.mult) \
                        .then_inc(of(L, "x"), 1)
            link(dve.memset(B["lg"][0:S], -BIG))
            link(dve.memset(B["mv"][0:S], -BIG))
            dve.wait_ge(*at(L, "logits", 1))
            lg, tmp, pr = B["lg"][0:S, :, 0:E], B["tmp"][0:S], B["pr"][0:S]
            ps = PS[0:S, 0, 0:NB * E].rearrange("p (b e) -> p b e", b=NB)
            wide = lambda a, m: a.unsqueeze(2).to_broadcast([S, NB, m])
            den, rd = B["den"][0:S], B["rd"][0:S]
            if L == "f0":
                link(dve.tensor_reduce(den, ps, AX, ALU.max))
                dve.tensor_tensor(tmp, ps, wide(den, E), ALU.subtract).then_inc(of(L, "sub"), 1)
                dve.wait_ge(*at(L, "exp", 1))
                link(dve.tensor_reduce(den, tmp, AX, ALU.add))
                link(dve.reciprocal(rd, den))
                link(dve.tensor_tensor(lg, tmp, wide(rd, E), ALU.mult))
            else:
                link(dve.tensor_tensor(lg, ps, w("f3_bg", S).unsqueeze(1).to_broadcast([S, NB, E]), ALU.add))
            for b in range(NB):
                ins = dve.max(B["best"][0:S, b, :], B["lg"][0:S, b, :])
                if b < NB - 1:
                    ins.then_inc(of(L, "each"), 1)
            link(ins)
            dve.wait_ge(*at(L, "each", NB - 1))
            link(dve.tensor_copy(B["mv"][0:S, :, 0:K], B["best"][0:S, :, 0:K]))
            for b in range(NB):
                ins = dve.match_replace(B["rep"][0:S, b, :], B["mv"][0:S, b, :], B["lg"][0:S, b, :], -BIG)
                if b < NB - 1:
                    ins.then_inc(of(L, "each"), 1)
            link(ins)
            dve.wait_ge(*at(L, "each", 2 * (NB - 1)))
            if L == "f0":
                link(dve.scalar_tensor_tensor(pr, B["rep"][0:S, :, 0:E], -BIG, lg, ALU.is_le, ALU.mult))
                link(dve.tensor_tensor(den, B["best"][0:S, :, 0], B["best"][0:S, :, 1], ALU.add))
                link(dve.tensor_scalar(den, den, 1e-6, None, ALU.add))
            else:
                dve.tensor_tensor(tmp, lg, wide(B["best"][0:S, :, 0], E), ALU.subtract).then_inc(of(L, "sub"), 1)
                dve.wait_ge(*at(L, "exp", 1))
                link(dve.scalar_tensor_tensor(pr, B["rep"][0:S, :, 0:E], -BIG, tmp, ALU.is_le, ALU.mult))
                link(dve.tensor_reduce(den, pr, AX, ALU.add))
            link(dve.reciprocal(rd, den))
            dve.tensor_tensor(pr, pr, wide(rd, E), ALU.mult).then_inc(of(L, "gates"), 1)
            dve.wait_ge(*at(L, "gt", 1))
            dve.tensor_copy(B["gt"][0:E].rearrange("p (a s) -> p a s", a=2), PS[0:E, 2:4, 0:HALF]).then_inc(of(L, "gtc"), 1)
            dve.sem_inc(of(L, "act"), 2)
            if L == "f3":
                dve.sem_inc(of(L, "up"), 2)
            with dve.Fori(0, E // 2) as i:
                def gate(j):
                    dve.wait_ge(*at(L, "bc", i * 4 + (j + 1)))
                    if L == "f0":
                        dve.wait_ge(*at(L, "up", i * 4 + (j + 3)))
                    else:
                        dve.wait_ge(*at(L, "swiglu", i * 4 + (j + 1)))
                    dve.tensor_tensor(B["a"][j % 2], B["a"][j % 2], bank(4 + j % 2), ALU.mult).then_inc(of(L, "act"), 1)

                for j in range(4):
                    if L == "f3":
                        b1 = B["w"][j // 2][:, width - 2:width - 1]
                        b1l = B["w"][j // 2][:, width - 1:width]
                        dve.wait_ge(*at(L, "h", i * 4 + (j + 1)))
                        dve.wait_ge(*at(L, "y_done", i * 4 + (j + 2)))
                        dve.tensor_scalar(B["a"][j % 2], bank(2 + j % 2), b1, 7.0, ALU.add, ALU.min) \
                            .then_inc(of(L, "glu_in"), 1)
                        dve.tensor_scalar(B["lin"][j % 2], bank(6 + j % 2), b1l, 7.0, ALU.add, ALU.max) \
                            .then_inc(of(L, "lin"), 1)
                        dve.wait_ge(*at(L, "lin", i * 4 + (j + 1)))
                        dve.sem_inc(of(L, "up"), 1)
                        if j:
                            gate(j - 1)
                    else:
                        gate(j)
                if L == "f3":
                    gate(3)
            assert L == "f3" or n[0] == F0_CHAIN, n
            if L == "f0":
                residual(dve, c + 1, lambda h: dve.wait_ge(*at(L, "y", 1)), bank)
            else:
                norm_dve(dve, c + 1, lambda h: (dve.wait_ge(*at(L, "y", 1)),
                                                dve.scalar_tensor_tensor(half(R, h), half(X, h), 2.0, bank(h), ALU.mult, ALU.add))[1])

        OTHER_SYNC, OTHER_POOL, OTHER_ACT, OTHER_DVE, OTHER_PE = {}, {}, {}, {}, {}

        NST, PAD = 16, 3

        def m1_buffers():
            lay = Layout()
            return dict(
                n=lay.take(T), xcp=lay.take(2, NB, S + PAD), xc=lay.take(2, T), z=lay.take(2, T), dbc=lay.take(T),
                u=lay.take(2, T), dtn=lay.take(2, T), aexp=lay.take(2, NST), y=lay.take(2, T), xm=lay.take(T),
                f=lay.take(2, T), t=[lay.take(2, T) for _ in range(4)],
                da=[lay.take(T) for _ in range(2)], dbx=[lay.take(T) for _ in range(2)],
                h=[lay.take(T) for _ in range(2)], hc=[lay.take(T) for _ in range(2)])

        MB = m1_buffers()

        def hcol(a, j, h):
            return a[:, j, h * HALF:(h + 1) * HALF]

        def m1_pe(pe):
            loaded(pe, "m_in")
            norm_pe(pe, C_M1)
            for h in range(2):
                x_ready(pe, C_M1, h)
                for j in range(4):
                    pe.matmul(bank(2 * j + h), w("m_in")[:, 128 * j:128 * j + 128], half(MB["n"], h), start=True, stop=True) \
                        .then_inc(sem("m_xz"), 1)
            pe.wait_ge(sem("m_xc"), 2)
            pe.wait_ge(sem("m_z"), 4)
            for h in range(2):
                for j in range(2):
                    mm = pe.matmul(PS[0:40, h, 0:HALF], w("m_xp")[:, 40 * j:40 * j + 40], hcol(MB["xc"], j, h),
                                   start=(j == 0), stop=(j == 1))
                mm.then_inc(sem("m_dbc"), 1)
            pe.wait_ge(sem("m_dbcf"), 2)
            for j in range(2):
                for h in range(2):
                    pe.matmul(bank(2 + 2 * j + h), w("m_dtw", 40)[:, 128 * j:128 * j + 128], half(MB["dbc"][0:40], h),
                              start=True, stop=True).then_inc(sem("m_dt"), 1)
            pe.wait_ge(sem("m_dtb_added"), 4)
            sel = w("m_sel", 40).rearrange("p (n c m) -> p n c m", n=NST, c=2)
            for n in range(NST):
                if n >= 2:
                    pe.wait_ge(sem("m_hc"), 2 * n - 2)
                for part in range(2):
                    for h in range(2):
                        mm = pe.matmul(bank(4 * (n % 2) + 2 * part + h), sel[:, n, part, :], half(MB["dbc"][0:40], h),
                                       start=True, stop=True)
                mm.then_inc(sem("m_bc"), 1)
            pe.wait_ge(sem("m_gated"), 2)
            for h in range(2):
                for j in range(2):
                    mm = pe.matmul(bank(h), w("m_out")[:, 128 * j:128 * j + 128], hcol(MB["y"], j, h), start=(j == 0), stop=(j == 1))
                mm.then_inc(sem("m_o"), 1)
            norm_pe(pe, C_M2)
            for h in range(2):
                x_ready(pe, C_M2, h)
                for j in range(2):
                    pe.matmul(bank(2 * j + h), w("m_w1")[:, 128 * j:128 * j + 128], half(MB["n"], h), start=True, stop=True) \
                        .then_inc(sem("m_xz"), 1)
            for h in range(2):
                pe.wait_ge(sem("m_z"), 4 + 2 * h + 2)
                for j in range(2):
                    mm = pe.matmul(bank(4 + h), w("m_w2")[:, 128 * j:128 * j + 128], hcol(MB["f"], j, h), start=(j == 0), stop=(j == 1))
                mm.then_inc(sem("m_o"), 1)
            norm_pe(pe, C_M)

        def m1_pool(pool):
            x_ready(pool, C_F0, 1)
            pool.memset(MB["xcp"][:, :, :, 0:PAD].rearrange("p a b s -> p (a b) s"), 0.0).then_inc(sem("m_pad"), 1)
            for n in range(NST):
                for j in range(2):
                    m = 2 * n + j
                    pool.wait_ge(sem("m_da"), m + 1)
                    pool.memset(MB["da"][j].rearrange("p (b s) -> p b s", b=NB)[:, :, 0:1], 0.0).then_inc(sem("m_cut"), 1)
                for j in range(2):
                    m = 2 * n + j
                    pool.wait_ge(sem("m_hc"), m + 1)
                    if n == 0:
                        pool.tensor_copy(MB["y"][:, j, :], MB["hc"][j]).then_inc(sem("m_sum"), 1)
                    else:
                        pool.wait_ge(sem("m_sum"), m - 1)
                        pool.tensor_tensor(MB["y"][:, j, :], MB["y"][:, j, :], MB["hc"][j], ALU.add).then_inc(sem("m_sum"), 1)

        def m1_act(act):
            loaded(act, "m_in")
            norm_act(act, C_M1)
            act.activation(MB["aexp"].rearrange("p a b -> p (a b)"), w("m_alog"), ACT.Exp).then_inc(sem("m_aexp"), 1)
            for j in range(2):
                for h in range(2):
                    act.wait_ge(sem("m_xz"), 4 * h + j + 3)
                    act.activation(hcol(MB["z"], j, h), bank(4 + 2 * j + h), ACT.Silu).then_inc(sem("m_z"), 1)
            for j in range(2):
                act.wait_ge(sem("m_conv"), 4 * (j + 1))
                act.activation(MB["xc"][:, j, :], MB["t"][0][:, j, :], ACT.Silu, bias=wcol("m_conv", 5 * j + 4)) \
                    .then_inc(sem("m_xc"), 1)
            for h in range(2):
                act.wait_ge(sem("m_dbc"), h + 1)
                act.activation(half(MB["dbc"][0:40], h), PS[0:40, h, 0:HALF], ACT.Copy).then_inc(sem("m_dbcf"), 1)
            act.wait_ge(sem("m_dtb_added"), 4)
            act.activation(MB["t"][1], MB["t"][0], ACT.Abs).then_inc(sem("m_e"), 1)
            act.wait_ge(sem("m_e"), 1)
            act.activation(MB["t"][1], MB["t"][1], ACT.Exp, scale=-1.0).then_inc(sem("m_e"), 1)
            act.wait_ge(sem("m_sp"), 1)
            act.activation(MB["t"][3], MB["t"][2], ACT.Ln).then_inc(sem("m_ln"), 1)
            act.wait_ge(sem("m_dtn"), 2)
            act.wait_ge(sem("m_aexp"), 1)
            for n in range(NST):
                for j in range(2):
                    m = 2 * n + j
                    if m >= 2:
                        act.wait_ge(sem("m_scan"), m - 1)
                    act.activation(MB["da"][j], MB["dtn"][:, j, :], ACT.Exp, scale=MB["aexp"][:, j, n:n + 1]) \
                        .then_inc(sem("m_da"), 1)
            norm_act(act, C_M2)
            for h in range(2):
                for j in range(2):
                    act.wait_ge(sem("m_xz"), 8 + 2 * h + j + 1)
                    act.activation(hcol(MB["f"], j, h), bank(2 * j + h), ACT.Gelu, bias=wcol("m_b1", j)).then_inc(sem("m_z"), 1)
            norm_act(act, C_M)

        def m1_dve(dve):
            loaded(dve, "m_in")
            rows = lambda h: (x_ready(dve, C_F0, h), dve.tensor_copy(half(R, h), half(X, h)))[1]
            norm_dve(dve, C_M1, rows, MB["n"], (wcol("m_ln1", 0), wcol("m_ln1", 1)))
            t = MB["t"]
            for h in range(2):
                for j in range(2):
                    dve.wait_ge(sem("m_xz"), 4 * h + j + 1)
                    dve.tensor_copy(MB["xcp"][:, j, 4 * h:4 * h + 4, PAD:], bank(2 * j + h).rearrange("p (b s) -> p b s", b=4)) \
                        .then_inc(sem("m_xcp"), 1)
            dve.wait_ge(sem("m_xcp"), 4)
            dve.wait_ge(sem("m_pad"), 1)
            for j in range(2):
                acc = t[0][:, j, :].rearrange("p (b s) -> p b s", b=NB)
                for k in range(4):
                    src, tap = MB["xcp"][:, j, :, k:k + S], wcol("m_conv", 5 * j + k)
                    if k == 0:
                        dve.tensor_scalar(acc, src, tap, None, ALU.mult).then_inc(sem("m_conv"), 1)
                    else:
                        dve.wait_ge(sem("m_conv"), 4 * j + k)
                        dve.scalar_tensor_tensor(acc, src, tap, acc, ALU.mult, ALU.add).then_inc(sem("m_conv"), 1)
            dve.wait_ge(sem("m_xc"), 2)
            for j in range(2):
                for h in range(2):
                    dve.wait_ge(sem("m_dt"), 2 * j + h + 1)
                    dve.tensor_scalar(hcol(t[0], j, h), bank(2 + 2 * j + h), wcol("m_dtb", j), None, ALU.add) \
                        .then_inc(sem("m_dtb_added"), 1)
            step, s = sem("m_sp"), [0]

            def link(ins):
                s[0] += 1
                ins.then_inc(step, 1)
                dve.wait_ge(step, s[0])

            dve.wait_ge(sem("m_e"), 2)
            link(dve.tensor_scalar(t[2], t[1], 1.0, None, ALU.add))
            dve.wait_ge(sem("m_ln"), 1)
            link(dve.tensor_scalar(t[2], t[2], -1.0, None, ALU.add))
            link(dve.tensor_scalar(MB["u"], t[2], 0.0, None, ALU.is_equal))
            link(dve.tensor_tensor(t[2], t[2], MB["u"], ALU.add))
            link(dve.reciprocal(t[2], t[2]))
            link(dve.tensor_tensor(t[3], t[3], t[2], ALU.mult))
            link(dve.tensor_tensor(t[3], t[3], MB["u"], ALU.add))
            link(dve.tensor_tensor(t[3], t[3], t[1], ALU.mult))
            link(dve.scalar_tensor_tensor(t[3], t[0], 0.0, t[3], ALU.max, ALU.add))
            dve.tensor_scalar(MB["dtn"], t[3], -1.0, None, ALU.mult).then_inc(sem("m_dtn"), 1)
            dve.tensor_tensor(MB["u"], t[3], MB["xc"], ALU.mult).then_inc(sem("m_dtn"), 1)
            dve.wait_ge(sem("m_dtn"), 2)
            pair = lambda a: a.rearrange("p (a s) -> p a s", a=2)
            for n in range(NST):
                for j in range(2):
                    m = 2 * n + j
                    dve.wait_ge(sem("m_bc"), n + 1)
                    dve.tensor_tensor(pair(MB["dbx"][j]), pair(MB["u"][:, j, :]), PS[:, 4 * (n % 2):4 * (n % 2) + 2, 0:HALF], ALU.mult) \
                        .then_inc(sem("m_dbx"), 1)
                for j in range(2):
                    m = 2 * n + j
                    dve.wait_ge(sem("m_dbx"), 2 * n + j + 1)
                    dve.wait_ge(sem("m_cut"), m + 1)
                    dve.tensor_tensor_scan(MB["h"][j], MB["da"][j], MB["dbx"][j], 0.0, ALU.mult, ALU.add).then_inc(sem("m_scan"), 1)
                for j in range(2):
                    m = 2 * n + j
                    dve.wait_ge(sem("m_scan"), m + 1)
                    if m >= 2:
                        dve.wait_ge(sem("m_sum"), m - 1)
                    dve.tensor_tensor(pair(MB["hc"][j]), pair(MB["h"][j]), PS[:, 4 * (n % 2) + 2:4 * (n % 2) + 4, 0:HALF], ALU.mult) \
                        .then_inc(sem("m_hc"), 1)
            for j in range(2):
                dve.wait_ge(sem("m_sum"), 2 * NST - 1 + j)
                y = MB["y"][:, j, :]
                dve.scalar_tensor_tensor(y, MB["xc"][:, j, :], wcol("m_d", j), y, ALU.mult, ALU.add).then_inc(sem("m_skip"), 1)
                dve.wait_ge(sem("m_skip"), j + 1)
                dve.wait_ge(sem("m_z"), 4)
                dve.tensor_tensor(y, y, MB["z"][:, j, :], ALU.mult).then_inc(sem("m_gated"), 1)

            def rows2(h):
                dve.wait_ge(sem("m_o"), h + 1)
                dve.tensor_tensor(half(MB["xm"], h), bank(h), half(X, h), ALU.add).then_inc(sem("m_xm"), 1)
                dve.wait_ge(sem("m_xm"), h + 1)
                return dve.tensor_copy(half(R, h), half(MB["xm"], h))

            norm_dve(dve, C_M2, rows2, MB["n"], (wcol("m_ln2", 0), wcol("m_ln2", 1)))

            def rows3(h):
                dve.wait_ge(sem("m_o"), h + 3)
                dve.scalar_tensor_tensor(half(R, h), bank(4 + h), wcol("m_b2"), half(MB["xm"], h), ALU.add, ALU.add) \
                    .then_inc(sem("m_xm"), 1)
                dve.wait_ge(sem("m_xm"), h + 3)
                return dve.tensor_tensor(half(R, h), half(R, h), half(X, h), ALU.add)

            norm_dve(dve, C_M, rows3)

        OTHER_PE["m1"], OTHER_POOL["m1"], OTHER_ACT["m1"], OTHER_DVE["m1"] = m1_pe, m1_pool, m1_act, m1_dve

        def x1_buffers():
            lay = Layout()
            return dict(q=lay.take(T), y=lay.take(T), ctx=lay.take(CTX), k=lay.take(CTX), v=lay.take(NT, 128),
                        pt=lay.take(NT, S), ones=lay.take(128), rd=lay.take(S))

        XB = x1_buffers()
        LAST = KT_TILES[-1][1]

        def x1_sync(sp):
            x_ready(sp, C_M, 1)
            with sp.Fori(0, NB) as i:
                sp.wait_ge(*at("x1", "ctx_used", i + 1))
                sp.dma_start(XB["ctx"], ctx_in[:, bass.ds(i * CTX, CTX)]).then_inc(of("x1", "ctx"), 16)

        def x1_pe(pe):
            loaded(pe, "x1_wq")
            for h in range(2):
                x_ready(pe, C_M, h)
                pe.matmul(bank(h), w("x1_wq"), half(X, h), start=True, stop=True).then_inc(of("x1", "q"), 1)
            pe.sem_inc(of("x1", "ctx_used"), 1)
            pe.wait_ge(*at("x1", "qf", 2))
            with pe.Fori(0, NB) as i:
                pe.wait_ge(*at("x1", "ctx", i * 16 + 16))
                pe.wait_ge(*at("x1", "exp", i * 4 + 1))
                for c0, n in KEY_CHUNKS:
                    pe.matmul(PSF[:, c0:c0 + n], w("x1_wk"), XB["ctx"][:, c0:c0 + n], start=True, stop=True) \
                        .then_inc(of("x1", "k"), 1)
                for t, (t0, n) in enumerate(KT_TILES):
                    mm = pe.matmul(PS[0:n, 3 + t // 4, (t % 4) * 128:(t % 4) * 128 + 128], XB["ctx"][:, t0:t0 + n],
                                   w("x1_wv"), start=True, stop=True)
                    if t % 4 == 3:
                        mm.then_inc(of("x1", "v"), 1)
                pe.wait_ge(*at("x1", "v", i * 3 + 3))
                pe.sem_inc(of("x1", "ctx_used"), 1)
                pe.wait_ge(*at("x1", "kf", i * 3 + 3))
                for t, (t0, n) in enumerate(KT_TILES):
                    mm = pe.matmul(PS[0:n, t // 4, (t % 4) * S:(t % 4 + 1) * S], XB["k"][:, t0:t0 + n],
                                   XB["q"][:, bass.ds(i * S, S)], start=True, stop=True)
                    if t % 4 == 3:
                        mm.then_inc(of("x1", "scores"), 1)
                pe.wait_ge(*at("x1", "vp", i * 4 + 4))
                pe.wait_ge(*at("x1", "exp", i * 4 + 5))
                pe.wait_ge(*at("x1", "o", i + 1))
                for t, (t0, n) in enumerate(KT_TILES):
                    pe.matmul(PS[:, 6, 0:S], XB["v"][0:n, t, :], XB["pt"][0:n, t, :], start=(t == 0), stop=(t == NT - 1))
                for t, (t0, n) in enumerate(KT_TILES):
                    mm = pe.matmul(PS[:, 7, 0:S], XB["ones"][0:n, :], XB["pt"][0:n, t, :], start=(t == 0), stop=(t == NT - 1))
                mm.then_inc(of("x1", "pv"), 1)
            norm_pe(pe, C_X1)

        def x1_act(act):
            for h in range(2):
                act.wait_ge(*at("x1", "q", h + 1))
                act.activation(half(XB["q"], h), bank(h), ACT.Copy).then_inc(of("x1", "qf"), 1)
            act.sem_inc(of("x1", "exp"), 1)
            with act.Fori(0, NB) as i:
                for j, (c0, n) in enumerate(KEY_CHUNKS):
                    act.wait_ge(*at("x1", "k", i * 3 + (j + 1)))
                    act.activation(XB["k"][:, c0:c0 + n], PSF[:, c0:c0 + n], ACT.Copy).then_inc(of("x1", "kf"), 1)
                for j in range(3):
                    act.wait_ge(*at("x1", "scores", i * 3 + (j + 1)))
                    for t, m, rows in ((4 * j, 4, 128),) if j < 2 else ((8, 3, 128), (11, 1, LAST)):
                        act.activation(XB["pt"][0:rows, t:t + m, :].rearrange("p t s -> p (t s)"),
                                       PS[0:rows, j, (t % 4) * S:(t % 4 + m) * S], ACT.Exp, scale=D ** -0.5) \
                            .then_inc(of("x1", "exp"), 1)
            norm_act(act, C_X1)

        def x1_dve(dve):
            x_ready(dve, C_M, 1)
            dve.memset(XB["ones"], 1.0).then_inc(of("x1", "vzero"), 1)
            dve.wait_ge(*at("x1", "vzero", 1))
            dve.sem_inc(of("x1", "o"), 1)
            with dve.Fori(0, NB) as i:
                for j in range(3):
                    dve.wait_ge(*at("x1", "v", i * 3 + (j + 1)))
                    for t, m, rows in ((4 * j, 4, 128),) if j < 2 else ((8, 3, 128), (11, 1, LAST)):
                        dve.tensor_copy(XB["v"][0:rows, t:t + m, :].rearrange("p t d -> p (t d)"),
                                        PS[0:rows, 3 + j, (t % 4) * 128:(t % 4 + m) * 128]).then_inc(of("x1", "vp"), 1)
                dve.wait_ge(*at("x1", "pv", i + 1))
                dve.reciprocal(XB["rd"], PS[:, 7, 0:S]).then_inc(of("x1", "rd"), 1)
                dve.wait_ge(*at("x1", "rd", i + 1))
                dve.tensor_tensor(XB["y"][:, bass.ds(i * S, S)], PS[:, 6, 0:S], XB["rd"], ALU.mult).then_inc(of("x1", "o"), 1)
            residual(dve, C_X1, lambda h: dve.wait_ge(*at("x1", "o", 1 + NB)), lambda h: half(XB["y"], h))

        OTHER_SYNC["x1"], OTHER_PE["x1"], OTHER_ACT["x1"], OTHER_DVE["x1"] = x1_sync, x1_pe, x1_act, x1_dve

        def f1_buffers():
            lay = Layout()
            return dict(xp=lay.take(NB, S), om=lay.take(2), t=[lay.take(T) for _ in range(2)], x=[lay.take(T) for _ in range(2)],
                        r=lay.take(T), k=lay.take(T))

        FB = f1_buffers()

        def f1_pe(pe):
            loaded(pe, "f1_wr")
            for n, name in enumerate(("f1_wr", "f1_wk")):
                pe.wait_ge(*at("f1", "x", n + 1))
                for h in range(2):
                    pe.matmul(bank(2 * n + h), w(name), half(FB["x"][n], h), start=True, stop=True).then_inc(of("f1", "h"), 1)
            for h in range(2):
                pe.wait_ge(*at("f1", "act", h + 1))
                pe.matmul(bank(4 + h), w("f1_wv"), half(FB["k"], h), start=True, stop=True).then_inc(of("f1", "y"), 1)
            norm_pe(pe, C_F1)

        def f1_act(act):
            for h in range(2):
                act.wait_ge(*at("f1", "h", h + 1))
                act.activation(half(FB["r"], h), bank(h), ACT.Sigmoid).then_inc(of("f1", "sig"), 1)
            for h in range(2):
                act.wait_ge(*at("f1", "h", h + 3))
                act.activation(half(FB["k"], h), bank(2 + h), ACT.Relu).then_inc(of("f1", "relu"), 1)
            norm_act(act, C_F1)

        def f1_dve(dve):
            loaded(dve, "f1_wr")
            for h in range(2):
                x_ready(dve, C_X1, h)
            xs = X[:, :].rearrange("p (b s) -> p b s", b=NB)
            dve.memset(FB["xp"][:, :, 0:1], 0.0).then_inc(of("f1", "each"), 1)
            dve.tensor_copy(FB["xp"][:, :, 1:S], xs[:, :, 0:S - 1]).then_inc(of("f1", "each"), 1)
            dve.tensor_scalar(FB["om"], w("f1_mu"), -1.0, 1.0, ALU.mult, ALU.add).then_inc(of("f1", "each"), 1)
            dve.wait_ge(*at("f1", "each", 3))
            flat = FB["xp"].rearrange("p b s -> p (b s)")
            for n in range(2):
                dve.tensor_scalar(FB["t"][n], flat, FB["om"][:, n:n + 1], None, ALU.mult).then_inc(of("f1", "each"), 1)
            for n in range(2):
                dve.wait_ge(*at("f1", "each", 4 + n))
                dve.scalar_tensor_tensor(FB["x"][n], X[:, :], wcol("f1_mu", n), FB["t"][n], ALU.mult, ALU.add).then_inc(of("f1", "x"), 1)
            for h in range(2):
                dve.wait_ge(*at("f1", "relu", h + 1))
                dve.tensor_tensor(half(FB["k"], h), half(FB["k"], h), half(FB["k"], h), ALU.mult).then_inc(of("f1", "act"), 1)

            def rows(h):
                dve.wait_ge(*at("f1", "y", h + 1))
                dve.wait_ge(*at("f1", "sig", h + 1))
                dve.tensor_tensor(half(R, h), half(FB["r"], h), bank(4 + h), ALU.mult).then_inc(of("f1", "rv"), 1)
                dve.wait_ge(*at("f1", "rv", h + 1))
                return dve.tensor_tensor(half(R, h), half(R, h), half(X, h), ALU.add)

            norm_dve(dve, C_F1, rows)

        OTHER_PE["f1"], OTHER_ACT["f1"], OTHER_DVE["f1"] = f1_pe, f1_act, f1_dve

        READY_STAGES = 2 * STAGES - 2 * NB

        PREPARED = room - (READY_STAGES * 1024 + 1024 + 512 + 4 * 512)

        def f2_buffers():
            lay = Layout(PREPARED)
            made = dict(stage=lay.take(READY_STAGES * 1024), up=lay.take(2, 512), down=lay.take(512),
                        t=[lay.take(512) for _ in range(4)])
            low = Layout()
            return dict(made, h=low.take(4, T), wd=low.take(512), b=low.take(5))

        UB = f2_buffers()

        def f1_sync(sp):
            x_ready(sp, C_M, 1)
            for n in range(READY_STAGES):
                sp.dma_start(UB["stage"][:, n * 1024:(n + 1) * 1024], stages_in[n:n + 1, :].partition_broadcast(128)) \
                    .then_inc(of("f2", f"stage{n}"), 16)

        def stage_sync(sp, i):
            for k in range(READY_STAGES):
                sp.wait_ge(*at("f2", "made", i * (6 * READY_STAGES) + 6 * (k + 1)))
                sp.dma_start(UB["stage"][:, k * 1024:(k + 1) * 1024],
                             stages_in[bass.ds(i * READY_STAGES + (READY_STAGES + k), 1), :].partition_broadcast(128)) \
                    .then_inc(of("f2", f"stage{k}"), 16)

        def x2_pool(pool):
            loaded(pool, "f2_we")
            made = of("f2", "made")
            n = 0
            for layer in ("up", "down"):
                R2 = 2 if layer == "up" else 1
                for k in range(STAGES):
                    span = 2 ** (k if layer == "up" else STAGES - 1 - k)
                    nb = 512 // (2 * span)
                    pool.wait_ge(*at("f2", f"stage{n % READY_STAGES}", 16 * (n // READY_STAGES + 1)))
                    if layer == "up" and k == 0:
                        src = [W[:, AT[p][0]:AT[p][0] + 512] for p in ("f2_we", "f2_be")]
                    elif k == 0:
                        src = [w("f2_wc")]
                    else:
                        src = [UB["up"][:, r, :] for r in range(2)] if layer == "up" else [UB["down"]]
                    dst = [UB["up"][:, r, :] for r in range(2)] if layer == "up" else [UB["down"]]
                    slot = n % READY_STAGES
                    ws = UB["stage"][:, slot * 1024:(slot + 1) * 1024].rearrange("p (b s i j) -> p b s i j", s=span, i=2, j=2)
                    for r in range(R2):
                        two = src[r].rearrange("p (b c s) -> p b c s", c=2, s=span)
                        for o in range(2):
                            for j in range(2):
                                t = UB["t"][2 * o + j][:, r * 256:(r + 1) * 256].rearrange("p (b s) -> p b s", s=span)
                                wij = ws[:, :, :, o, j] if layer == "up" else ws[:, :, :, j, o]
                                ins = pool.tensor_tensor(t, two[:, :, j, :], wij, ALU.mult)
                    ins.then_inc(made, 4)
                    pool.wait_ge(*at("f2", "made", 6 * n + 4))
                    for o in range(2):
                        for r in range(R2):
                            two = dst[r].rearrange("p (b c s) -> p b c s", c=2, s=span)
                            a, b = [UB["t"][2 * o + j][:, r * 256:(r + 1) * 256].rearrange("p (b s) -> p b s", s=span) for j in range(2)]
                            ins = pool.tensor_tensor(two[:, :, o, :], a, b, ALU.add)
                    ins.then_inc(made, 2)
                    pool.wait_ge(*at("f2", "made", 6 * n + 6))
                    n += 1


        KEYS = CTX + S
        QC = KEYS // 4
        X2T = [(t * 128, min(128, KEYS - t * 128)) for t in range(-(-KEYS // 128))]
        NX = len(X2T)
        PAIRS = H // 2
        GROUPS = [range(4 * g, min(4 * g + 4, NX)) for g in range(4)]

        def x2_buffers():
            lay = Layout()
            return dict(
                xn=lay.take(KEYS), sq=lay.take(KEYS), sd=lay.take(KEYS), mask=lay.take(CTX // 4 + 1),
                mrow=lay.take_bf16(KEYS), ones=lay.take_bf16(S), y=lay.take(T),
                k=[lay.take(KEYS) for _ in range(2)], v=[lay.take(NX, 128) for _ in range(2)],
                p=[lay.take(KEYS) for _ in range(2)], pt=[lay.take(NX, S) for _ in range(2)],
                qn=lay.take(PAIRS, S), qbd=lay.take(PAIRS, 2, S), o=lay.take(PAIRS, S),
                nm=lay.take(H), den=lay.take(H), rd=lay.take(H), rdt=lay.take(S), end=lay.at)

        B2 = x2_buffers()
        assert B2["end"] <= PREPARED, (B2["end"], PREPARED)
        quarter = lambda a, c: a[:, c * QC:(c + 1) * QC]

        def x2_sync(sp):
            x_ready(sp, C_A2, 1)
            with sp.Fori(0, NB) as i:
                sp.wait_ge(*at("x2", "ctx_used", i + 1))
                sp.dma_start(B2["xn"][:, 0:CTX], ctx_in[:, bass.ds(i * CTX, CTX)]).then_inc(of("x2", "ctx"), 16)
                sp.dma_start(B2["mask"].bitcast(U8)[0:1, 0:CTX], mask2_in[bass.ds(i, 1), :]).then_inc(of("x2", "mask"), 16)
                stage_sync(sp, i)

        def x2_pe(pe):
            loaded(pe, "x2_wq")
            x_ready(pe, C_A2, 1)
            pe.sem_inc(of("x2", "ctx_used"), 1)
            pe.sem_inc(of("x2", "scores"), 1)
            pe.sem_inc(of("x2", "pv"), 2)
            pe.wait_ge(*at("x2", "vzero", 4))
            with pe.Fori(0, NB) as i:
                def keys(p, c):
                    if c:
                        pe.wait_ge(*at("x2", "kf", i * 64 + (8 * p + 2 * c)))
                    elif p:
                        pe.wait_ge(*at("x2", "vp", i * 32 + 4 * p))
                    pe.matmul(PS[:, 6, 0:QC], w("x2_wk")[:, 128 * p:128 * p + 128], quarter(B2["xn"], c), start=True, stop=True) \
                        .then_inc(of("x2", "k"), 1)

                def norms(p, c):
                    pe.wait_ge(*at("x2", "kf", i * 64 + (8 * p + 8)))
                    if c:
                        pe.wait_ge(sem("x2_ssf"), i * 32 + (4 * p + c))
                    pe.matmul(PS[:, 6, 0:QC], w("blockdiag"), quarter(B2["sq"], c), start=True, stop=True).then_inc(sem("x2_ss"), 1)

                def values(p, g):
                    if g:
                        pe.wait_ge(*at("x2", "vp", i * 32 + (4 * p + g)))
                    else:
                        pe.wait_ge(sem("x2_ssf"), i * 32 + (4 * p + 4))
                    for t in GROUPS[g]:
                        t0, n = X2T[t]
                        mm = pe.matmul(PS[0:n, 6, (t % 4) * 128:(t % 4) * 128 + 128], B2["xn"][:, t0:t0 + n],
                                       w("x2_wv")[:, 128 * p:128 * p + 128], start=True, stop=True)
                    mm.then_inc(of("x2", "v"), 1)
                    if p == PAIRS - 1 and g == 3:
                        pe.wait_ge(*at("x2", "v", i * 32 + 32))
                        pe.sem_inc(of("x2", "ctx_used"), 1)

                def scores(h):
                    p, e = divmod(h, 2)
                    pe.wait_ge(*at("x2", "exp", i * H + (h + 1)))
                    pe.wait_ge(sem("x2_kn"), i * PAIRS + (p + 1))
                    for c in range(4):
                        pe.matmul(PS[0:S, c, 0:QC], B2["qbd"][:, p, e, :], quarter(B2["k"][p % 2], c), start=True, stop=False)
                        mm = pe.matmul(PS[0:S, c, 0:QC], B2["ones"][0:1, :], B2["mrow"][0:1, c * QC:(c + 1) * QC],
                                       start=False, stop=True)
                    mm.then_inc(of("x2", "scores"), 1)

                def turn(h, g):
                    done, n = "pt_dve" if g % 2 == 0 else "pt_act", 2 * h + g // 2
                    if g == 0:
                        pe.wait_ge(*at("x2", "exp", i * H + (h + 2)))
                    if n:
                        pe.wait_ge(*at("x2", done, i * (2 * H) + n))
                    for t in GROUPS[g]:
                        t0, n = X2T[t]
                        mm = pe.transpose(PS[0:n, 4 + g % 2, (t % 4) * S:(t % 4 + 1) * S], B2["p"][h % 2][0:S, t0:t0 + n],
                                          ident[0:S, 0:S])
                    mm.then_inc(of("x2", "t"), 1)

                def product(h, g):
                    p, e = divmod(h, 2)
                    if g == 0:
                        pe.wait_ge(*at("x2", "pt_dve", i * (2 * H) + (2 * h + 2)))
                        pe.wait_ge(*at("x2", "pt_act", i * (2 * H) + (2 * h + 2)))
                        pe.wait_ge(*at("x2", "vp", i * 32 + (4 * p + 4)))
                        if h == 0 or h == 8:
                            pe.wait_ge(*at("x2", "o", i * 2 + (h // 8 + 1)))
                    for t in GROUPS[g]:
                        n = X2T[t][1]
                        mm = pe.matmul(PS[64 * e:64 * e + 64, 7, (p % 4) * S:(p % 4 + 1) * S],
                                       B2["v"][p % 2][0:n, t, 64 * e:64 * e + 64], B2["pt"][h % 2][0:n, t, :],
                                       start=(t == 0), stop=(t == NX - 1))
                    if g == 3:
                        mm.then_inc(of("x2", "pv"), 1)

                pe.wait_ge(*at("x2", "ctx", i * 16 + 16))
                pe.wait_ge(sem("x2_lat"), i + 1)
                pe.wait_ge(*at("x2", "exp", i * H + 1))
                for c in range(4):
                    pe.matmul(PS[:, c, 0:QC], mean_w[:, :], quarter(B2["xn"], c), start=True, stop=True).then_inc(sem("x2_mean"), 1)
                for c in range(4):
                    pe.wait_ge(sem("x2_sq"), i * 4 + (c + 1))
                    pe.matmul(PS[:, c, 0:QC], mean_w[:, :], quarter(B2["sq"], c), start=True, stop=True).then_inc(sem("x2_var"), 1)
                pe.wait_ge(sem("x2_xn"), i * 4 + 4)
                for p in range(PAIRS):
                    mm = pe.matmul(PS[:, p // 4, (p % 4) * S:(p % 4 + 1) * S], w("x2_wq")[:, 128 * p:128 * p + 128],
                                   B2["xn"][:, CTX:KEYS], start=True, stop=True)
                mm.then_inc(of("x2", "q"), 1)
                pe.wait_ge(sem("x2_qsq"), i + 1)
                for a in range(2):
                    mm = pe.matmul(PS[:, 2 + a, 0:4 * S], w("blockdiag"), B2["sq"][:, a * 4 * S:(a + 1) * 4 * S], start=True, stop=True)
                mm.then_inc(sem("x2_qss"), 1)
                pe.wait_ge(*at("x2", "op0", i * 2 + 2))
                for c in range(4):
                    keys(0, c)
                for c in range(4):
                    norms(0, c)
                for g in range(4):
                    values(0, g)
                scores(0)
                for h in range(H):
                    p, nxt = h // 2, h // 2 + 1
                    more = nxt < PAIRS
                    if h % 2 == 0:
                        scores(h + 1)
                        for g in range(4):
                            if more:
                                keys(nxt, g)
                            turn(h, g)
                        for g in range(4):
                            if more:
                                norms(nxt, g)
                            product(h, g)
                    else:
                        for g in range(4):
                            if more:
                                values(nxt, g)
                            turn(h, g)
                        if h < H - 1:
                            scores(h + 1)
                        for g in range(4):
                            product(h, g)
                pe.wait_ge(*at("x2", "rd", i + 1))
                pe.transpose(PS[0:H, 6, 0:S], B2["rd"][0:S], ident[0:S, 0:S]).then_inc(of("x2", "rdt"), 1)
                pe.wait_ge(*at("x2", "rdtf", i + 1))
                sel = w("sel64", H).rearrange("p (g m) -> p g m", g=PAIRS)
                for p in range(PAIRS):
                    mm = pe.matmul(PS[:, p // 4, (p % 4) * S:(p % 4 + 1) * S], sel[:, p, :], B2["rdt"][0:H, :], start=True, stop=True)
                mm.then_inc(of("x2", "bc"), 1)
                pe.wait_ge(*at("x2", "normed", i + 1))
                for p in range(PAIRS):
                    mm = pe.matmul(PS[:, 2, 0:S], w("x2_wo")[:, 128 * p:128 * p + 128], B2["o"][:, p, :],
                                   start=(p == 0), stop=(p == PAIRS - 1))
                mm.then_inc(of("x2", "y"), 1)
                pe.wait_ge(sem("x2_yf"), i + 1)
            norm_pe(pe, C_X2)

        def x2_act(act):
            x_ready(act, C_A2, 1)
            act.sem_inc(of("x2", "exp"), 1)
            with act.Fori(0, NB) as i:
                def rsqrt(buf, before, after, k):
                    act.activation(buf, buf, ACT.Ln).then_inc(before, 1)
                    act.wait_ge(before, k)
                    act.activation(buf, buf, ACT.Exp, scale=-0.5).then_inc(after, 1)

                def keys(p, c):
                    act.wait_ge(*at("x2", "k", i * 32 + (4 * p + c + 1)))
                    act.activation(quarter(B2["k"][p % 2], c), PS[:, 6, 0:QC], ACT.Copy).then_inc(of("x2", "kf"), 1)
                    act.activation(quarter(B2["sq"], c), PS[:, 6, 0:QC], ACT.Square).then_inc(of("x2", "kf"), 1)

                def norms(p):
                    act.wait_ge(sem("x2_ssf"), i * 32 + (4 * p + 4))
                    rsqrt(B2["sd"], sem("x2_kln"), sem("x2_krs"), i * PAIRS + (p + 1))

                def probs(h):
                    act.wait_ge(*at("x2", "nm", i * H + (h + 1)))
                    act.activation(B2["p"][h % 2][0:S].rearrange("p (a b) -> p a b", a=4), PS[0:S, 0:4, 0:QC], ACT.Exp,
                                   bias=B2["nm"][0:S, h:h + 1], accum_out=B2["den"][0:S, h:h + 1]).then_inc(of("x2", "exp"), 1)

                def turned(h, g):
                    act.wait_ge(*at("x2", "t", i * (4 * H) + (4 * h + g + 1)))
                    if g == 1:
                        act.wait_ge(*at("x2", "pv", i * H + (h + 1)))
                        act.activation(B2["pt"][h % 2][:, 4:8, :].rearrange("p t s -> p (t s)"), PS[:, 5, 0:4 * S], ACT.Copy) \
                            .then_inc(of("x2", "pt_act"), 1)
                    else:
                        n = X2T[-1][1]
                        act.activation(B2["pt"][h % 2][0:n, 12, :], PS[0:n, 5, 0:S], ACT.Copy).then_inc(of("x2", "pt_act"), 1)

                for c in range(4):
                    act.wait_ge(sem("x2_cen"), i * 4 + (c + 1))
                    act.activation(quarter(B2["sq"], c), quarter(B2["xn"], c), ACT.Square).then_inc(sem("x2_sq"), 1)
                act.wait_ge(sem("x2_var"), i * 4 + 4)
                act.activation(B2["sq"].rearrange("p (a b) -> p a b", a=4), PS[:, 0:4, 0:QC], ACT.Ln, bias=epsc[:, :]) \
                    .then_inc(sem("x2_ln"), 1)
                act.wait_ge(sem("x2_ln"), i + 1)
                act.activation(B2["sq"], B2["sq"], ACT.Exp, scale=-0.5).then_inc(sem("x2_rs"), 1)
                act.wait_ge(*at("x2", "q", i + 1))
                act.wait_ge(sem("x2_xn"), i * 4 + 4)
                act.activation(B2["sq"][:, 0:T].rearrange("p (a b) -> p a b", a=2), PS[:, 0:2, 0:4 * S], ACT.Square) \
                    .then_inc(sem("x2_qsq"), 1)
                act.wait_ge(sem("x2_qcl"), i + 1)
                rsqrt(B2["sd"][:, 0:T], sem("x2_qln"), sem("x2_qrs"), i + 1)
                for c in range(4):
                    keys(0, c)
                norms(0)
                probs(0)
                for h in range(H):
                    nxt = h // 2 + 1
                    if h % 2 == 0:
                        more = nxt < PAIRS
                        if more:
                            keys(nxt, 0)
                        probs(h + 1)
                        if more:
                            keys(nxt, 1)
                        turned(h, 1)
                        if more:
                            keys(nxt, 2)
                            keys(nxt, 3)
                        turned(h, 3)
                        if more:
                            norms(nxt)
                    else:
                        turned(h, 1)
                        turned(h, 3)
                        if h < H - 1:
                            probs(h + 1)
            norm_act(act, C_X2)

        def x2_dve(dve):
            loaded(dve, "x2_wq")
            x_ready(dve, C_A2, 1)
            dve.memset(B2["qbd"].rearrange("p a b s -> p (a b s)"), 0.0).then_inc(of("x2", "vzero"), 1)
            dve.memset(B2["ones"], 1.0).then_inc(of("x2", "vzero"), 1)
            dve.memset(B2["mrow"][0:1, CTX:KEYS], 0.0).then_inc(of("x2", "vzero"), 1)
            dve.memset(B2["rdt"][0:H], 0.0).then_inc(of("x2", "vzero"), 1)
            dve.wait_ge(*at("x2", "vzero", 4))
            dve.sem_inc(of("x2", "o"), 1)
            with dve.Fori(0, NB) as i:
                def norms(p, c):
                    dve.wait_ge(sem("x2_ss"), i * 32 + (4 * p + c + 1))
                    dve.tensor_scalar(quarter(B2["sd"], c), PS[:, 6, 0:QC], 1.0 / 64, 1e-16, ALU.mult, ALU.max) \
                        .then_inc(sem("x2_ssf"), 1)

                def normed(p):
                    dve.wait_ge(sem("x2_krs"), i * PAIRS + (p + 1))
                    k = B2["k"][p % 2]
                    dve.scalar_tensor_tensor(k, k, wcol("x2_g", 1), B2["sd"], ALU.mult, ALU.mult).then_inc(sem("x2_kn"), 1)

                def values(p, g):
                    dve.wait_ge(*at("x2", "v", i * 32 + (4 * p + g + 1)))
                    n = len(GROUPS[g])
                    rows = 128 if g < 3 else X2T[-1][1]
                    dve.tensor_copy(B2["v"][p % 2][0:rows, 4 * g:4 * g + n, :].rearrange("p t d -> p (t d)"), PS[0:rows, 6, 0:128 * n]) \
                        .then_inc(of("x2", "vp"), 1)

                def maximum(h):
                    dve.wait_ge(*at("x2", "scores", i * H + (h + 2)))
                    dve.tensor_reduce(B2["nm"][0:S, h:h + 1], PS[0:S, 0:4, 0:QC], mybir.AxisListType.XY, ALU.max, negate=True) \
                        .then_inc(of("x2", "nm"), 1)

                def turned(h, g):
                    dve.wait_ge(*at("x2", "t", i * (4 * H) + (4 * h + g + 1)))
                    if g == 0:
                        dve.wait_ge(*at("x2", "pv", i * H + (h + 1)))
                    dve.tensor_copy(B2["pt"][h % 2][:, 4 * g:4 * g + 4, :].rearrange("p t s -> p (t s)"), PS[:, 4, 0:4 * S]) \
                        .then_inc(of("x2", "pt_dve"), 1)

                dve.wait_ge(*at("x2", "mask", i * 16 + 16))
                dve.tensor_scalar(B2["mrow"][0:1, 0:CTX], B2["mask"].bitcast(U8)[0:1, 0:CTX], 0.0, -BIG, ALU.is_equal, ALU.mult) \
                    .then_inc(of("x2", "mrow"), 1)
                dve.tensor_copy(B2["xn"][:, CTX:KEYS], X[:, bass.ds(i * S, S)]).then_inc(sem("x2_lat"), 1)
                for c in range(4):
                    dve.wait_ge(sem("x2_mean"), i * 4 + (c + 1))
                    dve.tensor_tensor(quarter(B2["xn"], c), quarter(B2["xn"], c), PS[:, c, 0:QC], ALU.subtract) \
                        .then_inc(sem("x2_cen"), 1)
                dve.wait_ge(sem("x2_rs"), i + 1)
                parts = ((0, CTX, 0), (CTX, S, 2))
                for a, n, g in parts:
                    dve.scalar_tensor_tensor(B2["xn"][:, a:a + n], B2["xn"][:, a:a + n], wcol("x2_ln", g), B2["sq"][:, a:a + n],
                                             ALU.mult, ALU.mult).then_inc(sem("x2_xn"), 1)
                for j, (a, n, g) in enumerate(parts):
                    dve.wait_ge(sem("x2_xn"), i * 4 + (j + 1))
                    dve.tensor_scalar(B2["xn"][:, a:a + n], B2["xn"][:, a:a + n], wcol("x2_ln", g + 1), None, ALU.add) \
                        .then_inc(sem("x2_xn"), 1)
                dve.wait_ge(sem("x2_qss"), i + 1)
                dve.tensor_scalar(B2["sd"][:, 0:T].rearrange("p (a b) -> p a b", a=2), PS[:, 2:4, 0:4 * S], 1.0 / 64, 1e-16,
                                  ALU.mult, ALU.max).then_inc(sem("x2_qcl"), 1)
                dve.wait_ge(sem("x2_qrs"), i + 1)
                dve.scalar_tensor_tensor(B2["qn"].rearrange("p (a b) s -> p a (b s)", a=2), PS[:, 0:2, 0:4 * S], wcol("x2_g", 0),
                                         B2["sd"][:, 0:T].rearrange("p (a b) -> p a b", a=2), ALU.mult, ALU.mult).then_inc(sem("x2_qn"), 1)
                dve.wait_ge(sem("x2_qn"), i + 1)
                for e in range(2):
                    r = slice(64 * e, 64 * e + 64)
                    dve.tensor_scalar(B2["qbd"][r, :, e, :], B2["qn"][r], 64 ** -0.5, None, ALU.mult).then_inc(of("x2", "op0"), 1)
                for c in range(4):
                    norms(0, c)
                for g in range(4):
                    values(0, g)
                normed(0)
                maximum(0)
                for h in range(H):
                    nxt = h // 2 + 1
                    more = nxt < PAIRS
                    if h % 2 == 0:
                        maximum(h + 1)
                        turned(h, 0)
                        turned(h, 2)
                        if more:
                            for c in range(4):
                                norms(nxt, c)
                            normed(nxt)
                    else:
                        for g in range(4):
                            if more:
                                values(nxt, g)
                            if g % 2 == 0:
                                turned(h, g)
                        if h < H - 1:
                            maximum(h + 1)
                    if h % 8 == 7:
                        dve.wait_ge(*at("x2", "pv", i * H + (h + 3)))
                        a = 4 * (h // 8)
                        dve.tensor_copy(B2["o"][:, a:a + 4, :].rearrange("p a s -> p (a s)"), PS[:, 7, 0:4 * S]).then_inc(of("x2", "o"), 1)
                dve.wait_ge(*at("x2", "exp", i * H + (H + 1)))
                dve.reciprocal(B2["rd"][0:S], B2["den"][0:S]).then_inc(of("x2", "rd"), 1)
                dve.wait_ge(*at("x2", "rdt", i + 1))
                dve.tensor_copy(B2["rdt"][0:H], PS[0:H, 6, 0:S]).then_inc(of("x2", "rdtf"), 1)
                dve.wait_ge(*at("x2", "bc", i + 1))
                dve.wait_ge(*at("x2", "o", i * 2 + 3))
                o = B2["o"].rearrange("p (a b) s -> p a (b s)", a=2)
                dve.tensor_tensor(o, o, PS[:, 0:2, 0:4 * S], ALU.mult).then_inc(of("x2", "normed"), 1)
                dve.wait_ge(*at("x2", "y", i + 1))
                dve.tensor_copy(B2["y"][:, bass.ds(i * S, S)], PS[:, 2, 0:S]).then_inc(sem("x2_yf"), 1)
            residual(dve, C_X2, lambda h: dve.wait_ge(sem("x2_yf"), NB), lambda h: half(B2["y"], h), wcol("x2_b"))

        OTHER_SYNC["x2"], OTHER_PE["x2"], OTHER_ACT["x2"], OTHER_DVE["x2"] = x2_sync, x2_pe, x2_act, x2_dve
        def f2_pe(pe):
            L = "f2"
            pe.wait_ge(*at(L, "made", 12 * STAGES))
            for t in range(4):
                pe.transpose(PS[:, 0, 128 * t:128 * t + 128], UB["down"][:, 128 * t:128 * t + 128], ident)
            for t in range(4):
                mm = pe.matmul(PS[:, 1, t:t + 1], UB["up"][0:1, 1, 128 * t:128 * t + 128], mean_w[0:1, 0:1], start=True, stop=True)
            mm.then_inc(of(L, "gt"), 1)
            pe.wait_ge(*at(L, "gtc", 3))
            def second(h):
                for t in range(4):
                    pe.wait_ge(*at(L, "act", 4 * h + t + 1))
                    mm = pe.matmul(bank(4 + h), UB["wd"][:, 128 * t:128 * t + 128], UB["h"][:, t, h * HALF:(h + 1) * HALF],
                                   start=(t == 0), stop=(t == 3))
                mm.then_inc(of(L, "y"), 1)

            for h in range(2):
                x_ready(pe, C_X2, h)
                for t in range(4):
                    if h:
                        pe.wait_ge(*at(L, "act", t + 1))
                    pe.matmul(bank(t), UB["up"][:, 0, 128 * t:128 * t + 128], half(X, h), start=True, stop=True) \
                        .then_inc(of(L, "h"), 1)
            for h in range(2):
                second(h)
            norm_pe(pe, C_F2)

        def f2_act(act):
            L = "f2"
            act.wait_ge(*at(L, "gtc", 2))
            for h in range(2):
                for t in range(4):
                    act.wait_ge(*at(L, "h", 4 * h + t + 1))
                    act.activation(UB["h"][:, t, h * HALF:(h + 1) * HALF], bank(t), ACT.Gelu, bias=UB["b"][:, t:t + 1]) \
                        .then_inc(of(L, "act"), 1)
            norm_act(act, C_F2)

        def f2_dve(dve):
            L = "f2"
            dve.wait_ge(*at(L, "gt", 1))
            dve.scalar_tensor_tensor(UB["b"][:, 0:4], PS[:, 1, 0:4], 128.0, w("f2_ub"), ALU.mult, ALU.add).then_inc(of(L, "gtc"), 1)
            dve.tensor_tensor(UB["b"][:, 4:5], wcol("f2_b", 0), wcol("f2_b", 1), ALU.add).then_inc(of(L, "gtc"), 1)
            dve.tensor_copy(UB["wd"], PS[:, 0, :]).then_inc(of(L, "gtc"), 1)
            dve.wait_ge(*at(L, "gtc", 3))
            residual(dve, C_F2, lambda h: dve.wait_ge(*at(L, "y", h + 1)), lambda h: bank(4 + h), UB["b"][:, 4:5])

        OTHER_SYNC["f1"], OTHER_POOL["x2"] = f1_sync, x2_pool
        OTHER_PE["f2"], OTHER_ACT["f2"], OTHER_DVE["f2"] = f2_pe, f2_act, f2_dve

        LAYERS = [
            ("a0", C_A0), ("x0", C_X0), ("f0", C_F0), ("m1", C_M), ("x1", C_X1), ("f1", C_F1),
            ("a2", C_A2), ("x2", C_X2), ("f2", C_F2), ("a3", C_A3), ("x3", C_X3), ("f3", C_F3)]
        SELF = {"a0": "window", "a2": "rope", "a3": "top"}
        block = scope.enter_context(nc.Block())

        @block.sync
        def _(sp):
            for n, first in enumerate(LOADS):
                a = AT[first][0]
                b = AT[LOADS[n + 1]][0] if n + 1 < len(LOADS) else PACKED
                if n == 0:
                    sp.dma_start(X[:, :], x_in).then_inc(sem("x_loaded"), 16)
                sp.dma_start(W[:, a:b], packed_in[:, a:b]).then_inc(sem(f"w_loaded{n}"), 16)
            for L, c in LAYERS:
                if L in ("x0", "x3"):
                    cross_sync(sp, L, c - 1, L == "x0")
                elif L in ("f0", "f3"):
                    moe_sync(sp, L, c - 1)
                elif L in OTHER_SYNC:
                    OTHER_SYNC[L](sp)
            x_ready(sp, LAYERS[-1][1], 1)
            sp.dma_start(out, X[:, :]).then_inc(sem("stored"), 16)
            sp.wait_ge(sem("stored"), 16)

        @block.gpsimd
        def _(pool):
            pool.memset(mean_w[:, :], 1.0 / D).then_inc(sem("consts"), 1)
            pool.memset(epsc[:, :], LN_EPS).then_inc(sem("consts"), 1)
            for L, c in LAYERS:
                if L in SELF:
                    self_pool(pool, SELF[L], c - 1)
                elif L in ("x0", "x3"):
                    cross_pool(pool, L, c - 1, L == "x0")
                elif L in ("f0", "f3"):
                    moe_pool(pool, L, c - 1)
                elif L in OTHER_POOL:
                    OTHER_POOL[L](pool)

        @block.scalar
        def _(act):
            act.wait_ge(sem("consts"), 2)
            for L, c in LAYERS:
                if L in SELF:
                    loaded(act, f"{L}_wq")
                    self_act(act, SELF[L], c - 1)
                elif L in ("x0", "x3"):
                    cross_act(act, L, c - 1, L == "x0")
                elif L in ("f0", "f3"):
                    moe_act(act, L, c - 1)
                else:
                    OTHER_ACT[L](act)

        @block.vector
        def _(dve):
            for L, c in LAYERS:
                if L in SELF:
                    x_ready(dve, c - 1, 1)
                    self_dve(dve, SELF[L], c - 1)
                elif L in ("x0", "x3"):
                    cross_dve(dve, L, c - 1, L == "x0")
                elif L in ("f0", "f3"):
                    moe_dve(dve, L, c - 1)
                else:
                    OTHER_DVE[L](dve)

        @block.tensor
        def _(pe):
            for L, c in LAYERS:
                if L in SELF:
                    self_pe(pe, SELF[L], c - 1)
                elif L in ("x0", "x3"):
                    cross_pe(pe, L, c - 1, L == "x0")
                elif L in ("f0", "f3"):
                    moe_pe(pe, L, c - 1)
                else:
                    OTHER_PE[L](pe)


def constants():
    c = {"ident": np.eye(128), "headmask": np.zeros((128, H)), "selx": np.zeros((128, 128)),
         "parity": np.zeros((128, 2)),
         "window": np.zeros((S, S)), "blockdiag": np.zeros((128, 128)), "sel64": np.zeros((H, 8, 128)),
         "maskab": np.zeros((128, 2)), "m_sel": np.zeros((40, 16, 2, 128))}
    for p in range(128):
        c["headmask"][p, p // DH] = 1
        c["sel64"][:, :, p] = (np.arange(H)[:, None] == 2 * np.arange(8)[None, :] + p // 64)
        c["selx"][p // SLOT * SLOT + DH, p] = 1
        c["parity"][p, p // DH % 2] = 1
    c["blockdiag"][0:64, 0:64] = 1
    c["blockdiag"][64:, 64:] = 1
    i, j = np.arange(S)[:, None], np.arange(S)[None, :]
    c["window"][...] = np.where((abs(i - j) <= 32) | (i == 0) | (j == 0), 0.0, -BIG)
    c["maskab"][0:2, 0] = [-9984, -16]
    for n in range(16):
        c["m_sel"][8 + n, n, 0] = 1
        c["m_sel"][24 + n, n, 1] = 1
    inv = np.float32(1.0) / np.float32(10000.0) ** (np.arange(0, DH, 2, dtype=np.float32) / np.float32(DH))
    ang = np.outer(np.arange(S, dtype=np.float32), inv.astype(np.float32)).astype(np.float32)
    cos, sin = np.cos(ang).T, np.sin(ang).T
    rows = np.arange(128) % DH // 2
    sign = np.where(np.arange(128) % 2 == 0, -1.0, 1.0)[:, None]
    c["cosq"], c["sinq"] = cos[rows] * DH ** -0.5, sin[rows] * sign * DH ** -0.5
    c["cosk"], c["sink"] = cos[rows], sin[rows] * sign
    return c


def slotted(wo):
    a = np.zeros((4, SLOT, 4, wo.shape[1]), wo.dtype)
    a[:, 0:DH] = wo.reshape(4, 4, DH, -1).transpose(1, 2, 0, 3)
    return a.reshape(128, -1)


def packed(v):
    swap = np.arange(128) ^ 1
    col = lambda *a: np.stack(a, 1)
    tiles = lambda a: a.reshape(-1, 128, a.shape[1]).transpose(1, 0, 2).reshape(128, -1)
    row = lambda a: np.broadcast_to(a, (128, a.shape[0]))
    c = constants()
    for L, N in (("a0", "L0_attn_"), ("x0", "L0_xattn_"), ("a3", "L3_attn_")):
        c.update({f"{L}_wq": v[N + "Wq"], f"{L}_wk": v[N + "Wk"], f"{L}_wv": v[N + "Wv"], f"{L}_wo": slotted(v[N + "Wo"]),
                  f"{L}_bv": row(v[N + "bv"]), f"{L}_b": col(v[N + "bq"], v[N + "bk"], v[N + "bo"])})
    c.update({"f0_wg": v["L0_ffn_wg"], "f0_b2": v["L0_ffn_b2"]})
    M = "L1_attn_"
    dtw = np.zeros((40, 256), np.float32)
    dtw[0:8] = v[M + "dt_proj_w"].T
    conv = np.concatenate([v[M + "conv_w"], v[M + "conv_b"][:, None]], 1)
    c.update({"m_ln1": col(v[M + "ln1_w"], v[M + "ln1_b"]), "m_ln2": col(v[M + "ln2_w"], v[M + "ln2_b"]),
              "m_in": v[M + "in_proj_w"].T, "m_conv": tiles(conv), "m_xp": tiles(v[M + "x_proj_w"].T), "m_dtw": dtw,
              "m_dtb": v[M + "dt_proj_b"].reshape(2, 128).T, "m_alog": tiles(v[M + "A_log"]),
              "m_d": v[M + "D"].reshape(2, 128).T, "m_out": tiles(v[M + "out_proj_w"].T), "m_w1": v[M + "ffn_w1"].T,
              "m_b1": v[M + "ffn_b1"].reshape(2, 128).T, "m_w2": tiles(v[M + "ffn_w2"].T), "m_b2": v[M + "ffn_b2"][:, None]})
    c.update({"x1_wq": v["L1_xattn_wq"].T, "x1_wk": v["L1_xattn_wk"].T, "x1_wv": v["L1_xattn_wv"].T,
              "f1_wr": v["L1_ffn_W_r"].T, "f1_wk": v["L1_ffn_W_k"].T, "f1_wv": v["L1_ffn_W_v"].T,
              "f1_mu": col(v["L1_ffn_mu_r"], v["L1_ffn_mu_k"])})
    N = "L2_attn_"
    c.update({"a2_wq": v[N + "wq"].T, "a2_wk": v[N + "wk"].T, "a2_wqs": v[N + "wq"].T[:, swap],
              "a2_wks": v[N + "wk"].T[:, swap], "a2_wv": v[N + "wv"].T, "a2_wo": slotted(v[N + "wo"].T)})
    N = "L2_xattn_"
    twice = lambda a: np.concatenate([a, a])
    c.update({"x2_ln": col(v[N + "ln_x_g"], v[N + "ln_x_b"], v[N + "ln_l_g"], v[N + "ln_l_b"]),
              "x2_g": col(twice(v[N + "qn_g"]), twice(v[N + "kn_g"])), "x2_wq": v[N + "Wq"],
              "x2_wk": v[N + "Wkv"][:, 0:1024], "x2_wv": v[N + "Wkv"][:, 1024:], "x2_wo": tiles(v[N + "Wout"]),
              "x2_b": v[N + "bout"][:, None]})
    N = "L2_ffn_"
    c.update({"f2_we": v[N + "W_exp"], "f2_wc": v[N + "W_con"].T, "f2_be": row(v[N + "b_exp"]),
              "f2_ub": v[N + "up_bias"].reshape(4, 128).T, "f2_b": col(v[N + "b_con"], v[N + "down_bias"])})
    N = "L3_xattn_"
    c.update({"x3_wq": v[N + "Wq"], "x3_wk": v[N + "Wk"], "x3_wv": v[N + "Wv"], "x3_wo": slotted(v[N + "Wp"]),
              "x3_b": v[N + "bp"][:, None]})
    N = "L3_ffn_"
    c.update({"f3_scale": v[N + "scale"][:, None], "f3_wg": v[N + "gate_w"].T, "f3_bg": row(v[N + "gate_b"]),
              "f3_b2": v[N + "mlp2_b"]})
    a = np.zeros((128, PACKED), np.float32)
    for name, (at, n) in AT.items():
        piece = np.asarray(c[name])
        a[0:piece.shape[0], at:at + n] = piece.reshape(piece.shape[0], n)
    return a


def experts(w1, w2, b1, width):
    E, n = w1.shape[0], len(b1)
    a = np.zeros((E, 128, width), np.float32)
    halves = w1.shape[2] // 128
    a[:, :, 0:128 * halves] = w1
    a[:, :, 128 * halves:128 * halves + 128] = w2
    for e in range(E):
        a[e, e, 128 * halves + 128:128 * halves + 256] = 1
    for j, b in enumerate(b1):
        a[:, :, width - n + j] = b
    return a.transpose(1, 0, 2).reshape(128, -1)


def arrays_of(v):
    v = {k: np.asarray(a) for k, a in v.items()}
    w1, b1 = v["L3_ffn_mlp1_w"].transpose(0, 2, 1), v["L3_ffn_mlp1_b"]
    w1 = np.concatenate([w1[:, :, 0::2], w1[:, :, 1::2]], 2)
    spread = lambda a: a.reshape(9, 256 * 4)
    return {
        "x_in": v["x"].transpose(2, 0, 1).reshape(D, T), "ctx_in": v["ctx_1024"].transpose(2, 0, 1).reshape(D, NB * CTX),
        "mask0_in": v["mask_Bx1x1xS2_if1"].reshape(NB, CTX), "mask2_in": v["mask_BxS2_bf1"].view(np.uint8),
        "packed_in": packed(v),
        "expert0_in": experts(v["L0_ffn_w1"], v["L0_ffn_w2"], [v["L0_ffn_b1"]], EXPERT0),
        "expert3_in": experts(w1, v["L3_ffn_mlp2_w"].transpose(0, 2, 1), [b1[:, 0::2], b1[:, 1::2]], EXPERT3),
        "stages_in": np.concatenate([spread(v["L2_ffn_up_weights"]), spread(v["L2_ffn_down_weights"])[::-1]]),
    }


def kernel(**inputs):
    import concourse.bacc as bacc
    from concourse.bass_utils import run_bass_kernel_spmd
    nc = bacc.Bacc("TRN2", target_bir_lowering=False, num_devices=1)
    arrays = {n: np.ascontiguousarray(a) for n, a in arrays_of(inputs).items()}
    args = [nc.dram_tensor(n, a.shape, mybir.dt.from_np(a.dtype), kind="ExternalInput").ap() for n, a in arrays.items()]
    args.append(nc.dram_tensor("out", (D, T), F32, kind="ExternalOutput").ap())
    build(nc, *args)
    r = run_bass_kernel_spmd(nc, [arrays], core_ids=[0])
    return r.results[0]["out"].reshape(D, NB, S).transpose(1, 2, 0)
```

```python
from contextlib import ExitStack

import numpy as np
import concourse.bass as bass
from concourse import mybir

ALU = mybir.AluOpType
ACT = mybir.ActivationFunctionType
AX = mybir.AxisListType.X
F32 = mybir.dt.float32
BF16 = mybir.dt.bfloat16
I32 = mybir.dt.int32
U8 = mybir.dt.uint8

D = 128
NB, S = 8, 100
T = NB * S
HALF = T // 2
CTX = 1444
H, DH = 16, 8
SLOT = 32
BIG = 1e30
LN_EPS = 1e-5
CHUNK = 512
KT_TILES = [(t * 128, min(128, CTX - t * 128)) for t in range(-(-CTX // 128))]
E0, K0 = 8, 2
E3, K3 = 16, 4
TOP = int(S * (1.0 - 0.9))

STAGES = 9
F0_CHAIN = 14

PIECES = [
    ("ident", 128), ("headmask", H), ("selx", 128), ("parity", 2), ("window", S), ("blockdiag", 128), ("sel64", 8 * 128),
    ("cosq", S), ("sinq", S), ("cosk", S), ("sink", S), ("maskab", 2),
    ("a0_wq", 128), ("a0_wk", 128), ("a0_wv", 128), ("a0_wo", 512), ("a0_bv", 128), ("a0_b", 3),
    ("x0_wq", 128), ("x0_wk", 128), ("x0_wv", 128), ("x0_wo", 512), ("x0_bv", 128), ("x0_b", 3),
    ("f0_wg", E0), ("f0_b2", 128),
    ("m_ln1", 2), ("m_ln2", 2), ("m_in", 512), ("m_conv", 2 * 5), ("m_xp", 2 * 40), ("m_dtw", 256), ("m_dtb", 2),
    ("m_alog", 32), ("m_d", 2), ("m_out", 256), ("m_w1", 256), ("m_b1", 2), ("m_w2", 256), ("m_b2", 1),
    ("m_sel", 16 * 256),
    ("x1_wq", 128), ("x1_wk", 128), ("x1_wv", 128),
    ("f1_wr", 128), ("f1_wk", 128), ("f1_wv", 128), ("f1_mu", 2),
    ("a2_wq", 128), ("a2_wk", 128), ("a2_wqs", 128), ("a2_wks", 128), ("a2_wv", 128), ("a2_wo", 512),
    ("x2_ln", 4), ("x2_g", 2), ("x2_wq", 1024), ("x2_wk", 1024), ("x2_wv", 1024), ("x2_wo", 1024), ("x2_b", 1),
    ("f2_we", 512), ("f2_wc", 512), ("f2_be", 512), ("f2_ub", 4), ("f2_b", 2),
    ("a3_wq", 128), ("a3_wk", 128), ("a3_wv", 128), ("a3_wo", 512), ("a3_bv", 128), ("a3_b", 3),
    ("x3_wq", 128), ("x3_wk", 128), ("x3_wv", 128), ("x3_wo", 512), ("x3_b", 1),
    ("f3_scale", 1), ("f3_wg", E3), ("f3_bg", E3), ("f3_b2", 128),
]
AT, _n = {}, 0
for _name, _w in PIECES:
    AT[_name] = (_n, _w)
    _n += _w
PACKED = _n
LOADS = ["ident", "x0_wq", "m_ln1", "x2_ln"]
EXPERT0 = 128 * 3 + 1
EXPERT3 = 128 * 4 + 2


def build(nc, x_in, ctx_in, mask0_in, mask2_in, packed_in, expert0_in, expert3_in, stages_in, out):
    with ExitStack() as scope:
        sems = {}

        def sem(name):
            if name not in sems:
                sems[name] = scope.enter_context(nc.semaphore(name))
            return sems[name]

        BEFORE, PIECES_OF_STEP = 10, 8

        LEFT = {}
        for kind, called, totals in (
            ("self", ("a0", "a2", "a3"), lambda L: dict(
                qk=2, qf=2, kf=2, scores=2 + NB, pv=2 + NB, staged=2 * NB, sub=1 + NB, v=NB, probs=NB, pt=1 + 2 * NB,
                t=2 * NB, vp=NB, oa=1 + NB, zero=2, exp=NB, chain=NB * {"a0": 5, "a2": 3, "a3": 10}[L], win=3 * NB, y=2)),
            ("cross", ("x0", "x1", "x2", "x3"), lambda L: {
                "x1": dict(ctx=16 * NB, ctx_used=1 + NB, exp=1 + 4 * NB, k=3 * NB, kf=3 * NB, pv=NB, vzero=1, q=2, qf=2, rd=NB,
                           scores=3 * NB, v=3 * NB, vp=4 * NB, o=1 + NB),
                "x2": dict(ctx=16 * NB, ctx_used=1 + NB, exp=1 + NB * H, nm=NB * H, o=1 + 2 * NB, mask=16 * NB, mrow=NB,
                           pv=2 + NB * H, q=NB, op0=2 * NB, rd=NB, rdt=NB, rdtf=NB, bc=NB, normed=NB, scores=1 + NB * H, y=NB,
                           vzero=4),
            }.get(L) or dict(
                q=2, qf=3, qlink=8, qw=16, scores=3 * NB * H, nm=3 * NB * H, joined=2 * NB, pv=2 + NB * H, exp=4 * NB * H, t=3 * NB * H, ctx=16 * NB,
                k=BEFORE + 6 * PIECES_OF_STEP + 6, kf=BEFORE + 6 * PIECES_OF_STEP + 6, split=3 * NB, split_act=3 * NB, kw=16 * NB, o=1 + NB, bc=8,
                rd=16, normed=8, y=2, vzero=2, ones=32, mxs=2 * NB, mlink=8 * NB, mx0=48 * NB, mx1=48 * NB,
                op0=16 * 13 * NB, op1=16 * 13 * NB, mask=16 * NB, mrow=NB, m01=NB, mneg=NB)),
            ("ffn", ("f0", "f1", "f2", "f3"), lambda L: {
                "f1": dict(x=2, h=4, sig=2, relu=2, act=2, y=2, rv=2, each=5),
                "f2": dict(made=12 * STAGES, gt=1, gtc=3, h=8, act=8, y=2),
            }.get(L) or dict(
                y_done=3 + 2 * E0, w0=8 * E0, w1=8 * E0, h=2 * E0, act=2 + 2 * E0, bc=2 * E0, up=2 + 2 * E0, gates=1, gt=1,
                gtc=1, logits=1, y=1, sub=1, exp=1, chain=F0_CHAIN, each=2 * (NB - 1))),
        ):
            before = {}
            for L in called:
                LEFT[L] = (kind, dict(before))
                for name, n in totals(L).items():
                    before[name] = before.get(name, 0) + n

        def of(L, name):
            return sem(f"{LEFT[L][0]}_{name}")

        def at(L, name, value):
            return of(L, name), value + LEFT[L][1].get(name, 0)

        W = scope.enter_context(nc.sbuf_tensor("weights", [128, PACKED], F32))
        PS = scope.enter_context(nc.psum_tensor("ps", [128, 8, CHUNK], F32))
        PSF = PS[:, :, :].rearrange("p b c -> p (b c)")
        X = scope.enter_context(nc.sbuf_tensor("x", [128, T], F32))
        R = scope.enter_context(nc.sbuf_tensor("residual", [128, T], F32))
        SQ = scope.enter_context(nc.sbuf_tensor("squares", [128, T], F32))
        mean_w = scope.enter_context(nc.sbuf_tensor("mean_w", [128, 128], F32))
        epsc = scope.enter_context(nc.sbuf_tensor("eps_column", [128, 1], F32))
        room = (212900 - 4 * (PACKED + 3 * T + 129 + 570)) // 4
        ARENA = scope.enter_context(nc.sbuf_tensor("arena", [128, room], F32))

        class Layout:

            def __init__(self, start=0):
                self.at = start

            def take(self, *shape):
                n = int(np.prod(shape))
                a = ARENA[:, self.at:self.at + n]
                self.at += n
                assert self.at <= room, (self.at, room)
                if len(shape) == 2:
                    a = a.rearrange("p (a b) -> p a b", a=shape[0])
                if len(shape) == 3:
                    a = a.rearrange("p (a b c) -> p a b c", a=shape[0], b=shape[1])
                return a

            def take_bf16(self, n):
                a = ARENA[:, self.at:self.at + (n + 1) // 2].bitcast(BF16)
                self.at += (n + 1) // 2
                return a

        def w(name, rows=128):
            a, n = AT[name]
            return W[0:rows, a:a + n]

        def wcol(name, j=0):
            a, _ = AT[name]
            return W[:, a + j:a + j + 1]

        def pool_wait(pool, s, value):
            pool.wait_ge(s, value)
            pool.sem_inc(sem("pool_passed"), 1)

        def sync_wait(sp, s, value):
            sp.wait_ge(s, value)
            sp.sem_inc(sem("sync_passed"), 1)

        ident = w("ident")

        def half(a, h):
            return a[:, h * HALF:(h + 1) * HALF]

        def loaded(eng, name):
            n = max(i for i, first in enumerate(LOADS) if AT[first][0] <= AT[name][0])
            eng.wait_ge(sem(f"w_loaded{n}"), 16)

        def x_ready(eng, c, h):
            if c < 0:
                eng.wait_ge(sem("x_loaded"), 16)
            else:
                eng.wait_ge(sem("ln_out"), 2 * c + h + 1)

        def norm_pe(pe, c):
            for h in range(2):
                pe.wait_ge(sem("ln_row"), 2 * c + h + 1)
                if c == 0 and h == 0:
                    pe.wait_ge(sem("consts"), 2)
                pe.matmul(PS[:, 6 + h, 0:HALF], mean_w[:, :], half(R, h), start=True, stop=True) \
                    .then_inc(sem("ln_mean"), 1)
            for h in range(2):
                pe.wait_ge(sem("ln_square"), 2 * c + h + 1)
                pe.matmul(PS[:, 6 + h, 0:HALF], mean_w[:, :], half(SQ, h), start=True, stop=True) \
                    .then_inc(sem("ln_var"), 1)

        def norm_act(act, c):
            for h in range(2):
                act.wait_ge(sem("ln_centred"), 2 * c + h + 1)
                act.activation(half(SQ, h), half(R, h), ACT.Square).then_inc(sem("ln_square"), 1)
            for h in range(2):
                act.wait_ge(sem("ln_var"), 2 * c + h + 1)
                act.activation(half(SQ, h), PS[:, 6 + h, 0:HALF], ACT.Ln, bias=epsc[:, :]).then_inc(sem("ln_log"), 1)
            for h in range(2):
                act.wait_ge(sem("ln_log"), 2 * c + h + 1)
                act.activation(half(SQ, h), half(SQ, h), ACT.Exp, scale=-0.5).then_inc(sem("ln_rstd"), 1)

        def norm_dve(dve, c, rows, dst=None, affine=None):
            dst = X if dst is None else dst
            for h in range(2):
                rows(h).then_inc(sem("ln_row"), 1)
            for h in range(2):
                dve.wait_ge(sem("ln_mean"), 2 * c + h + 1)
                dve.tensor_tensor(half(R, h), half(R, h), PS[:, 6 + h, 0:HALF], ALU.subtract) \
                    .then_inc(sem("ln_centred"), 1)
            for h in range(2):
                dve.wait_ge(sem("ln_rstd"), 2 * c + h + 1)
                if affine is None:
                    dve.tensor_tensor(half(dst, h), half(R, h), half(SQ, h), ALU.mult).then_inc(sem("ln_out"), 1)
                else:
                    gain, shift = affine
                    dve.scalar_tensor_tensor(half(dst, h), half(R, h), gain, half(SQ, h), ALU.mult, ALU.mult) \
                        .then_inc(sem("ln_scaled"), 1)
                    dve.wait_ge(sem("ln_scaled"), 2 * (0 if c == C_M1 else 1) + h + 1)
                    dve.tensor_scalar(half(dst, h), half(dst, h), shift, None, ALU.add).then_inc(sem("ln_out"), 1)

        def residual(dve, c, ready, y, bias=None):
            def rows(h):
                ready(h)
                if bias is None:
                    return dve.tensor_tensor(half(R, h), y(h), half(X, h), ALU.add)
                return dve.scalar_tensor_tensor(half(R, h), y(h), bias, half(X, h), ALU.add, ALU.add)
            norm_dve(dve, c, rows)

        def bank(b, n=HALF):
            return PS[:, b, 0:n]

        C_A0, C_X0, C_F0, C_M1, C_M2, C_M, C_X1, C_F1, C_A2, C_X2, C_F2, C_A3, C_X3, C_F3 = range(14)

        class Step:

            def __init__(self, k, i=None):
                self.k, self.i = k, i

            def n(self, times, plus=0):
                if self.i is None:
                    return self.k * times + plus
                return self.i * (2 * times) + (self.k * times + plus)

            def buf(self, ahead=0):
                return (self.k + ahead) % 2

            def piece(self, j):
                if self.i is not None:
                    return self.n(PIECES_OF_STEP, BEFORE + j)
                return BEFORE + 6 * PIECES_OF_STEP + (5 + j if self.k == 7 else j if j == 0 else j - 3)

        RUN = [Step(6), Step(7)]

        def steps(eng, body):
            with eng.Fori(0, (NB - 2) // 2) as i:
                for k in range(2):
                    body(Step(k, i), True, True)
            body(RUN[0], True, False)
            body(RUN[1], False, False)

        def self_buffers():
            lay = Layout()
            return dict(
                q=lay.take(T), k=lay.take(T), ta=lay.take(T), tb=lay.take(T), o=lay.take(4, T),
                xb=[lay.take(S) for _ in range(2)], qbd=[lay.take(H, S) for _ in range(2)],
                v=[lay.take(H, SLOT) for _ in range(2)], p=[lay.take(H, S) for _ in range(2)],
                pt=[lay.take(H, S) for _ in range(2)], s2=lay.take(H, S), s3=lay.take(H, S),
                best=[lay.take(H, 8) for _ in range(2)], mx=[lay.take(H) for _ in range(2)],
                den=[lay.take(H) for _ in range(2)])

        SB = self_buffers()
        SPRE = {"window": "a0", "rope": "a2", "top": "a3"}

        def self_pe(pe, kind, c):
            L = SPRE[kind]
            names = ["wq", "wk"] + (["wqs", "wks"] if kind == "rope" else [])
            loaded(pe, f"{L}_wq")
            for h in range(2):
                x_ready(pe, c, h)
                for j, name in enumerate(names):
                    mm = pe.matmul(bank(2 * j + h), w(f"{L}_{name}"), half(X, h), start=True, stop=True)
                mm.then_inc(of(L, "qk"), 1)
            pe.wait_ge(*at(L, "qf", 2))
            pe.wait_ge(*at(L, "kf", 2))
            pe.sem_inc(of(L, "scores"), 2)
            pe.sem_inc(of(L, "pv"), 2)

            def scores(b, ahead):
                k = b.buf(ahead)
                pe.wait_ge(*at(L, "staged", b.n(2, 2 * ahead + 2)))
                pe.wait_ge(*at(L, "sub", b.n(1, ahead + 1)))
                pe.matmul(PS[0:S, 6, k * 128:k * 128 + D], SB["xb"][k], w(f"{L}_wv"), start=True, stop=True) \
                    .then_inc(of(L, "v"), 1)
                for hd in range(H):
                    mm = pe.matmul(PS[0:S, hd // 4, (hd % 4) * S:(hd % 4 + 1) * S], SB["qbd"][k][:, hd, :],
                                   SB["k"][:, bass.ds(b.n(S, S * ahead), S)], start=True, stop=True)
                mm.then_inc(of(L, "scores"), 1)

            def body(b, following, more):
                k = b.buf()
                if following:
                    scores(b, 1)
                pe.wait_ge(*at(L, "probs", b.n(1, 1)))
                for j in range(2):
                    pe.wait_ge(*at(L, "pt", b.n(2, j + 1)))
                    for q in range(8):
                        mm = pe.transpose(PS[0:S, 4 + q // 4, (q % 4) * S:(q % 4 + 1) * S],
                                          SB["p"][k][0:S, 8 * j + q, :], ident[0:S, 0:S])
                    mm.then_inc(of(L, "t"), 1)
                pe.wait_ge(*at(L, "pt", b.n(2, 3)))
                pe.wait_ge(*at(L, "vp", b.n(1, 1)))
                pe.wait_ge(*at(L, "oa", b.n(1, 1)))
                for hd in range(H):
                    q = hd % 4
                    mm = pe.matmul(PS[SLOT * q:SLOT * (q + 1), 7, (hd // 4) * S:(hd // 4 + 1) * S],
                                   SB["v"][k][0:S, hd, :], SB["pt"][k][0:S, hd, :], start=True, stop=True)
                mm.then_inc(of(L, "pv"), 1)

            scores(Step(0), 0)
            steps(pe, body)
            pe.wait_ge(*at(L, "oa", 1 + NB))
            project_out_pe(pe, L, SB["o"])
            norm_pe(pe, c + 1)

        def project_out_pe(pe, L, o):
            wo = w(f"{L}_wo").rearrange("p (g n) -> p g n", g=4)
            for h in range(2):
                for g in range(4):
                    mm = pe.matmul(bank(h), wo[:, g, :], o[:, g, h * HALF:(h + 1) * HALF],
                                   start=(g == 0), stop=(g == 3))
                mm.then_inc(of(L, "y"), 1)

        def self_pool(pool, kind, c):
            L = SPRE[kind]
            x_ready(pool, c, 1)
            for k in range(2):
                pool.memset(SB["v"][k], 0.0).then_inc(of(L, "zero"), 1)
            pool.wait_ge(*at(L, "qf", 2))
            loaded(pool, "headmask")
            hm = w("headmask").unsqueeze(2).to_broadcast([128, H, S])
            with pool.Fori(0, NB // 2) as i:
                for k in range(2):
                    b0 = i * (2 * S) + k * S
                    pool.wait_ge(*at(L, "scores", i * 2 + (k + 1)))
                    pool.tensor_copy(SB["xb"][k], X[:, bass.ds(b0, S)]).then_inc(of(L, "staged"), 1)
                    pool.tensor_tensor(SB["qbd"][k], SB["q"][:, bass.ds(b0, S)].unsqueeze(1).to_broadcast([128, H, S]),
                                       hm, ALU.mult).then_inc(of(L, "staged"), 1)

        def self_act(act, kind, c):
            L = SPRE[kind]
            if kind != "rope":
                for h in range(2):
                    act.wait_ge(*at(L, "qk", h + 1))
                    act.activation(half(SB["k"], h), bank(2 + h), ACT.Identity, bias=wcol(f"{L}_b", 1)) \
                        .then_inc(of(L, "kf"), 1)
            act.sem_inc(of(L, "pt"), 1)
            act.sem_inc(of(L, "oa"), 1)
            with act.Fori(0, NB // 2) as i:
                for k in range(2):
                    act.wait_ge(*at(L, "sub", i * 2 + (k + 2)))
                    act.activation(SB["p"][k][0:S], SB["p"][k][0:S], ACT.Exp).then_inc(of(L, "exp"), 1)
                    act.wait_ge(*at(L, "pv", i * 2 + (k + 1)))
                    for j in range(2):
                        act.wait_ge(*at(L, "t", i * 4 + (2 * k + j + 1)))
                        act.activation(SB["pt"][k][0:S, 8 * j:8 * j + 8, :].rearrange("p (a b) s -> p a (b s)", a=2),
                                       PS[0:S, 4:6, 0:4 * S], ACT.Copy).then_inc(of(L, "pt"), 1)
                    act.wait_ge(*at(L, "pv", i * 2 + (k + 3)))
                    act.activation(SB["o"][:, :, bass.ds(i * (2 * S) + k * S, S)],
                                   PS[:, 7, 0:4 * S].rearrange("p (g s) -> p g s", g=4), ACT.Copy) \
                        .then_inc(of(L, "oa"), 1)
            norm_act(act, c + 1)

        def self_dve(dve, kind, c):
            L = SPRE[kind]
            scale = DH ** -0.5
            loaded(dve, f"{L}_wq")
            for h in range(2):
                dve.wait_ge(*at(L, "qk", h + 1))
                if kind == "rope":
                    for n, (name, dst) in enumerate((("q", SB["q"]), ("k", SB["k"]))):
                        base = 8 * h + 4 * n
                        tabs = [w(t + name).unsqueeze(1).to_broadcast([128, 4, S]) for t in ("cos", "sin")]
                        for j, tmp in enumerate((SB["ta"], SB["tb"])):
                            dve.tensor_tensor(half(tmp, h).rearrange("p (b s) -> p b s", b=4),
                                              bank(n * 2 + h + 4 * j).rearrange("p (b s) -> p b s", b=4),
                                              tabs[j], ALU.mult).then_inc(sem("rope"), 1)
                        dve.wait_ge(sem("rope"), 4 * h + 2 * n + 2)
                        dve.tensor_tensor(half(dst, h), half(SB["ta"], h), half(SB["tb"], h), ALU.add) \
                            .then_inc(of(L, f"{name}f"), 1)
                        dve.wait_ge(*at(L, f"{name}f", h + 1))
                else:
                    dve.tensor_scalar(half(SB["q"], h), bank(h), wcol(f"{L}_b", 0), scale, ALU.add, ALU.mult) \
                        .then_inc(of(L, "qf"), 1)
            dve.wait_ge(*at(L, "zero", 2))
            dve.sem_inc(of(L, "sub"), 1)
            links = {"window": 5, "rope": 3, "top": 10}[kind]
            chain = of(L, "chain")

            def before(b, ahead):
                k = b.buf(ahead)
                P, MX = SB["p"][k], SB["mx"][k]
                dve.wait_ge(*at(L, "pv", b.n(1, ahead + 1)))
                dve.wait_ge(*at(L, "v", b.n(1, ahead + 1)))
                vps = PS[0:S, 6, k * 128:k * 128 + D].rearrange("p (h d) -> p h d", h=H)
                if kind == "rope":
                    dve.tensor_copy(SB["v"][k][0:S, :, 0:DH], vps).then_inc(of(L, "vp"), 1)
                else:
                    dve.tensor_tensor(SB["v"][k][0:S, :, 0:DH], vps,
                                      w(f"{L}_bv", S).rearrange("p (h d) -> p h d", h=H), ALU.add) \
                        .then_inc(of(L, "vp"), 1)
                dve.wait_ge(*at(L, "scores", b.n(1, ahead + 3)))
                sps = PS[0:S, 0:4, 0:4 * S].rearrange("p a (b s) -> p a b s", b=4)
                n = [0]

                def link(ins):
                    n[0] += 1
                    ins.then_inc(chain, 1)
                    dve.wait_ge(*at(L, "chain", b.n(links, links * ahead + n[0])))

                four = lambda a: a[0:S].rearrange("p (a b) s -> p a b s", a=4)
                wide = lambda a: a[0:S].rearrange("p (a b) -> p a b", a=4).unsqueeze(3).to_broadcast([S, 4, 4, S])
                if kind == "window":
                    win = w("window", S).unsqueeze(1).to_broadcast([S, 4, S])
                    for a in range(4):
                        ins = dve.tensor_tensor(SB["s2"][0:S, 4 * a:4 * a + 4, :],
                                                PS[0:S, a, 0:4 * S].rearrange("p (b s) -> p b s", b=4), win, ALU.add)
                        if a < 3:
                            ins.then_inc(of(L, "win"), 1)
                    link(ins)
                    dve.wait_ge(*at(L, "win", b.n(3, 3 * ahead + 3)))
                    link(dve.tensor_reduce(MX[0:S], SB["s2"][0:S], AX, ALU.max))
                    link(dve.tensor_tensor(P[0:S], SB["s2"][0:S], MX[0:S].unsqueeze(2).to_broadcast([S, H, S]), ALU.subtract))
                elif kind == "rope":
                    link(dve.tensor_reduce(MX[0:S], sps, AX, ALU.max))
                    for a in range(4):
                        ins = dve.tensor_tensor(P[0:S, 4 * a:4 * a + 4, :],
                                                PS[0:S, a, 0:4 * S].rearrange("p (b s) -> p b s", b=4),
                                                MX[0:S, 4 * a:4 * a + 4].unsqueeze(2).to_broadcast([S, 4, S]), ALU.subtract)
                        if a < 3:
                            ins.then_inc(of(L, "win"), 1)
                    dve.wait_ge(*at(L, "win", b.n(3, 3 * ahead + 3)))
                else:
                    S0, S2, S3, B8, B9 = P, SB["s2"], SB["s3"], SB["best"][0], SB["best"][1]
                    link(dve.tensor_copy(four(S0), sps))
                    dve.sem_inc(sem("dve_passed"), 1)
                    for hd in range(H):
                        ins = dve.max(B8[0:S, hd, :], S0[0:S, hd, :])
                        if hd < H - 1:
                            ins.then_inc(of(L, "each"), 1)
                    link(ins)
                    dve.wait_ge(*at(L, "each", b.n(3 * (H - 1), (3 * ahead + 1) * (H - 1))))
                    dve.sem_inc(sem("dve_passed"), 1)
                    for hd in range(H):
                        ins = dve.match_replace(S2[0:S, hd, :], B8[0:S, hd, :], S0[0:S, hd, :], -BIG)
                        if hd < H - 1:
                            ins.then_inc(of(L, "each"), 1)
                    link(ins)
                    dve.wait_ge(*at(L, "each", b.n(3 * (H - 1), (3 * ahead + 2) * (H - 1))))
                    dve.sem_inc(sem("dve_passed"), 1)
                    for hd in range(H):
                        ins = dve.max(B9[0:S, hd, :], S2[0:S, hd, :])
                        if hd < H - 1:
                            ins.then_inc(of(L, "each"), 1)
                    link(ins)
                    dve.wait_ge(*at(L, "each", b.n(3 * (H - 1), (3 * ahead + 3) * (H - 1))))
                    link(dve.memset(B9[0:S, :, TOP - 8:8], -BIG))
                    dve.sem_inc(sem("dve_passed"), 1)
                    for hd in range(H):
                        ins = dve.match_replace(S3[0:S, hd, :], B9[0:S, hd, :], S2[0:S, hd, :], -BIG)
                        if hd < H - 1:
                            ins.then_inc(of(L, "last"), 1)
                    link(ins)
                    dve.wait_ge(*at(L, "last", b.n(H - 1, (ahead + 1) * (H - 1))))
                    dve.scalar_tensor_tensor(P[0:S], S3[0:S], -BIG, S0[0:S], ALU.is_le, ALU.mult) \
                        .then_inc(of(L, "each2"), 1)
                    dve.wait_ge(*at(L, "each2", b.n(1, ahead + 1)))
                    link(dve.tensor_scalar(MX[0:S], B8[0:S, :, 0], 0.0, None, ALU.max))
                    link(dve.tensor_tensor(P[0:S], P[0:S], MX[0:S].unsqueeze(2).to_broadcast([S, H, S]), ALU.subtract))
                assert n[0] == links - 2, (kind, n, links)
                if kind == "rope":
                    ins.then_inc(of(L, "sub"), 1)
                else:
                    dve.sem_inc(of(L, "sub"), 1)

            def after(b):
                k = b.buf()
                P, DEN = SB["p"][k], SB["den"][k]
                dve.wait_ge(*at(L, "exp", b.n(1, 1)))
                dve.tensor_reduce(DEN[0:S], P[0:S], AX, ALU.add).then_inc(chain, 1)
                dve.wait_ge(*at(L, "chain", b.n(links, links - 1)))
                dve.reciprocal(DEN[0:S], DEN[0:S]).then_inc(chain, 1)
                dve.wait_ge(*at(L, "chain", b.n(links, links)))
                dve.tensor_tensor(P[0:S], P[0:S], DEN[0:S].unsqueeze(2).to_broadcast([S, H, S]), ALU.mult) \
                    .then_inc(of(L, "probs"), 1)

            def body(b, following, more):
                after(b)
                if following:
                    before(b, 1)

            before(Step(0), 0)
            steps(dve, body)
            residual(dve, c + 1, lambda h: dve.wait_ge(*at(L, "y", h + 1)), bank,
                     None if kind == "rope" else wcol(f"{L}_b", 2))

        NT = len(KT_TILES)
        KEY_CHUNKS = [(0, 512), (512, 512), (1024, CTX - 1024)]
        KPART, QPART = (0, 0, 0, 1, 1, 2), (0, 1, 2, 0, 1, 0)
        MASK_ROW, MAX_ROW, ROWS = 96, 98, 101
        PAIR, VW = H // 2, DH + 1

        def cross_buffers():
            lay = Layout()
            two = range(2)
            d = dict(
                o=lay.take(4, T), ctx=[lay.take(CTX) for _ in two], kf=lay.take(CTX),
                v=[lay.take(NT, H, VW) for _ in two], pt=lay.take(2, NT, S),
                mx=[lay.take(H) for _ in two], neg=lay.take(S))
            bf = lay.take_bf16
            d["kp"] = bf(3 * CTX).rearrange("p (c n) -> p c n", c=3)
            d["kk"] = [bf(PAIR * CTX).rearrange("p (a n) -> p a n", a=PAIR) for _ in two]
            d["qq"] = [bf(H * S).rearrange("p (a n) -> p a n", a=PAIR) for _ in two]
            d["mc"] = [bf(3 * S).rearrange("p (c n) -> p c n", c=3) for _ in two]
            d["mask"] = d["m01"] = lay.take(CTX)
            d["q"] = d["kf"][:, 0:T]
            d["mrow"] = [a[:, 0:CTX // 2].bitcast(BF16) for a in (R, SQ)]
            d["mx3"] = [a[:, CTX // 2:CTX // 2 + 3 * H].rearrange("p (h c) -> p h c", c=3) for a in (R, SQ)]
            d["ones"] = SQ[0:ROWS - MASK_ROW, 0:CTX // 2].bitcast(BF16)
            d["qp"] = d["pt"].rearrange("p k t s -> p (k t s)").bitcast(BF16).rearrange("p (c b e n) -> p c b e n", c=3, b=NB, e=2)
            d["pt"] = [d["pt"][:, k] for k in two]
            d["rd"] = d["kk"][0].rearrange("p a n -> p (a n)")[:, 0:2 * 4 * T].bitcast(F32).rearrange("p (n c) -> p n c", n=8)
            return d

        CB = cross_buffers()
        k_parts = nc.dram_tensor("k_parts", (2, 3, 128, CTX), BF16, kind="Internal").ap()
        q_parts = nc.dram_tensor("q_parts", (3, 128, NB * 2 * S), BF16, kind="Internal").ap()
        def cross_sync(sp, L, c, masked):
            def keys_in(b, ahead):
                k = b.buf(ahead)
                sync_wait(sp, *at(L, "split", b.n(3, 3 * ahead + 3)))
                sp.dma_start(k_parts[k].rearrange("c p n -> p c n"), CB["kp"]).then_inc(of(L, "kw"), 16)
                sync_wait(sp, *at(L, "kw", b.n(16, 16 * ahead + 16)))

            def operand(b, ahead, half_):
                k, done = b.buf(ahead), of(L, f"op{half_}")
                pairs = slice(4 * half_, 4 * half_ + 4)
                for j in range(6):
                    rows = slice(16 * j, 16 * j + 16)
                    sp.dma_start(CB["kk"][k][rows, pairs, :],
                                 k_parts[k, KPART[j]].rearrange("(a r) n -> r a n", a=PAIR)[:, pairs, :]).then_inc(done, 16)
                    sp.dma_start(CB["qq"][k][rows, pairs, :],
                                 q_parts[QPART[j]].rearrange("(a r) n -> r a n", a=PAIR)[:, pairs, bass.ds(b.n(2 * S, 2 * S * ahead), 2 * S)]) \
                        .then_inc(done, 16)
                if masked:
                    sync_wait(sp, *at(L, "mrow", b.n(1, ahead + 1)))
                    sp.dma_start(CB["kk"][k][MASK_ROW:MASK_ROW + 2, pairs, :],
                                 CB["mrow"][k][0:2].unsqueeze(1).to_broadcast([2, 4, CTX])).then_inc(done, 16)

            def maxima(b, ahead, half_):
                sync_wait(sp, *at(L, "mxs", b.n(2, 2 * ahead + half_ + 1)))
                k = b.buf(ahead)
                for part in range(3):
                    sp.dma_start(CB["qq"][k][MAX_ROW + part:MAX_ROW + part + 1, 4 * half_:4 * half_ + 4, :]
                                 .rearrange("c a (e n) -> c (a e) n", e=2), CB["mc"][half_][0:8, part, :]) \
                        .then_inc(of(L, f"mx{half_}"), 16)

            def context(b, ahead):
                k = b.buf(ahead)
                sp.dma_start(CB["ctx"][k], ctx_in[:, bass.ds(b.n(CTX, CTX * ahead), CTX)]).then_inc(of(L, "ctx"), 16)

            def mask(b, ahead):
                if masked:
                    if ahead == 3:
                        sync_wait(sp, *at(L, "kf", b.n(PIECES_OF_STEP, BEFORE + PIECES_OF_STEP)))
                    elif ahead:
                        sync_wait(sp, *at(L, "kf", 3 * ahead))
                    sp.dma_start(CB["mask"].bitcast(I32), mask0_in[bass.ds(b.n(1, ahead), 1), :].partition_broadcast(128)) \
                        .then_inc(of(L, "mask"), 16)

            zero = Step(0)
            x_ready(sp, c, 1)
            context(zero, 0)
            sp.wait_ge(*at(L, "vzero", 1))
            for k in range(2):
                sp.dma_start(CB["kk"][k][MASK_ROW:ROWS], CB["ones"].unsqueeze(1).to_broadcast([ROWS - MASK_ROW, PAIR, CTX])) \
                    .then_inc(of(L, "ones"), 16)
            context(zero, 1)
            mask(zero, 0)
            sp.wait_ge(*at(L, "qf", 3))
            sp.dma_start(q_parts.rearrange("c p n -> p c n"), CB["qp"].rearrange("p c b e n -> p c (b e n)")).then_inc(of(L, "qw"), 16)
            sp.wait_ge(*at(L, "qw", 16))
            sp.wait_ge(*at(L, "ones", 32))
            mask(zero, 1)
            for ahead in range(2):
                keys_in(zero, ahead)
                for half_ in range(2):
                    if ahead:
                        sp.wait_ge(*at(L, "scores", 24 * half_ + 1))
                    operand(zero, ahead, half_)
            sp.wait_ge(*at(L, "k", 9))
            context(zero, 2)
            mask(zero, 2)
            maxima(zero, 0, 0)

            def body(b):
                n = 0 if b.i is not None else b.k
                maxima(b, 0, 1)
                if n + 2 < NB:
                    keys_in(b, 2)
                if n + 1 < NB:
                    maxima(b, 1, 0)
                if n + 2 < NB:
                    sync_wait(sp, *at(L, "pv", b.n(H, 2 + 8)))
                    operand(b, 2, 0)
                if n + 3 < NB:
                    sync_wait(sp, *at(L, "k", b.n(PIECES_OF_STEP, BEFORE + PIECES_OF_STEP)))
                    context(b, 3)
                    mask(b, 3)
                if n + 2 < NB:
                    sync_wait(sp, *at(L, "pv", b.n(H, 2 + H)))
                    operand(b, 2, 1)

            with sp.Fori(0, 2) as i:
                for k in range(2):
                    body(Step(k, i))
            for k in range(4, NB):
                body(Step(k))

        def cross_pe(pe, L, c, masked):
            phase1 = MAX_ROW if masked else MASK_ROW
            ops = 16 * (13 if masked else 12)

            def piece(n, mms):
                if not isinstance(n, int) or n:
                    pe.wait_ge(*at(L, "kf", n))
                for dst, lhs, rhs in mms:
                    mm = pe.matmul(dst, lhs, rhs, start=True, stop=True)
                mm.then_inc(of(L, "k"), 1)

            def keys(b, ahead, n, j):
                if j == 0:
                    pe.wait_ge(*at(L, "ctx", b.n(16, 16 * ahead + 16) if b.i is not None or ahead > 1 else 32))
                c0, m = KEY_CHUNKS[j]
                piece(n, [(PS[:, 6, 0:m], w(f"{L}_wk"), CB["ctx"][b.buf(ahead)][:, c0:c0 + m])])

            def values(b, ahead, n, j):
                ctx = CB["ctx"][b.buf(ahead)]
                piece(n, [(PS[0:m, 6, (t % 4) * 128:(t % 4) * 128 + 128], ctx[:, t0:t0 + m], w(f"{L}_wv"))
                                for t, (t0, m) in list(enumerate(KT_TILES))[4 * j:4 * j + 4]])

            def turn_maxima(b, ahead, n, j):
                pe.wait_ge(*at(L, "joined", b.n(2, 2 * ahead + j + 1)))
                pe.wait_ge(*at(L, "kf", n))
                pe.transpose(PS[0:8, 6, 0:S], CB["mx"][b.buf(ahead)][0:S, 8 * j:8 * j + 8], ident[0:S, 0:S]) \
                    .then_inc(of(L, "k"), 1)

            def rows_of_queries(b, ahead, h, apart=1, first=0):
                if h % 8 == 0:
                    pe.wait_ge(*at(L, f"op{h // 8}", b.n(ops, ops * (ahead + 1))))
                k = b.buf(ahead)
                for j, (c0, m) in enumerate(KEY_CHUNKS):
                    if b.i is not None or ahead or h >= apart:
                        pe.wait_ge(*at(L, "nm", b.n(3 * H, 3 * (H * ahead + h - apart) + j + 1)))
                    pe.matmul(PSF[0:S, CHUNK * first + c0:CHUNK * first + c0 + m], CB["qq"][k][0:phase1, h // 2, (h % 2) * S:(h % 2 + 1) * S],
                              CB["kk"][k][0:phase1, h // 2, c0:c0 + m], start=True, stop=True).then_inc(of(L, "scores"), 1)

            def rows_of_keys(b, ahead, h):
                if h % 8 == 0:
                    pe.wait_ge(*at(L, f"mx{h // 8}", b.n(48, 48 * (ahead + 1))))
                k = b.buf(ahead)
                for g in range(3):
                    if b.i is not None or ahead or h:
                        pe.wait_ge(*at(L, "exp", b.n(4 * H, 4 * (H * ahead + h - 1) + (1, 2, 4)[g])))
                    for t in range(4 * g, 4 * g + 4):
                        t0, m = KT_TILES[t]
                        mm = pe.matmul(PS[0:m, 3 + g, (t % 4) * S:(t % 4 + 1) * S], CB["kk"][k][0:ROWS, h // 2, t0:t0 + m],
                                       CB["qq"][k][0:ROWS, h // 2, (h % 2) * S:(h % 2 + 1) * S], start=True, stop=True)
                    mm.then_inc(of(L, "t"), 1)

            def product(b, h):
                pe.wait_ge(*at(L, "exp", b.n(4 * H, 4 * (h + 1))))
                if h == 0:
                    pe.wait_ge(*at(L, "o", b.n(1, 1)))
                q = h % 4
                for t, (t0, m) in enumerate(KT_TILES):
                    mm = pe.matmul(PS[SLOT * q:SLOT * q + VW, 7, (h // 4) * S:(h // 4 + 1) * S],
                                   CB["v"][b.buf()][0:m, t, h, :], CB["pt"][h % 2][0:m, t, :], start=(t == 0), stop=(t == NT - 1))
                mm.then_inc(of(L, "pv"), 1)

            loaded(pe, f"{L}_wq")
            for h in range(2):
                x_ready(pe, c, h)
                pe.matmul(bank(h), w(f"{L}_wq"), half(X, h), start=True, stop=True).then_inc(of(L, "q"), 1)
            zero = Step(0)
            for ahead in range(2):
                for j in range(3):
                    keys(zero, ahead, 3 * ahead + j, j)
            for j in range(3):
                values(zero, 0, 6 + j, j)
            pe.sem_inc(of(L, "pv"), 2)
            for h in range(H):
                rows_of_queries(zero, 0, h, apart=2, first=3 * (h % 2))
                if h == 9:
                    turn_maxima(zero, 0, 9, 0)
            pe.wait_ge(*at(L, "ones", 32))
            pe.wait_ge(*at(L, "nm", 3 * H))
            rows_of_keys(zero, 0, 0)

            def body(b, following, more):
                n = b.piece
                for h in range(H):
                    if following:
                        rows_of_queries(b, 1, h)
                    if h < H - 1:
                        rows_of_keys(b, 0, h + 1)
                    elif following:
                        rows_of_keys(b, 1, 0)
                    if h == 1:
                        turn_maxima(b, 0, n(0), 1)
                    if more and 2 <= h <= 4:
                        keys(b, 2, n(h - 1), h - 2)
                    if following:
                        if h == 9:
                            turn_maxima(b, 1, n(4), 0)
                        if 10 <= h <= 12:
                            values(b, 1, n(h - 5), h - 10)
                    product(b, h)

            steps(pe, body)
            pe.wait_ge(*at(L, "o", 1 + NB))
            selx = w("selx")
            for g in range(4):
                for h in range(2):
                    if 2 * g + h >= 6:
                        pe.wait_ge(*at(L, "rd", 2 * g + h - 5))
                    pe.matmul(bank((2 * g + h) % 6), selx, CB["o"][:, g, h * HALF:(h + 1) * HALF], start=True, stop=True) \
                        .then_inc(of(L, "bc"), 1)
            pe.wait_ge(*at(L, "normed", 8))
            project_out_pe(pe, L, CB["o"])
            norm_pe(pe, c + 1)

        def cross_pool(pool, L, c, masked):
            zero = Step(0)

            def split(b, ahead):
                n = lambda j: b.n(3, 3 * ahead + j)
                pool.wait_ge(*at(L, "split_act", b.n(3, 3 * ahead + 3)))
                pool.tensor_tensor(CB["kf"], CB["kf"], CB["kp"][:, 0, :], ALU.subtract).then_inc(of(L, "split"), 1)
                pool_wait(pool, *at(L, "split", n(1)))
                pool.tensor_copy(CB["kp"][:, 1, :], CB["kf"]).then_inc(of(L, "split"), 1)
                pool.wait_ge(*at(L, "split", n(2)))
                pool.tensor_tensor(CB["kp"][:, 2, :], CB["kf"], CB["kp"][:, 1, :], ALU.subtract).then_inc(of(L, "split"), 1)

            loaded(pool, "headmask")
            x_ready(pool, c, 1)
            split(zero, 1)

            def body(b, following, more):
                if more:
                    split(b, 2)

            with pool.Fori(0, (NB - 2) // 2) as i:
                for k in range(2):
                    body(Step(k, i), True, True)

        def cross_act(act, L, c, masked):
            last = KT_TILES[-1][1]

            def first_part(b, ahead, n, j):
                act.wait_ge(*at(L, "kf", n + 1))
                if j == 0 and (b.i is not None or ahead):
                    act.wait_ge(*at(L, "kw", b.n(16, 16 * ahead)))
                c0, m = KEY_CHUNKS[j]
                act.activation(CB["kp"][:, 0, c0:c0 + m], CB["kf"][:, c0:c0 + m], ACT.Copy).then_inc(of(L, "split_act"), 1)

            for ahead in range(2):
                for j in range(3):
                    first_part(Step(0), ahead, 3 * ahead + j, j)
                if not ahead:
                    act.wait_ge(*at(L, "split", 1))
                    act.activation(CB["kp"][:, 1, :], CB["kf"], ACT.Copy).then_inc(of(L, "split"), 1)

            def body(b, following, more):
                for h in range(H):
                    if more and 3 <= h <= 5:
                        first_part(b, 2, b.piece(h - 2), h - 3)
                    pt = CB["pt"][h % 2]
                    act.wait_ge(*at(L, "pv", b.n(H, h + 1)))
                    for g in range(3):
                        act.wait_ge(*at(L, "t", b.n(3 * H, 3 * h + g + 1)))
                        for t, m, rows in ((4 * g, 4, 128),) if g < 2 else ((8, 3, 128), (11, 1, last)):
                            act.activation(pt[0:rows, t:t + m, :].rearrange("p t s -> p (t s)"),
                                           PS[0:rows, 3 + g, (t % 4) * S:(t % 4 + m) * S], ACT.Exp).then_inc(of(L, "exp"), 1)

            steps(act, body)
            for n in range(8):
                act.wait_ge(*at(L, "bc", n + 1))
                act.activation(CB["rd"][:, n, :], bank(n % 6), ACT.Ln).then_inc(of(L, "rd"), 1)
            for n in range(8):
                act.wait_ge(*at(L, "rd", n + 1))
                act.activation(CB["rd"][:, n, :], CB["rd"][:, n, :], ACT.Exp, scale=-1.0).then_inc(of(L, "rd"), 1)
            norm_act(act, c + 1)

        def cross_dve(dve, L, c, masked):
            has_bias = L == "x0"
            scale = 1.0 if L == "x0" else DH ** -0.5
            chain, links = of(L, "mlink"), 4

            def mask(b, ahead):
                k = b.buf(ahead)
                dve.wait_ge(*at(L, "mask", b.n(16, 16 * ahead + 16)))
                dve.tensor_scalar(CB["m01"], CB["mask"].bitcast(I32), 0.0, 0.0, ALU.is_equal, ALU.is_equal).then_inc(of(L, "m01"), 1)
                if b.i is not None:
                    dve.wait_ge(*at(L, "op1", b.n(208, 208 * (ahead - 1))))
                elif ahead:
                    dve.wait_ge(*at(L, "ones", 32))
                dve.wait_ge(*at(L, "m01", b.n(1, ahead + 1)))
                dve.tensor_scalar(CB["mrow"][k][0:2], CB["m01"][0:2], 0.0, wcol("maskab", 0)[0:2], ALU.is_equal, ALU.mult) \
                    .then_inc(of(L, "mrow"), 1)

            def key_piece(b, ahead, n, j):
                c0, m = KEY_CHUNKS[j]
                if j == 0:
                    if b.i is not None or ahead:
                        dve.wait_ge(*at(L, "split", b.n(3, 3 * ahead)))
                dve.wait_ge(*at(L, "k", n + 1))
                src, dst = PS[:, 6, 0:m], CB["kf"][:, c0:c0 + m]
                if masked:
                    ins = dve.scalar_tensor_tensor(dst, src, wcol(f"{L}_b", 1), CB["m01"][:, c0:c0 + m], ALU.add, ALU.mult)
                else:
                    ins = dve.tensor_copy(dst, src)
                ins.then_inc(of(L, "kf"), 1)

            def value_piece(b, ahead, n, j):
                dve.wait_ge(*at(L, "k", n + 1))
                for t, m, rows in ((4 * j, 4, 128),) if j < 2 else ((8, 3, 128), (11, 1, KT_TILES[-1][1])):
                    src = PS[0:rows, 6, (t % 4) * 128:(t % 4 + m) * 128].rearrange("p (t h d) -> p t h d", t=m, h=H)
                    dst = CB["v"][b.buf(ahead)][0:rows, t:t + m, :, 0:DH]
                    if has_bias:
                        bv = w(f"{L}_bv", rows).rearrange("p (h d) -> p h d", h=H).unsqueeze(1).to_broadcast([rows, m, H, DH])
                        ins = dve.tensor_tensor(dst, src, bv, ALU.add)
                    else:
                        ins = dve.tensor_copy(dst, src)
                ins.then_inc(of(L, "kf"), 1)

            def split_maxima(b, ahead, n, j):
                dve.wait_ge(*at(L, "k", n + 1))
                mc, neg, src = CB["mc"][j][0:8], CB["neg"][0:8], PS[0:8, 6, 0:S]
                base = 2 * ahead + j
                done = lambda m: dve.wait_ge(*at(L, "mlink", b.n(2 * links, base * links + m)))
                dve.tensor_copy(mc[:, 0, :], src).then_inc(chain, 1)
                done(1)
                dve.tensor_tensor(neg, src, mc[:, 0, :], ALU.subtract).then_inc(chain, 1)
                done(2)
                dve.sem_inc(of(L, "kf"), 1)
                dve.tensor_copy(mc[:, 1, :], neg).then_inc(chain, 1)
                done(3)
                dve.tensor_tensor(mc[:, 2, :], neg, mc[:, 1, :], ALU.subtract).then_inc(chain, 1)
                done(4)
                dve.sem_inc(of(L, "mxs"), 1)

            def maximum(b, ahead, h, first=0):
                parts = CB["mx3"][b.buf(ahead)][0:S]
                for j, (c0, m) in enumerate(KEY_CHUNKS):
                    dve.wait_ge(*at(L, "scores", b.n(3 * H, 3 * (H * ahead + h) + j + 1)))
                    dve.tensor_reduce(parts[:, h, j:j + 1], PSF[0:S, CHUNK * first + c0:CHUNK * first + c0 + m], AX, ALU.max) \
                        .then_inc(of(L, "nm"), 1)
                if h % 8 == 7:
                    dve.wait_ge(*at(L, "nm", b.n(3 * H, 3 * (H * ahead + h + 1))))
                    dve.tensor_reduce(CB["mx"][b.buf(ahead)][0:S, h - 7:h + 1], parts[:, h - 7:h + 1, :], AX, ALU.max, negate=True) \
                        .then_inc(of(L, "joined"), 1)

            x_ready(dve, c, 1)
            dve.memset(CB["ones"], 1.0).then_inc(of(L, "vzero"), 1)
            for k in range(2):
                dve.memset(CB["qq"][k][MASK_ROW:128], 1.0 if masked else 0.0)
                dve.memset(CB["v"][k][:, :, :, DH:VW].rearrange("p t h d -> p (t h) d"), 1.0)
            dve.memset(PS[:, 7, 0:4 * S], 0.0).then_inc(of(L, "vzero"), 1)
            loaded(dve, f"{L}_wq")
            for h in range(2):
                dve.wait_ge(*at(L, "q", h + 1))
                dve.tensor_scalar(half(CB["q"], h), bank(h), wcol(f"{L}_b", 0) if has_bias else 0.0, scale,
                                  ALU.add, ALU.mult).then_inc(of(L, "qlink"), 1)
            loaded(dve, "parity")
            by_batch = lambda a: a.rearrange("p (b n) -> p b n", b=NB)
            part = CB["kp"][:, 0, 0:T]
            for j in range(3):
                dve.wait_ge(*at(L, "qlink", 2 + 2 * j))
                dve.tensor_copy(part, CB["q"]).then_inc(of(L, "qlink"), 1)
                dve.wait_ge(*at(L, "qlink", 3 + 2 * j))
                for e in range(2):
                    ins = dve.tensor_scalar(CB["qp"][:, j, :, e, :], by_batch(part), wcol("parity", e), None, ALU.mult)
                ins.then_inc(of(L, "qf"), 1)
                dve.wait_ge(*at(L, "qf", j + 1))
                dve.tensor_tensor(CB["q"], CB["q"], part, ALU.subtract).then_inc(of(L, "qlink"), 1)
            dve.sem_inc(of(L, "o"), 1)
            dve.wait_ge(*at(L, "qlink", 8))
            zero = Step(0)
            for ahead in range(2):
                if masked:
                    mask(zero, ahead)
                for j in range(3):
                    key_piece(zero, ahead, 3 * ahead + j, j)
                if not ahead:
                    dve.wait_ge(*at(L, "split_act", 3))
                    dve.tensor_tensor(CB["kf"], CB["kf"], CB["kp"][:, 0, :], ALU.subtract).then_inc(of(L, "split"), 1)
                    dve.wait_ge(*at(L, "split", 2))
                    dve.tensor_tensor(CB["kp"][:, 2, :], CB["kf"], CB["kp"][:, 1, :], ALU.subtract).then_inc(of(L, "split"), 1)
            for j in range(3):
                value_piece(zero, 0, 6 + j, j)
            for h in range(H):
                maximum(zero, 0, h, 3 * (h % 2))
                if h == 9:
                    split_maxima(zero, 0, 9, 0)

            def body(b, following, more):
                n = b.piece
                for h in range(H):
                    if following:
                        maximum(b, 1, h)
                    if h == 1:
                        split_maxima(b, 0, n(0), 1)
                        if more and masked:
                            mask(b, 2)
                    if more and 2 <= h <= 4:
                        key_piece(b, 2, n(h - 1), h - 2)
                    if following:
                        if h == 9:
                            split_maxima(b, 1, n(4), 0)
                        if 10 <= h <= 12:
                            value_piece(b, 1, n(h - 5), h - 10)
                dve.wait_ge(*at(L, "pv", b.n(H, H + 2)))
                dve.tensor_copy(CB["o"][:, :, bass.ds(b.n(S), S)], PS[:, 7, 0:4 * S].rearrange("p (g s) -> p g s", g=4)) \
                    .then_inc(of(L, "o"), 1)

            steps(dve, body)
            for g in range(4):
                for h in range(2):
                    n = 2 * g + h
                    dve.wait_ge(*at(L, "rd", 8 + n + 1))
                    o = CB["o"][:, g, h * HALF:(h + 1) * HALF]
                    dve.tensor_tensor(o, o, CB["rd"][:, n, :], ALU.mult).then_inc(of(L, "normed"), 1)
            residual(dve, c + 1, lambda h: dve.wait_ge(*at(L, "y", h + 1)), bank,
                     wcol(f"{L}_b", 2 if has_bias else 0))

        OTHER_SYNC, OTHER_POOL, OTHER_ACT, OTHER_DVE, OTHER_PE = {}, {}, {}, {}, {}

        def moe_buffers(E, width):
            lay = Layout()
            return dict(
                x=lay.take(T), lg=lay.take(NB, 2 * E if E > 8 else E + 8), tmp=lay.take(NB, E), pr=lay.take(NB, E),
                best=lay.take(NB, 8), mv=lay.take(NB, 8), rep=lay.take(NB, 2 * E if E > 8 else E + 8),
                den=lay.take(NB), rd=lay.take(NB), gt=lay.take(T),
                a=[lay.take(HALF) for _ in range(2)], s=[lay.take(HALF) for _ in range(2)],
                lin=[lay.take(HALF) for _ in range(2)], w=[lay.take(width) for _ in range(2)])

        MOE = {"f0": (E0, K0, EXPERT0, moe_buffers(E0, EXPERT0)), "f3": (E3, K3, EXPERT3, moe_buffers(E3, EXPERT3))}

        def moe_sync(sp, L, c):
            E, _, width, B = MOE[L]
            x_ready(sp, c, 1)
            src = expert0_in if L == "f0" else expert3_in
            with sp.Fori(0, E // 2) as i:
                for k in range(2):
                    sp.wait_ge(*at(L, "y_done", i * 4 + (2 * k + 1)))
                    sp.dma_start(B["w"][k], src[:, bass.ds(i * (2 * width) + k * width, width)]) \
                        .then_inc(of(L, f"w{k}"), 16)

        def moe_pe(pe, L, c):
            E, _, width, B = MOE[L]
            w2 = 128 if L == "f0" else 256
            loaded(pe, f"{L}_wg")
            x = X if L == "f0" else B["x"]
            if L == "f3":
                for h in range(2):
                    pe.wait_ge(*at(L, "sq", h + 1))
                    pe.matmul(bank(6 + h), mean_w[:, :], half(SQ, h), start=True, stop=True).then_inc(of(L, "ms"), 1)
                pe.wait_ge(*at(L, "x", 2))
            else:
                x_ready(pe, c, 0)
                x_ready(pe, c, 1)
            for b in range(NB):
                mm = pe.matmul(PS[0:S, 0, b * E:(b + 1) * E], x[:, b * S:(b + 1) * S], w(f"{L}_wg"), start=True, stop=True)
            mm.then_inc(of(L, "logits"), 1)
            pe.wait_ge(*at(L, "gates", 1))
            for b in range(NB):
                mm = pe.transpose(PS[0:E, 2 + b // 4, (b % 4) * S:(b % 4 + 1) * S], B["pr"][0:S, b, :], ident[0:S, 0:S])
            mm.then_inc(of(L, "gt"), 1)
            pe.wait_ge(*at(L, "gtc", 1))
            for h in range(2):
                pe.matmul(bank(h), w(f"{L}_b2", E), half(B["gt"][0:E], h), start=True, stop=False, skip_group_check=True)
            pe.sem_inc(of(L, "y_done"), 3)
            with pe.Fori(0, E // 2) as i:
                def second(j):
                    pe.wait_ge(*at(L, "act", i * 4 + (j + 3)))
                    pe.matmul(bank(j % 2), B["w"][j // 2][:, w2:w2 + 128], B["a"][j % 2], start=False, stop=False, skip_group_check=True) \
                        .then_inc(of(L, "y_done"), 1)

                for j in range(4):
                    wk = B["w"][j // 2]
                    if j % 2 == 0:
                        pe.wait_ge(*at(L, f"w{j // 2}", i * 16 + 16))
                    pe.wait_ge(*at(L, "up", i * 4 + (j + 1)))
                    if L == "f3":
                        pe.matmul(bank(6 + j % 2), wk[:, 128:256], half(x, j % 2), start=True, stop=True)
                    pe.matmul(bank(2 + j % 2), wk[:, 0:128], half(x, j % 2), start=True, stop=True) \
                        .then_inc(of(L, "h"), 1)
                    pe.wait_ge(*at(L, "act", i * 4 + (j + 1)))
                    sel = wk[:, w2 + 128:w2 + 256]
                    pe.matmul(bank(4 + j % 2), sel, half(B["gt"], j % 2), start=True, stop=True) \
                        .then_inc(of(L, "bc"), 1)
                    if j:
                        second(j - 1)
                second(3)
            pe.wait_ge(*at(L, "y_done", 3 + 2 * E))
            pe.sem_inc(of(L, "y"), 1)
            norm_pe(pe, c + 1)

        def moe_pool(pool, L, c):
            E, _, width, B = MOE[L]
            if L == "f3":
                with pool.Fori(0, E // 2) as i:
                    for j in range(4):
                        pool.wait_ge(*at(L, "sig", i * 4 + (j + 1)))
                        pool.tensor_tensor(B["s"][j % 2], B["s"][j % 2], B["a"][j % 2], ALU.mult).then_inc(of(L, "glu"), 1)

        def moe_act(act, L, c):
            E, _, width, B = MOE[L]
            if L == "f3":
                for h in range(2):
                    x_ready(act, c, h)
                    act.activation(half(SQ, h), half(X, h), ACT.Square).then_inc(of(L, "sq"), 1)
                for h in range(2):
                    act.wait_ge(*at(L, "ms", h + 1))
                    act.activation(half(SQ, h), bank(6 + h), ACT.Ln, bias=epsc[:, :]).then_inc(of(L, "rms"), 1)
                for h in range(2):
                    act.wait_ge(*at(L, "rms", h + 1))
                    act.activation(half(SQ, h), half(SQ, h), ACT.Exp, scale=-0.5).then_inc(of(L, "rms"), 1)
            act.wait_ge(*at(L, "sub", 1))
            act.activation(B["tmp"][0:S], B["tmp"][0:S], ACT.Exp).then_inc(of(L, "exp"), 1)
            if L == "f0":
                act.sem_inc(of(L, "up"), 2)
            with act.Fori(0, E // 2) as i:
                for j in range(4):
                    if L == "f0":
                        act.wait_ge(*at(L, "h", i * 4 + (j + 1)))
                        act.wait_ge(*at(L, "y_done", i * 4 + (j + 2)))
                        act.activation(B["a"][j % 2], bank(2 + j % 2), ACT.Gelu, bias=B["w"][j // 2][:, width - 1:width]) \
                            .then_inc(of(L, "up"), 1)
                    else:
                        act.wait_ge(*at(L, "glu_in", i * 4 + (j + 1)))
                        act.activation(B["s"][j % 2], B["a"][j % 2], ACT.Sigmoid, scale=1.702).then_inc(of(L, "sig"), 1)
            norm_act(act, c + 1)

        def moe_dve(dve, L, c):
            E, K, width, B = MOE[L]
            chain, n = of(L, "chain"), [0]

            def link(ins):
                n[0] += 1
                ins.then_inc(chain, 1)
                dve.wait_ge(*at(L, "chain", n[0]))

            x_ready(dve, c, 1)
            link(dve.memset(B["gt"], 0.0))
            if L == "f3":
                for h in range(2):
                    dve.wait_ge(*at(L, "rms", h + 3))
                    dve.scalar_tensor_tensor(half(B["x"], h), half(X, h), wcol("f3_scale"), half(SQ, h), ALU.mult, ALU.mult) \
                        .then_inc(of(L, "x"), 1)
            link(dve.memset(B["lg"][0:S], -BIG))
            link(dve.memset(B["mv"][0:S], -BIG))
            dve.wait_ge(*at(L, "logits", 1))
            lg, tmp, pr = B["lg"][0:S, :, 0:E], B["tmp"][0:S], B["pr"][0:S]
            ps = PS[0:S, 0, 0:NB * E].rearrange("p (b e) -> p b e", b=NB)
            wide = lambda a, m: a.unsqueeze(2).to_broadcast([S, NB, m])
            den, rd = B["den"][0:S], B["rd"][0:S]
            if L == "f0":
                link(dve.tensor_reduce(den, ps, AX, ALU.max))
                dve.tensor_tensor(tmp, ps, wide(den, E), ALU.subtract).then_inc(of(L, "sub"), 1)
                dve.wait_ge(*at(L, "exp", 1))
                link(dve.tensor_reduce(den, tmp, AX, ALU.add))
                link(dve.reciprocal(rd, den))
                link(dve.tensor_tensor(lg, tmp, wide(rd, E), ALU.mult))
            else:
                link(dve.tensor_tensor(lg, ps, w("f3_bg", S).unsqueeze(1).to_broadcast([S, NB, E]), ALU.add))
            for b in range(NB):
                ins = dve.max(B["best"][0:S, b, :], B["lg"][0:S, b, :])
                if b < NB - 1:
                    ins.then_inc(of(L, "each"), 1)
            link(ins)
            dve.wait_ge(*at(L, "each", NB - 1))
            link(dve.tensor_copy(B["mv"][0:S, :, 0:K], B["best"][0:S, :, 0:K]))
            for b in range(NB):
                ins = dve.match_replace(B["rep"][0:S, b, :], B["mv"][0:S, b, :], B["lg"][0:S, b, :], -BIG)
                if b < NB - 1:
                    ins.then_inc(of(L, "each"), 1)
            link(ins)
            dve.wait_ge(*at(L, "each", 2 * (NB - 1)))
            if L == "f0":
                link(dve.scalar_tensor_tensor(pr, B["rep"][0:S, :, 0:E], -BIG, lg, ALU.is_le, ALU.mult))
                link(dve.tensor_tensor(den, B["best"][0:S, :, 0], B["best"][0:S, :, 1], ALU.add))
                link(dve.tensor_scalar(den, den, 1e-6, None, ALU.add))
            else:
                dve.tensor_tensor(tmp, lg, wide(B["best"][0:S, :, 0], E), ALU.subtract).then_inc(of(L, "sub"), 1)
                dve.wait_ge(*at(L, "exp", 1))
                link(dve.scalar_tensor_tensor(pr, B["rep"][0:S, :, 0:E], -BIG, tmp, ALU.is_le, ALU.mult))
                link(dve.tensor_reduce(den, pr, AX, ALU.add))
            link(dve.reciprocal(rd, den))
            dve.tensor_tensor(pr, pr, wide(rd, E), ALU.mult).then_inc(of(L, "gates"), 1)
            dve.wait_ge(*at(L, "gt", 1))
            dve.tensor_copy(B["gt"][0:E].rearrange("p (a s) -> p a s", a=2), PS[0:E, 2:4, 0:HALF]).then_inc(of(L, "gtc"), 1)
            dve.sem_inc(of(L, "act"), 2)
            if L == "f3":
                dve.sem_inc(of(L, "up"), 2)
            with dve.Fori(0, E // 2) as i:
                def gate(j):
                    if L == "f0":
                        dve.wait_ge(*at(L, "bc", i * 4 + (j + 1)))
                        dve.wait_ge(*at(L, "up", i * 4 + (j + 3)))
                        dve.tensor_tensor(B["a"][j % 2], B["a"][j % 2], bank(4 + j % 2), ALU.mult).then_inc(of(L, "act"), 1)
                    else:
                        dve.wait_ge(*at(L, "glu", i * 4 + (j + 1)))
                        dve.wait_ge(*at(L, "lin", i * 8 + (2 * j + 2)))
                        dve.tensor_tensor(B["a"][j % 2], B["s"][j % 2], B["lin"][j % 2], ALU.mult).then_inc(of(L, "act"), 1)

                for j in range(4):
                    if L == "f3":
                        b1 = B["w"][j // 2][:, width - 2:width - 1]
                        b1l = B["w"][j // 2][:, width - 1:width]
                        lin = B["lin"][j % 2]
                        if j:
                            gate(j - 1)
                        dve.wait_ge(*at(L, "h", i * 4 + (j + 1)))
                        dve.wait_ge(*at(L, "y_done", i * 4 + (j + 2)))
                        dve.tensor_scalar(B["a"][j % 2], bank(2 + j % 2), b1, 7.0, ALU.add, ALU.min) \
                            .then_inc(of(L, "glu_in"), 1)
                        dve.tensor_scalar(lin, bank(6 + j % 2), b1l, 7.0, ALU.add, ALU.max).then_inc(of(L, "up"), 1)
                        dve.wait_ge(*at(L, "up", i * 4 + (j + 3)))
                        dve.tensor_scalar(lin, lin, 7.0, 1.0, ALU.min, ALU.add).then_inc(of(L, "lin"), 1)
                        dve.wait_ge(*at(L, "bc", i * 4 + (j + 1)))
                        dve.wait_ge(*at(L, "lin", i * 8 + (2 * j + 1)))
                        dve.tensor_tensor(lin, lin, bank(4 + j % 2), ALU.mult).then_inc(of(L, "lin"), 1)
                    else:
                        gate(j)
                if L == "f3":
                    gate(3)
            assert L == "f3" or n[0] == F0_CHAIN, n
            if L == "f0":
                residual(dve, c + 1, lambda h: dve.wait_ge(*at(L, "y", 1)), bank)
            else:
                norm_dve(dve, c + 1, lambda h: (dve.wait_ge(*at(L, "y", 1)),
                                                dve.scalar_tensor_tensor(half(R, h), half(X, h), 2.0, bank(h), ALU.mult, ALU.add))[1])

        OTHER_SYNC, OTHER_POOL, OTHER_ACT, OTHER_DVE, OTHER_PE = {}, {}, {}, {}, {}

        NST, PAD = 16, 3

        def m1_buffers():
            lay = Layout()
            return dict(
                n=lay.take(T), xcp=lay.take(2, NB, S + PAD), xc=lay.take(2, T), z=lay.take(2, T), dbc=lay.take(T),
                u=lay.take(2, T), dtn=lay.take(2, T), aexp=lay.take(2, NST), y=lay.take(2, T), xm=lay.take(T),
                f=lay.take(2, T), t=[lay.take(2, T) for _ in range(4)],
                da=[lay.take(T) for _ in range(2)], dbx=[lay.take(T) for _ in range(2)],
                h=[lay.take(T) for _ in range(2)], hc=[lay.take(T) for _ in range(2)])

        MB = m1_buffers()

        def hcol(a, j, h):
            return a[:, j, h * HALF:(h + 1) * HALF]

        def m1_pe(pe):
            loaded(pe, "m_in")
            norm_pe(pe, C_M1)
            for h in range(2):
                x_ready(pe, C_M1, h)
                for j in range(4):
                    pe.matmul(bank(2 * j + h), w("m_in")[:, 128 * j:128 * j + 128], half(MB["n"], h), start=True, stop=True) \
                        .then_inc(sem("m_xz"), 1)
            pe.wait_ge(sem("m_xc"), 2)
            pe.wait_ge(sem("m_z"), 4)
            for h in range(2):
                for j in range(2):
                    mm = pe.matmul(PS[0:40, h, 0:HALF], w("m_xp")[:, 40 * j:40 * j + 40], hcol(MB["xc"], j, h),
                                   start=(j == 0), stop=(j == 1))
                mm.then_inc(sem("m_dbc"), 1)
            pe.wait_ge(sem("m_dbcf"), 2)
            for j in range(2):
                for h in range(2):
                    pe.matmul(bank(2 + 2 * j + h), w("m_dtw", 40)[:, 128 * j:128 * j + 128], half(MB["dbc"][0:40], h),
                              start=True, stop=True).then_inc(sem("m_dt"), 1)
            pe.wait_ge(sem("m_dtb_added"), 4)
            sel = w("m_sel", 40).rearrange("p (n c m) -> p n c m", n=NST, c=2)
            for n in range(NST):
                if n >= 2:
                    pe.wait_ge(sem("m_hc"), 2 * n - 2)
                for part in range(2):
                    for h in range(2):
                        mm = pe.matmul(bank(4 * (n % 2) + 2 * part + h), sel[:, n, part, :], half(MB["dbc"][0:40], h),
                                       start=True, stop=True)
                mm.then_inc(sem("m_bc"), 1)
            pe.wait_ge(sem("m_gated"), 2)
            for h in range(2):
                for j in range(2):
                    mm = pe.matmul(bank(h), w("m_out")[:, 128 * j:128 * j + 128], hcol(MB["y"], j, h), start=(j == 0), stop=(j == 1))
                mm.then_inc(sem("m_o"), 1)
            norm_pe(pe, C_M2)
            for h in range(2):
                x_ready(pe, C_M2, h)
                for j in range(2):
                    pe.matmul(bank(2 * j + h), w("m_w1")[:, 128 * j:128 * j + 128], half(MB["n"], h), start=True, stop=True) \
                        .then_inc(sem("m_xz"), 1)
            for h in range(2):
                pe.wait_ge(sem("m_z"), 4 + 2 * h + 2)
                for j in range(2):
                    mm = pe.matmul(bank(4 + h), w("m_w2")[:, 128 * j:128 * j + 128], hcol(MB["f"], j, h), start=(j == 0), stop=(j == 1))
                mm.then_inc(sem("m_o"), 1)
            norm_pe(pe, C_M)

        def m1_pool(pool):
            x_ready(pool, C_F0, 1)
            pool.memset(MB["xcp"][:, :, :, 0:PAD].rearrange("p a b s -> p (a b) s"), 0.0).then_inc(sem("m_pad"), 1)
            for n in range(NST):
                for j in range(2):
                    m = 2 * n + j
                    pool.wait_ge(sem("m_da"), m + 1)
                    pool.memset(MB["da"][j].rearrange("p (b s) -> p b s", b=NB)[:, :, 0:1], 0.0).then_inc(sem("m_cut"), 1)
                for j in range(2):
                    m = 2 * n + j
                    pool.wait_ge(sem("m_hc"), m + 1)
                    if n == 0:
                        pool.tensor_copy(MB["y"][:, j, :], MB["hc"][j]).then_inc(sem("m_sum"), 1)
                    else:
                        pool.wait_ge(sem("m_sum"), m - 1)
                        pool.tensor_tensor(MB["y"][:, j, :], MB["y"][:, j, :], MB["hc"][j], ALU.add).then_inc(sem("m_sum"), 1)

        def m1_act(act):
            loaded(act, "m_in")
            norm_act(act, C_M1)
            act.activation(MB["aexp"].rearrange("p a b -> p (a b)"), w("m_alog"), ACT.Exp).then_inc(sem("m_aexp"), 1)
            for j in range(2):
                for h in range(2):
                    act.wait_ge(sem("m_xz"), 4 * h + j + 3)
                    act.activation(hcol(MB["z"], j, h), bank(4 + 2 * j + h), ACT.Silu).then_inc(sem("m_z"), 1)
            for j in range(2):
                act.wait_ge(sem("m_conv"), 4 * (j + 1))
                act.activation(MB["xc"][:, j, :], MB["t"][0][:, j, :], ACT.Silu, bias=wcol("m_conv", 5 * j + 4)) \
                    .then_inc(sem("m_xc"), 1)
            for h in range(2):
                act.wait_ge(sem("m_dbc"), h + 1)
                act.activation(half(MB["dbc"][0:40], h), PS[0:40, h, 0:HALF], ACT.Copy).then_inc(sem("m_dbcf"), 1)
            act.wait_ge(sem("m_dtb_added"), 4)
            act.activation(MB["t"][1], MB["t"][0], ACT.Abs).then_inc(sem("m_e"), 1)
            act.wait_ge(sem("m_e"), 1)
            act.activation(MB["t"][1], MB["t"][1], ACT.Exp, scale=-1.0).then_inc(sem("m_e"), 1)
            act.wait_ge(sem("m_sp"), 1)
            act.activation(MB["t"][3], MB["t"][2], ACT.Ln).then_inc(sem("m_ln"), 1)
            act.wait_ge(sem("m_sp"), 4)
            act.activation(MB["t"][2], MB["t"][2], ACT.Ln).then_inc(sem("m_ln"), 1)
            act.wait_ge(sem("m_ln"), 2)
            act.activation(MB["t"][2], MB["t"][2], ACT.Exp, scale=-1.0).then_inc(sem("m_ln"), 1)
            act.wait_ge(sem("m_dtn"), 2)
            act.wait_ge(sem("m_aexp"), 1)
            for n in range(NST):
                for j in range(2):
                    m = 2 * n + j
                    if m >= 2:
                        act.wait_ge(sem("m_scan"), m - 1)
                    act.activation(MB["da"][j], MB["dtn"][:, j, :], ACT.Exp, scale=MB["aexp"][:, j, n:n + 1]) \
                        .then_inc(sem("m_da"), 1)
            norm_act(act, C_M2)
            for h in range(2):
                for j in range(2):
                    act.wait_ge(sem("m_xz"), 8 + 2 * h + j + 1)
                    act.activation(hcol(MB["f"], j, h), bank(2 * j + h), ACT.Gelu, bias=wcol("m_b1", j)).then_inc(sem("m_z"), 1)
            norm_act(act, C_M)

        def m1_dve(dve):
            loaded(dve, "m_in")
            rows = lambda h: (x_ready(dve, C_F0, h), dve.tensor_copy(half(R, h), half(X, h)))[1]
            norm_dve(dve, C_M1, rows, MB["n"], (wcol("m_ln1", 0), wcol("m_ln1", 1)))
            t = MB["t"]
            for h in range(2):
                for j in range(2):
                    dve.wait_ge(sem("m_xz"), 4 * h + j + 1)
                    dve.tensor_copy(MB["xcp"][:, j, 4 * h:4 * h + 4, PAD:], bank(2 * j + h).rearrange("p (b s) -> p b s", b=4)) \
                        .then_inc(sem("m_xcp"), 1)
            dve.wait_ge(sem("m_xcp"), 4)
            dve.wait_ge(sem("m_pad"), 1)
            for j in range(2):
                acc = t[0][:, j, :].rearrange("p (b s) -> p b s", b=NB)
                for k in range(4):
                    src, tap = MB["xcp"][:, j, :, k:k + S], wcol("m_conv", 5 * j + k)
                    if k == 0:
                        dve.tensor_scalar(acc, src, tap, None, ALU.mult).then_inc(sem("m_conv"), 1)
                    else:
                        dve.wait_ge(sem("m_conv"), 4 * j + k)
                        dve.scalar_tensor_tensor(acc, src, tap, acc, ALU.mult, ALU.add).then_inc(sem("m_conv"), 1)
            dve.wait_ge(sem("m_xc"), 2)
            for j in range(2):
                for h in range(2):
                    dve.wait_ge(sem("m_dt"), 2 * j + h + 1)
                    dve.tensor_scalar(hcol(t[0], j, h), bank(2 + 2 * j + h), wcol("m_dtb", j), None, ALU.add) \
                        .then_inc(sem("m_dtb_added"), 1)
            step, s = sem("m_sp"), [0]

            def link(ins):
                s[0] += 1
                ins.then_inc(step, 1)
                dve.wait_ge(step, s[0])

            dve.wait_ge(sem("m_e"), 2)
            link(dve.tensor_scalar(t[2], t[1], 1.0, None, ALU.add))
            dve.wait_ge(sem("m_ln"), 1)
            link(dve.tensor_scalar(t[2], t[2], -1.0, None, ALU.add))
            link(dve.tensor_scalar(MB["u"], t[2], 0.0, None, ALU.is_equal))
            link(dve.tensor_tensor(t[2], t[2], MB["u"], ALU.add))
            dve.wait_ge(sem("m_ln"), 3)
            link(dve.tensor_tensor(t[3], t[3], t[2], ALU.mult))
            link(dve.tensor_tensor(t[3], t[3], MB["u"], ALU.add))
            link(dve.tensor_tensor(t[3], t[3], t[1], ALU.mult))
            link(dve.scalar_tensor_tensor(t[3], t[0], 0.0, t[3], ALU.max, ALU.add))
            dve.tensor_scalar(MB["dtn"], t[3], -1.0, None, ALU.mult).then_inc(sem("m_dtn"), 1)
            dve.tensor_tensor(MB["u"], t[3], MB["xc"], ALU.mult).then_inc(sem("m_dtn"), 1)
            dve.wait_ge(sem("m_dtn"), 2)
            pair = lambda a: a.rearrange("p (a s) -> p a s", a=2)
            for n in range(NST):
                for j in range(2):
                    m = 2 * n + j
                    dve.wait_ge(sem("m_bc"), n + 1)
                    dve.tensor_tensor(pair(MB["dbx"][j]), pair(MB["u"][:, j, :]), PS[:, 4 * (n % 2):4 * (n % 2) + 2, 0:HALF], ALU.mult) \
                        .then_inc(sem("m_dbx"), 1)
                for j in range(2):
                    m = 2 * n + j
                    dve.wait_ge(sem("m_dbx"), 2 * n + j + 1)
                    dve.wait_ge(sem("m_cut"), m + 1)
                    dve.tensor_tensor_scan(MB["h"][j], MB["da"][j], MB["dbx"][j], 0.0, ALU.mult, ALU.add).then_inc(sem("m_scan"), 1)
                for j in range(2):
                    m = 2 * n + j
                    dve.wait_ge(sem("m_scan"), m + 1)
                    if m >= 2:
                        dve.wait_ge(sem("m_sum"), m - 1)
                    dve.tensor_tensor(pair(MB["hc"][j]), pair(MB["h"][j]), PS[:, 4 * (n % 2) + 2:4 * (n % 2) + 4, 0:HALF], ALU.mult) \
                        .then_inc(sem("m_hc"), 1)
            for j in range(2):
                dve.wait_ge(sem("m_sum"), 2 * NST - 1 + j)
                y = MB["y"][:, j, :]
                dve.scalar_tensor_tensor(y, MB["xc"][:, j, :], wcol("m_d", j), y, ALU.mult, ALU.add).then_inc(sem("m_skip"), 1)
                dve.wait_ge(sem("m_skip"), j + 1)
                dve.wait_ge(sem("m_z"), 4)
                dve.tensor_tensor(y, y, MB["z"][:, j, :], ALU.mult).then_inc(sem("m_gated"), 1)

            def rows2(h):
                dve.wait_ge(sem("m_o"), h + 1)
                dve.tensor_tensor(half(MB["xm"], h), bank(h), half(X, h), ALU.add).then_inc(sem("m_xm"), 1)
                dve.wait_ge(sem("m_xm"), h + 1)
                return dve.tensor_copy(half(R, h), half(MB["xm"], h))

            norm_dve(dve, C_M2, rows2, MB["n"], (wcol("m_ln2", 0), wcol("m_ln2", 1)))

            def rows3(h):
                dve.wait_ge(sem("m_o"), h + 3)
                dve.scalar_tensor_tensor(half(R, h), bank(4 + h), wcol("m_b2"), half(MB["xm"], h), ALU.add, ALU.add) \
                    .then_inc(sem("m_xm"), 1)
                dve.wait_ge(sem("m_xm"), h + 3)
                return dve.tensor_tensor(half(R, h), half(R, h), half(X, h), ALU.add)

            norm_dve(dve, C_M, rows3)

        OTHER_PE["m1"], OTHER_POOL["m1"], OTHER_ACT["m1"], OTHER_DVE["m1"] = m1_pe, m1_pool, m1_act, m1_dve

        def x1_buffers():
            lay = Layout()
            return dict(q=lay.take(T), y=lay.take(T), ctx=lay.take(CTX), k=lay.take(CTX), v=lay.take(NT, 128),
                        pt=lay.take(NT, S), ones=lay.take(128), rd=lay.take(S))

        XB = x1_buffers()
        LAST = KT_TILES[-1][1]

        def x1_sync(sp):
            x_ready(sp, C_M, 1)
            with sp.Fori(0, NB) as i:
                sp.wait_ge(*at("x1", "ctx_used", i + 1))
                sp.dma_start(XB["ctx"], ctx_in[:, bass.ds(i * CTX, CTX)]).then_inc(of("x1", "ctx"), 16)

        def x1_pe(pe):
            loaded(pe, "x1_wq")
            for h in range(2):
                x_ready(pe, C_M, h)
                pe.matmul(bank(h), w("x1_wq"), half(X, h), start=True, stop=True).then_inc(of("x1", "q"), 1)
            pe.sem_inc(of("x1", "ctx_used"), 1)
            pe.wait_ge(*at("x1", "qf", 2))
            with pe.Fori(0, NB) as i:
                pe.wait_ge(*at("x1", "ctx", i * 16 + 16))
                pe.wait_ge(*at("x1", "exp", i * 4 + 1))
                for c0, n in KEY_CHUNKS:
                    pe.matmul(PSF[:, c0:c0 + n], w("x1_wk"), XB["ctx"][:, c0:c0 + n], start=True, stop=True) \
                        .then_inc(of("x1", "k"), 1)
                for t, (t0, n) in enumerate(KT_TILES):
                    mm = pe.matmul(PS[0:n, 3 + t // 4, (t % 4) * 128:(t % 4) * 128 + 128], XB["ctx"][:, t0:t0 + n],
                                   w("x1_wv"), start=True, stop=True)
                    if t % 4 == 3:
                        mm.then_inc(of("x1", "v"), 1)
                pe.wait_ge(*at("x1", "v", i * 3 + 3))
                pe.sem_inc(of("x1", "ctx_used"), 1)
                pe.wait_ge(*at("x1", "kf", i * 3 + 3))
                for t, (t0, n) in enumerate(KT_TILES):
                    mm = pe.matmul(PS[0:n, t // 4, (t % 4) * S:(t % 4 + 1) * S], XB["k"][:, t0:t0 + n],
                                   XB["q"][:, bass.ds(i * S, S)], start=True, stop=True)
                    if t % 4 == 3:
                        mm.then_inc(of("x1", "scores"), 1)
                pe.wait_ge(*at("x1", "vp", i * 4 + 4))
                pe.wait_ge(*at("x1", "exp", i * 4 + 5))
                pe.wait_ge(*at("x1", "o", i + 1))
                for t, (t0, n) in enumerate(KT_TILES):
                    pe.matmul(PS[:, 6, 0:S], XB["v"][0:n, t, :], XB["pt"][0:n, t, :], start=(t == 0), stop=(t == NT - 1))
                for t, (t0, n) in enumerate(KT_TILES):
                    mm = pe.matmul(PS[:, 7, 0:S], XB["ones"][0:n, :], XB["pt"][0:n, t, :], start=(t == 0), stop=(t == NT - 1))
                mm.then_inc(of("x1", "pv"), 1)
            norm_pe(pe, C_X1)

        def x1_act(act):
            for h in range(2):
                act.wait_ge(*at("x1", "q", h + 1))
                act.activation(half(XB["q"], h), bank(h), ACT.Copy).then_inc(of("x1", "qf"), 1)
            act.sem_inc(of("x1", "exp"), 1)
            with act.Fori(0, NB) as i:
                for j, (c0, n) in enumerate(KEY_CHUNKS):
                    act.wait_ge(*at("x1", "k", i * 3 + (j + 1)))
                    act.activation(XB["k"][:, c0:c0 + n], PSF[:, c0:c0 + n], ACT.Copy).then_inc(of("x1", "kf"), 1)
                for j in range(3):
                    act.wait_ge(*at("x1", "scores", i * 3 + (j + 1)))
                    for t, m, rows in ((4 * j, 4, 128),) if j < 2 else ((8, 3, 128), (11, 1, LAST)):
                        act.activation(XB["pt"][0:rows, t:t + m, :].rearrange("p t s -> p (t s)"),
                                       PS[0:rows, j, (t % 4) * S:(t % 4 + m) * S], ACT.Exp, scale=D ** -0.5) \
                            .then_inc(of("x1", "exp"), 1)
            norm_act(act, C_X1)

        def x1_dve(dve):
            x_ready(dve, C_M, 1)
            dve.memset(XB["ones"], 1.0).then_inc(of("x1", "vzero"), 1)
            dve.wait_ge(*at("x1", "vzero", 1))
            dve.sem_inc(of("x1", "o"), 1)
            with dve.Fori(0, NB) as i:
                for j in range(3):
                    dve.wait_ge(*at("x1", "v", i * 3 + (j + 1)))
                    for t, m, rows in ((4 * j, 4, 128),) if j < 2 else ((8, 3, 128), (11, 1, LAST)):
                        dve.tensor_copy(XB["v"][0:rows, t:t + m, :].rearrange("p t d -> p (t d)"),
                                        PS[0:rows, 3 + j, (t % 4) * 128:(t % 4 + m) * 128]).then_inc(of("x1", "vp"), 1)
                dve.wait_ge(*at("x1", "pv", i + 1))
                dve.reciprocal(XB["rd"], PS[:, 7, 0:S]).then_inc(of("x1", "rd"), 1)
                dve.wait_ge(*at("x1", "rd", i + 1))
                dve.tensor_tensor(XB["y"][:, bass.ds(i * S, S)], PS[:, 6, 0:S], XB["rd"], ALU.mult).then_inc(of("x1", "o"), 1)
            residual(dve, C_X1, lambda h: dve.wait_ge(*at("x1", "o", 1 + NB)), lambda h: half(XB["y"], h))

        OTHER_SYNC["x1"], OTHER_PE["x1"], OTHER_ACT["x1"], OTHER_DVE["x1"] = x1_sync, x1_pe, x1_act, x1_dve

        def f1_buffers():
            lay = Layout()
            return dict(xp=lay.take(NB, S), om=lay.take(2), t=[lay.take(T) for _ in range(2)], x=[lay.take(T) for _ in range(2)],
                        r=lay.take(T), k=lay.take(T))

        FB = f1_buffers()

        def f1_pe(pe):
            loaded(pe, "f1_wr")
            for n, name in enumerate(("f1_wr", "f1_wk")):
                pe.wait_ge(*at("f1", "x", n + 1))
                for h in range(2):
                    pe.matmul(bank(2 * n + h), w(name), half(FB["x"][n], h), start=True, stop=True).then_inc(of("f1", "h"), 1)
            for h in range(2):
                pe.wait_ge(*at("f1", "act", h + 1))
                pe.matmul(bank(4 + h), w("f1_wv"), half(FB["k"], h), start=True, stop=True).then_inc(of("f1", "y"), 1)
            norm_pe(pe, C_F1)

        def f1_act(act):
            for h in range(2):
                act.wait_ge(*at("f1", "h", h + 1))
                act.activation(half(FB["r"], h), bank(h), ACT.Sigmoid).then_inc(of("f1", "sig"), 1)
            for h in range(2):
                act.wait_ge(*at("f1", "h", h + 3))
                act.activation(half(FB["k"], h), bank(2 + h), ACT.Relu).then_inc(of("f1", "relu"), 1)
            norm_act(act, C_F1)

        def f1_dve(dve):
            loaded(dve, "f1_wr")
            for h in range(2):
                x_ready(dve, C_X1, h)
            xs = X[:, :].rearrange("p (b s) -> p b s", b=NB)
            dve.memset(FB["xp"][:, :, 0:1], 0.0).then_inc(of("f1", "each"), 1)
            dve.tensor_copy(FB["xp"][:, :, 1:S], xs[:, :, 0:S - 1]).then_inc(of("f1", "each"), 1)
            dve.tensor_scalar(FB["om"], w("f1_mu"), -1.0, 1.0, ALU.mult, ALU.add).then_inc(of("f1", "each"), 1)
            dve.wait_ge(*at("f1", "each", 3))
            flat = FB["xp"].rearrange("p b s -> p (b s)")
            for n in range(2):
                dve.tensor_scalar(FB["t"][n], flat, FB["om"][:, n:n + 1], None, ALU.mult).then_inc(of("f1", "each"), 1)
            for n in range(2):
                dve.wait_ge(*at("f1", "each", 4 + n))
                dve.scalar_tensor_tensor(FB["x"][n], X[:, :], wcol("f1_mu", n), FB["t"][n], ALU.mult, ALU.add).then_inc(of("f1", "x"), 1)
            for h in range(2):
                dve.wait_ge(*at("f1", "relu", h + 1))
                dve.tensor_tensor(half(FB["k"], h), half(FB["k"], h), half(FB["k"], h), ALU.mult).then_inc(of("f1", "act"), 1)

            def rows(h):
                dve.wait_ge(*at("f1", "y", h + 1))
                dve.wait_ge(*at("f1", "sig", h + 1))
                dve.tensor_tensor(half(R, h), half(FB["r"], h), bank(4 + h), ALU.mult).then_inc(of("f1", "rv"), 1)
                dve.wait_ge(*at("f1", "rv", h + 1))
                return dve.tensor_tensor(half(R, h), half(R, h), half(X, h), ALU.add)

            norm_dve(dve, C_F1, rows)

        OTHER_PE["f1"], OTHER_ACT["f1"], OTHER_DVE["f1"] = f1_pe, f1_act, f1_dve

        READY_STAGES = 2 * STAGES - 2 * NB

        PREPARED = room - (READY_STAGES * 1024 + 1024 + 512 + 4 * 512)

        def f2_buffers():
            lay = Layout(PREPARED)
            made = dict(stage=lay.take(READY_STAGES * 1024), up=lay.take(2, 512), down=lay.take(512),
                        t=[lay.take(512) for _ in range(4)])
            low = Layout()
            return dict(made, h=low.take(4, T), wd=low.take(512), b=low.take(5))

        UB = f2_buffers()

        def f1_sync(sp):
            x_ready(sp, C_M, 1)
            for n in range(READY_STAGES):
                sp.dma_start(UB["stage"][:, n * 1024:(n + 1) * 1024], stages_in[n:n + 1, :].partition_broadcast(128)) \
                    .then_inc(of("f2", f"stage{n}"), 16)

        def stage_sync(sp, i):
            for k in range(READY_STAGES):
                sp.wait_ge(*at("f2", "made", i * (6 * READY_STAGES) + 6 * (k + 1)))
                sp.dma_start(UB["stage"][:, k * 1024:(k + 1) * 1024],
                             stages_in[bass.ds(i * READY_STAGES + (READY_STAGES + k), 1), :].partition_broadcast(128)) \
                    .then_inc(of("f2", f"stage{k}"), 16)

        def x2_pool(pool):
            loaded(pool, "f2_we")
            made = of("f2", "made")
            n = 0
            for layer in ("up", "down"):
                R2 = 2 if layer == "up" else 1
                for k in range(STAGES):
                    span = 2 ** (k if layer == "up" else STAGES - 1 - k)
                    nb = 512 // (2 * span)
                    pool.wait_ge(*at("f2", f"stage{n % READY_STAGES}", 16 * (n // READY_STAGES + 1)))
                    if layer == "up" and k == 0:
                        src = [W[:, AT[p][0]:AT[p][0] + 512] for p in ("f2_we", "f2_be")]
                    elif k == 0:
                        src = [w("f2_wc")]
                    else:
                        src = [UB["up"][:, r, :] for r in range(2)] if layer == "up" else [UB["down"]]
                    dst = [UB["up"][:, r, :] for r in range(2)] if layer == "up" else [UB["down"]]
                    slot = n % READY_STAGES
                    ws = UB["stage"][:, slot * 1024:(slot + 1) * 1024].rearrange("p (b s i j) -> p b s i j", s=span, i=2, j=2)
                    for r in range(R2):
                        two = src[r].rearrange("p (b c s) -> p b c s", c=2, s=span)
                        for o in range(2):
                            for j in range(2):
                                t = UB["t"][2 * o + j][:, r * 256:(r + 1) * 256].rearrange("p (b s) -> p b s", s=span)
                                wij = ws[:, :, :, o, j] if layer == "up" else ws[:, :, :, j, o]
                                ins = pool.tensor_tensor(t, two[:, :, j, :], wij, ALU.mult)
                    ins.then_inc(made, 4)
                    pool.wait_ge(*at("f2", "made", 6 * n + 4))
                    for o in range(2):
                        for r in range(R2):
                            two = dst[r].rearrange("p (b c s) -> p b c s", c=2, s=span)
                            a, b = [UB["t"][2 * o + j][:, r * 256:(r + 1) * 256].rearrange("p (b s) -> p b s", s=span) for j in range(2)]
                            ins = pool.tensor_tensor(two[:, :, o, :], a, b, ALU.add)
                    ins.then_inc(made, 2)
                    pool.wait_ge(*at("f2", "made", 6 * n + 6))
                    n += 1


        KEYS = CTX + S
        QC = KEYS // 4
        X2T = [(t * 128, min(128, KEYS - t * 128)) for t in range(-(-KEYS // 128))]
        NX = len(X2T)
        PAIRS = H // 2
        GROUPS = [range(4 * g, min(4 * g + 4, NX)) for g in range(4)]

        def pieces_of(kind, n):
            return [(kind, n, j) for j in range(4)] if n < (H if kind == "T" else PAIRS) else []

        FIRST_PIECES = [pieces_of("K", 0) + pieces_of("N", 0) + pieces_of("K", 1) + pieces_of("V", 0)[0:3],
                        pieces_of("V", 0)[3:] + pieces_of("N", 1)]

        class Round:

            def __init__(self, i, last):
                self.i, self.last = i, last
                self.order = FIRST_PIECES[0] + FIRST_PIECES[1] + [q for h in range(H) for part in self.slot(h) for q in part]
                self.taken = {
                    "x2_out_dve": [q for q in self.order if q[0] in "KMN" or (q[0] in "VT" and q[2] % 2 == 0)],
                    "x2_out_act": [q for q in self.order if q[0] in "KMR" or (q[0] in "VT" and q[2] % 2)]}

            def slot(self, h):
                t, nxt = pieces_of("T", h), h // 2 + 1
                nr, vl = pieces_of("N", nxt) if h else [], pieces_of("V", nxt)
                if h >= H - 2:
                    return t, [] if self.last else pieces_of("M" if h == H - 2 else "R", 0)
                if h % 2 == 0:
                    return [t[0], t[1]] + nr[0:1] + [t[2]] + nr[1:2] + [t[3]] + nr[2:], vl[0:2]
                return [t[0], t[1]] + vl[2:3] + [t[2], t[3]] + vl[3:], pieces_of("K", nxt + 1)

            def bank(self, q):
                return 4 + self.order.index(q) % 3

            def mine(self, eng_name, pieces):
                return [q for q in pieces if q in self.taken[eng_name]]

        FULL = Round(None, False)

        def emptied(eng, b, q, by=("x2_out_dve", "x2_out_act")):
            for name, mine in b.taken.items():
                if q in mine and name in by and (q[0] not in "KM" or name == by[0]):
                    eng.wait_ge(sem(name), b.i * len(FULL.taken[name]) + (2 + mine.index(q)))

        def made(eng, b, q):
            eng.wait_ge(sem("x2_piece"), b.i * len(FULL.order) + (1 + b.order.index(q)))

        def rounds(eng, body):
            with eng.Fori(0, NB - 1) as i:
                body(Round(i, False))
            body(Round(NB - 1, True))

        def x2_buffers():
            lay = Layout()
            return dict(
                xn=lay.take(KEYS), sq=lay.take(KEYS), sd=lay.take(KEYS), mask=lay.take(CTX // 4 + 1),
                mrow=lay.take_bf16(KEYS), ones=lay.take_bf16(S), y=lay.take(T),
                k=[lay.take(KEYS) for _ in range(2)], v=[lay.take(NX, 128) for _ in range(2)],
                p=[lay.take(KEYS) for _ in range(2)], pt=[lay.take(NX, S) for _ in range(2)],
                qn=lay.take(PAIRS, S), qbd=lay.take(PAIRS, 2, S), o=lay.take(PAIRS, S),
                nm=lay.take(H), den=lay.take(H), rd=lay.take(H), rdt=lay.take(S), end=lay.at)

        B2 = x2_buffers()
        assert B2["end"] <= PREPARED, (B2["end"], PREPARED)
        qsq, qsd = B2["p"][0][:, 0:T], B2["p"][1][:, 0:T]
        quarter = lambda a, c: a[:, c * QC:(c + 1) * QC]

        def x2_sync(sp):
            x_ready(sp, C_A2, 1)
            with sp.Fori(0, NB) as i:
                sp.wait_ge(*at("x2", "ctx_used", i + 1))
                sp.dma_start(B2["xn"][:, 0:CTX], ctx_in[:, bass.ds(i * CTX, CTX)]).then_inc(of("x2", "ctx"), 16)
                sp.dma_start(B2["mask"].bitcast(U8)[0:1, 0:CTX], mask2_in[bass.ds(i, 1), :]).then_inc(of("x2", "mask"), 16)
                stage_sync(sp, i)

        def x2_pe(pe):
            loaded(pe, "x2_wq")
            x_ready(pe, C_A2, 1)
            pe.sem_inc(of("x2", "ctx_used"), 1)
            pe.sem_inc(of("x2", "scores"), 1)
            pe.sem_inc(of("x2", "pv"), 2)
            pe.wait_ge(*at("x2", "vzero", 4))
            pe.wait_ge(*at("x2", "ctx", 16))
            pe.wait_ge(sem("x2_lat"), 1)
            pe.wait_ge(*at("x2", "exp", 1))
            for c in range(4):
                pe.matmul(PS[:, c, 0:QC], mean_w[:, :], quarter(B2["xn"], c), start=True, stop=True).then_inc(sem("x2_mean"), 1)
            for c in range(4):
                pe.wait_ge(sem("x2_sq"), c + 1)
                pe.matmul(PS[:, c, 0:QC], mean_w[:, :], quarter(B2["sq"], c), start=True, stop=True).then_inc(sem("x2_var"), 1)

            def body(b):
                i = b.i

                def piece(q):
                    kind, n, j = q
                    at_order, b6 = b.order.index(q), b.bank(q)
                    if at_order >= 3:
                        emptied(pe, b, b.order[at_order - 3])
                    else:
                        for name, mine in FULL.taken.items():
                            pe.wait_ge(sem(name), i * len(mine) + 1)
                    if kind == "K":
                        mm = pe.matmul(PS[:, b6, 0:QC], w("x2_wk")[:, 128 * n:128 * n + 128], quarter(B2["xn"], j), start=True, stop=True)
                    elif kind == "N":
                        emptied(pe, b, ("K", n, 3), ("x2_out_act",))
                        mm = pe.matmul(PS[:, b6, 0:QC], w("blockdiag"), quarter(B2["sq"], j), start=True, stop=True)
                    elif kind == "M":
                        if j == 0:
                            pe.wait_ge(*at("x2", "ctx", i * 16 + 32))
                            pe.wait_ge(sem("x2_lat"), i + 2)
                        mm = pe.matmul(PS[:, b6, 0:QC], mean_w[:, :], quarter(B2["xn"], j), start=True, stop=True)
                    elif kind == "R":
                        emptied(pe, b, ("M", 0, 3), ("x2_out_act",))
                        mm = pe.matmul(PS[:, b6, 0:QC], mean_w[:, :], quarter(B2["sq"], j), start=True, stop=True)
                    elif kind == "V":
                        for t in GROUPS[j]:
                            t0, m = X2T[t]
                            mm = pe.matmul(PS[0:m, b6, (t % 4) * 128:(t % 4) * 128 + 128], B2["xn"][:, t0:t0 + m],
                                           w("x2_wv")[:, 128 * n:128 * n + 128], start=True, stop=True)
                    else:
                        if j == 0:
                            pe.wait_ge(*at("x2", "exp", i * H + (n + 2)))
                        for t in GROUPS[j]:
                            t0, m = X2T[t]
                            mm = pe.transpose(PS[0:m, b6, (t % 4) * S:(t % 4 + 1) * S], B2["p"][n % 2][0:S, t0:t0 + m],
                                              ident[0:S, 0:S])
                    mm.then_inc(sem("x2_piece"), 1)
                    if q == ("V", PAIRS - 1, 3):
                        made(pe, b, q)
                        pe.sem_inc(of("x2", "ctx_used"), 1)

                def scores(h):
                    p, e = divmod(h, 2)
                    pe.wait_ge(*at("x2", "exp", i * H + (h + 1)))
                    pe.wait_ge(sem("x2_kn"), i * PAIRS + (p + 1))
                    for c in range(4):
                        pe.matmul(PS[0:S, c, 0:QC], B2["qbd"][:, p, e, :], quarter(B2["k"][p % 2], c), start=True, stop=False)
                        mm = pe.matmul(PS[0:S, c, 0:QC], B2["ones"], B2["mrow"][:, c * QC:(c + 1) * QC],
                                       start=False, stop=True)
                    mm.then_inc(of("x2", "scores"), 1)

                def product(h):
                    p, e = divmod(h, 2)
                    for j in (2, 3):
                        emptied(pe, b, ("T", h, j))
                        emptied(pe, b, ("V", p, j))
                    if h == 0 or h == 8:
                        pe.wait_ge(*at("x2", "o", i * 2 + (h // 8 + 1)))
                    for t in range(NX):
                        n = X2T[t][1]
                        mm = pe.matmul(PS[64 * e:64 * e + 64, 7, (p % 4) * S:(p % 4 + 1) * S],
                                       B2["v"][p % 2][0:n, t, 64 * e:64 * e + 64], B2["pt"][h % 2][0:n, t, :],
                                       start=(t == 0), stop=(t == NX - 1))
                    mm.then_inc(of("x2", "pv"), 1)

                pe.wait_ge(sem("x2_xn"), i * 4 + 2)
                for p in range(PAIRS):
                    mm = pe.matmul(PS[:, p // 4, (p % 4) * S:(p % 4 + 1) * S], w("x2_wq")[:, 128 * p:128 * p + 128],
                                   B2["xn"][:, CTX:KEYS], start=True, stop=True)
                mm.then_inc(of("x2", "q"), 1)
                pe.wait_ge(sem("x2_xn"), i * 4 + 4)
                for q in FIRST_PIECES[0][0:4]:
                    piece(q)
                pe.wait_ge(sem("x2_qsq"), i + 1)
                for a in range(2):
                    mm = pe.matmul(PS[:, 2 + a, 0:4 * S], w("blockdiag"), qsq[:, a * 4 * S:(a + 1) * 4 * S], start=True, stop=True)
                mm.then_inc(sem("x2_qss"), 1)
                for q in FIRST_PIECES[0][4:]:
                    piece(q)
                pe.wait_ge(*at("x2", "op0", i * 2 + 2))
                scores(0)
                for q in FIRST_PIECES[1]:
                    piece(q)
                for h in range(H):
                    before, after = b.slot(h)
                    for q in before:
                        piece(q)
                    if h < H - 1:
                        scores(h + 1)
                    product(h)
                    for q in after:
                        piece(q)
                pe.wait_ge(*at("x2", "rd", i + 1))
                pe.transpose(PS[0:H, 3, 0:S], B2["rd"][0:S], ident[0:S, 0:S]).then_inc(of("x2", "rdt"), 1)
                pe.wait_ge(*at("x2", "rdtf", i + 1))
                sel = w("sel64", H).rearrange("p (g m) -> p g m", g=PAIRS)
                for p in range(PAIRS):
                    mm = pe.matmul(PS[:, p // 4, (p % 4) * S:(p % 4 + 1) * S], sel[:, p, :], B2["rdt"][0:H, :], start=True, stop=True)
                mm.then_inc(of("x2", "bc"), 1)
                pe.wait_ge(*at("x2", "normed", i + 1))
                for p in range(PAIRS):
                    mm = pe.matmul(PS[:, 2, 0:S], w("x2_wo")[:, 128 * p:128 * p + 128], B2["o"][:, p, :],
                                   start=(p == 0), stop=(p == PAIRS - 1))
                mm.then_inc(of("x2", "y"), 1)
                pe.wait_ge(sem("x2_yf"), i + 1)

            rounds(pe, body)
            norm_pe(pe, C_X2)

        def x2_act(act):
            x_ready(act, C_A2, 1)
            act.sem_inc(of("x2", "exp"), 1)
            act.sem_inc(sem("x2_out_act"), 1)
            for c in range(4):
                act.wait_ge(sem("x2_cen"), c + 1)
                act.activation(quarter(B2["sq"], c), quarter(B2["xn"], c), ACT.Square).then_inc(sem("x2_sq"), 1)
            act.wait_ge(sem("x2_var"), 4)
            act.activation(B2["sq"].rearrange("p (a b) -> p a b", a=4), PS[:, 0:4, 0:QC], ACT.Ln, bias=epsc[:, :]) \
                .then_inc(sem("x2_ln"), 1)
            act.wait_ge(sem("x2_ln"), 1)
            act.activation(B2["sq"], B2["sq"], ACT.Exp, scale=-0.5).then_inc(sem("x2_rs"), 1)

            def body(b):
                i = b.i

                def rsqrt(buf, before, after, k):
                    act.activation(buf, buf, ACT.Ln).then_inc(before, 1)
                    act.wait_ge(before, k)
                    act.activation(buf, buf, ACT.Exp, scale=-0.5).then_inc(after, 1)

                def norms(p):
                    emptied(act, b, ("N", p, 3))
                    rsqrt(B2["sd"], sem("x2_kln"), sem("x2_krs"), i * PAIRS + (p + 1))

                def probs(h):
                    act.wait_ge(*at("x2", "nm", i * H + (h + 1)))
                    act.activation(B2["p"][h % 2][0:S].rearrange("p (a b) -> p a b", a=4), PS[0:S, 0:4, 0:QC], ACT.Exp,
                                   bias=B2["nm"][0:S, h:h + 1], accum_out=B2["den"][0:S, h:h + 1]).then_inc(of("x2", "exp"), 1)

                def take(pieces):
                    for q in b.mine("x2_out_act", pieces):
                        kind, n, j = q
                        if kind == "M":
                            emptied(act, b, q)
                            act.activation(quarter(B2["sq"], j), quarter(B2["xn"], j), ACT.Square).then_inc(sem("x2_out_act"), 1)
                            continue
                        if kind == "K":
                            emptied(act, b, q)
                            act.activation(quarter(B2["sq"], j), quarter(B2["k"][n % 2], j), ACT.Square).then_inc(sem("x2_out_act"), 1)
                            continue
                        made(act, b, q)
                        ps = PS[:, b.bank(q), :]
                        if kind == "R":
                            act.activation(quarter(B2["sq"], j), ps[:, 0:QC], ACT.Ln, bias=epsc[:, :]).then_inc(sem("x2_out_act"), 1)
                            continue
                        wide = 128 if kind == "V" else S
                        act.wait_ge(*at("x2", "pv", i * H + (n + 1 if kind == "T" else max(2 * n, 2))))
                        dst = B2["v" if kind == "V" else "pt"][n % 2]
                        tiles = GROUPS[j]
                        rows = 128 if j < 3 else X2T[-1][1]
                        act.activation(dst[0:rows, tiles[0]:tiles[-1] + 1, :].rearrange("p t s -> p (t s)"),
                                       ps[0:rows, 0:wide * len(tiles)], ACT.Copy).then_inc(sem("x2_out_act"), 1)

                act.wait_ge(*at("x2", "q", i + 1))
                act.activation(qsq.rearrange("p (a b) -> p a b", a=2), PS[:, 0:2, 0:4 * S], ACT.Square).then_inc(sem("x2_qsq"), 1)
                take(FIRST_PIECES[0][0:4])
                act.wait_ge(sem("x2_qcl"), i + 1)
                act.activation(qsd, qsd, ACT.Ln).then_inc(sem("x2_qln"), 1)
                emptied(act, b, ("N", 0, 3))
                act.activation(B2["sd"], B2["sd"], ACT.Ln).then_inc(sem("x2_kln"), 1)
                act.wait_ge(sem("x2_qln"), i + 1)
                act.activation(qsd, qsd, ACT.Exp, scale=-0.5).then_inc(sem("x2_qrs"), 1)
                act.wait_ge(sem("x2_kln"), i * PAIRS + 1)
                act.activation(B2["sd"], B2["sd"], ACT.Exp, scale=-0.5).then_inc(sem("x2_krs"), 1)
                take(FIRST_PIECES[0][8:])
                probs(0)
                take(FIRST_PIECES[1])
                for h in range(H):
                    before, after = b.slot(h)
                    take(before)
                    if h % 2 == 0 and h // 2 + 1 < PAIRS:
                        norms(h // 2 + 1)
                    if h < H - 1:
                        probs(h + 1)
                    take(after)
                if not b.last:
                    emptied(act, b, ("R", 0, 3))
                    act.activation(B2["sq"], B2["sq"], ACT.Exp, scale=-0.5).then_inc(sem("x2_rs"), 1)

            rounds(act, body)
            norm_act(act, C_X2)

        def x2_dve(dve):
            loaded(dve, "x2_wq")
            x_ready(dve, C_A2, 1)
            dve.memset(B2["qbd"].rearrange("p a b s -> p (a b s)"), 0.0).then_inc(of("x2", "vzero"), 1)
            dve.memset(B2["ones"], 0.0).then_inc(sem("x2_zero"), 1)
            dve.wait_ge(sem("x2_zero"), 1)
            dve.memset(B2["ones"][0:1], 1.0).then_inc(of("x2", "vzero"), 1)
            dve.memset(B2["mrow"], 0.0).then_inc(of("x2", "vzero"), 1)
            dve.memset(B2["rdt"][0:H], 0.0).then_inc(of("x2", "vzero"), 1)
            dve.wait_ge(*at("x2", "vzero", 4))
            dve.sem_inc(of("x2", "o"), 1)
            dve.sem_inc(sem("x2_out_dve"), 1)

            def affine(n, plus=0):
                dve.wait_ge(sem("x2_rs"), n + (1 + plus))
                for j, (a, m, g) in enumerate(((CTX, S, 2), (0, CTX, 0))):
                    rows = B2["xn"][:, a:a + m]
                    dve.scalar_tensor_tensor(rows, rows, wcol("x2_ln", g), B2["sq"][:, a:a + m], ALU.mult, ALU.mult).then_inc(sem("x2_xn"), 1)
                    dve.wait_ge(sem("x2_xn"), n * 4 + (4 * plus + 2 * j + 1))
                    dve.tensor_scalar(rows, rows, wcol("x2_ln", g + 1), None, ALU.add).then_inc(sem("x2_xn"), 1)

            dve.tensor_copy(B2["xn"][:, CTX:KEYS], X[:, 0:S]).then_inc(sem("x2_lat"), 1)
            for c in range(4):
                dve.wait_ge(sem("x2_mean"), c + 1)
                dve.tensor_tensor(quarter(B2["xn"], c), quarter(B2["xn"], c), PS[:, c, 0:QC], ALU.subtract).then_inc(sem("x2_cen"), 1)
            affine(0)

            def body(b):
                i = b.i

                def normed(p):
                    dve.wait_ge(sem("x2_krs"), i * PAIRS + (p + 1))
                    k = B2["k"][p % 2]
                    dve.scalar_tensor_tensor(k, k, wcol("x2_g", 1), B2["sd"], ALU.mult, ALU.mult).then_inc(sem("x2_kn"), 1)

                def take(pieces):
                    for q in b.mine("x2_out_dve", pieces):
                        kind, n, j = q
                        made(dve, b, q)
                        ps = PS[:, b.bank(q), :]
                        if kind == "K":
                            ins = dve.tensor_copy(quarter(B2["k"][n % 2], j), ps[:, 0:QC])
                        elif kind == "M":
                            ins = dve.tensor_tensor(quarter(B2["xn"], j), quarter(B2["xn"], j), ps[:, 0:QC], ALU.subtract)
                        elif kind == "N":
                            ins = dve.tensor_scalar(quarter(B2["sd"], j), ps[:, 0:QC], 1.0 / 64, 1e-16, ALU.mult, ALU.max)
                        else:
                            wide = 128 if kind == "V" else S
                            dve.wait_ge(*at("x2", "pv", i * H + (n + 1 if kind == "T" else max(2 * n, 2))))
                            dst = B2["v" if kind == "V" else "pt"][n % 2]
                            tiles = GROUPS[j]
                            ins = dve.tensor_copy(dst[:, tiles[0]:tiles[-1] + 1, :].rearrange("p t s -> p (t s)"), ps[:, 0:wide * len(tiles)])
                        ins.then_inc(sem("x2_out_dve"), 1)

                def maximum(h):
                    dve.wait_ge(*at("x2", "scores", i * H + (h + 2)))
                    dve.tensor_reduce(B2["nm"][0:S, h:h + 1], PS[0:S, 0:4, 0:QC], mybir.AxisListType.XY, ALU.max, negate=True) \
                        .then_inc(of("x2", "nm"), 1)

                dve.wait_ge(*at("x2", "mask", i * 16 + 16))
                dve.tensor_scalar(B2["mrow"][0:1, 0:CTX], B2["mask"].bitcast(U8)[0:1, 0:CTX], 0.0, -BIG, ALU.is_equal, ALU.mult) \
                    .then_inc(of("x2", "mrow"), 1)
                take(FIRST_PIECES[0][0:4])
                dve.wait_ge(sem("x2_qss"), i + 1)
                dve.tensor_scalar(qsd.rearrange("p (a b) -> p a b", a=2), PS[:, 2:4, 0:4 * S], 1.0 / 64, 1e-16,
                                  ALU.mult, ALU.max).then_inc(sem("x2_qcl"), 1)
                take(FIRST_PIECES[0][4:12])
                dve.wait_ge(sem("x2_qrs"), i + 1)
                dve.scalar_tensor_tensor(B2["qn"].rearrange("p (a b) s -> p a (b s)", a=2), PS[:, 0:2, 0:4 * S], wcol("x2_g", 0),
                                         qsd.rearrange("p (a b) -> p a b", a=2), ALU.mult, ALU.mult).then_inc(sem("x2_qn"), 1)
                dve.wait_ge(sem("x2_qn"), i + 1)
                for e in range(2):
                    r = slice(64 * e, 64 * e + 64)
                    dve.tensor_scalar(B2["qbd"][r, :, e, :], B2["qn"][r], 64 ** -0.5, None, ALU.mult).then_inc(of("x2", "op0"), 1)
                take(FIRST_PIECES[0][12:])
                normed(0)
                maximum(0)
                take(FIRST_PIECES[1])
                for h in range(H):
                    before, after = b.slot(h)
                    take(before)
                    if h < H - 1:
                        maximum(h + 1)
                    if h == H - 2 and not b.last:
                        made(dve, b, ("V", PAIRS - 1, 3))
                        dve.tensor_copy(B2["xn"][:, CTX:KEYS], X[:, bass.ds(i * S + S, S)]).then_inc(sem("x2_lat"), 1)
                    take(after)
                    if h % 2 == 0 and h // 2 + 1 < PAIRS:
                        normed(h // 2 + 1)
                    if h % 8 == 7:
                        dve.wait_ge(*at("x2", "pv", i * H + (h + 3)))
                        a = 4 * (h // 8)
                        dve.tensor_copy(B2["o"][:, a:a + 4, :].rearrange("p a s -> p (a s)"), PS[:, 7, 0:4 * S]).then_inc(of("x2", "o"), 1)
                dve.wait_ge(*at("x2", "exp", i * H + (H + 1)))
                dve.reciprocal(B2["rd"][0:S], B2["den"][0:S]).then_inc(of("x2", "rd"), 1)
                dve.wait_ge(*at("x2", "rdt", i + 1))
                dve.tensor_copy(B2["rdt"][0:H], PS[0:H, 3, 0:S]).then_inc(of("x2", "rdtf"), 1)
                dve.wait_ge(*at("x2", "bc", i + 1))
                dve.wait_ge(*at("x2", "o", i * 2 + 3))
                o = B2["o"].rearrange("p (a b) s -> p a (b s)", a=2)
                dve.tensor_tensor(o, o, PS[:, 0:2, 0:4 * S], ALU.mult).then_inc(of("x2", "normed"), 1)
                if not b.last:
                    affine(i, 1)
                dve.wait_ge(*at("x2", "y", i + 1))
                dve.tensor_copy(B2["y"][:, bass.ds(i * S, S)], PS[:, 2, 0:S]).then_inc(sem("x2_yf"), 1)

            rounds(dve, body)
            residual(dve, C_X2, lambda h: dve.wait_ge(sem("x2_yf"), NB), lambda h: half(B2["y"], h), wcol("x2_b"))

        OTHER_SYNC["x2"], OTHER_PE["x2"], OTHER_ACT["x2"], OTHER_DVE["x2"] = x2_sync, x2_pe, x2_act, x2_dve
        def f2_pe(pe):
            L = "f2"
            pe.wait_ge(*at(L, "made", 12 * STAGES))
            for t in range(4):
                pe.transpose(PS[:, 0, 128 * t:128 * t + 128], UB["down"][:, 128 * t:128 * t + 128], ident)
            for t in range(4):
                mm = pe.matmul(PS[:, 1, t:t + 1], UB["up"][0:1, 1, 128 * t:128 * t + 128], mean_w[0:1, 0:1], start=True, stop=True)
            mm.then_inc(of(L, "gt"), 1)
            pe.wait_ge(*at(L, "gtc", 3))
            def second(h):
                for t in range(4):
                    pe.wait_ge(*at(L, "act", 4 * h + t + 1))
                    mm = pe.matmul(bank(4 + h), UB["wd"][:, 128 * t:128 * t + 128], UB["h"][:, t, h * HALF:(h + 1) * HALF],
                                   start=(t == 0), stop=(t == 3))
                mm.then_inc(of(L, "y"), 1)

            for h in range(2):
                x_ready(pe, C_X2, h)
                for t in range(4):
                    if h:
                        pe.wait_ge(*at(L, "act", t + 1))
                    pe.matmul(bank(t), UB["up"][:, 0, 128 * t:128 * t + 128], half(X, h), start=True, stop=True) \
                        .then_inc(of(L, "h"), 1)
            for h in range(2):
                second(h)
            norm_pe(pe, C_F2)

        def f2_act(act):
            L = "f2"
            act.wait_ge(*at(L, "gtc", 2))
            for h in range(2):
                for t in range(4):
                    act.wait_ge(*at(L, "h", 4 * h + t + 1))
                    act.activation(UB["h"][:, t, h * HALF:(h + 1) * HALF], bank(t), ACT.Gelu, bias=UB["b"][:, t:t + 1]) \
                        .then_inc(of(L, "act"), 1)
            norm_act(act, C_F2)

        def f2_dve(dve):
            L = "f2"
            dve.wait_ge(*at(L, "gt", 1))
            dve.scalar_tensor_tensor(UB["b"][:, 0:4], PS[:, 1, 0:4], 128.0, w("f2_ub"), ALU.mult, ALU.add).then_inc(of(L, "gtc"), 1)
            dve.tensor_tensor(UB["b"][:, 4:5], wcol("f2_b", 0), wcol("f2_b", 1), ALU.add).then_inc(of(L, "gtc"), 1)
            dve.tensor_copy(UB["wd"], PS[:, 0, :]).then_inc(of(L, "gtc"), 1)
            dve.wait_ge(*at(L, "gtc", 3))
            residual(dve, C_F2, lambda h: dve.wait_ge(*at(L, "y", h + 1)), lambda h: bank(4 + h), UB["b"][:, 4:5])

        OTHER_SYNC["f1"], OTHER_POOL["x2"] = f1_sync, x2_pool
        OTHER_PE["f2"], OTHER_ACT["f2"], OTHER_DVE["f2"] = f2_pe, f2_act, f2_dve

        LAYERS = [
            ("a0", C_A0), ("x0", C_X0), ("f0", C_F0), ("m1", C_M), ("x1", C_X1), ("f1", C_F1),
            ("a2", C_A2), ("x2", C_X2), ("f2", C_F2), ("a3", C_A3), ("x3", C_X3), ("f3", C_F3)]
        SELF = {"a0": "window", "a2": "rope", "a3": "top"}
        block = scope.enter_context(nc.Block())

        @block.sync
        def _(sp):
            for n, first in enumerate(LOADS):
                a = AT[first][0]
                b = AT[LOADS[n + 1]][0] if n + 1 < len(LOADS) else PACKED
                if n == 0:
                    sp.dma_start(X[:, :], x_in).then_inc(sem("x_loaded"), 16)
                if n == 1:
                    sp.wait_ge(sem("w_loaded0"), 16)
                sp.dma_start(W[:, a:b], packed_in[:, a:b]).then_inc(sem(f"w_loaded{n}"), 16)
            for L, c in LAYERS:
                if L in ("x0", "x3"):
                    cross_sync(sp, L, c - 1, L == "x0")
                elif L in ("f0", "f3"):
                    moe_sync(sp, L, c - 1)
                elif L in OTHER_SYNC:
                    OTHER_SYNC[L](sp)
            x_ready(sp, LAYERS[-1][1], 1)
            sp.dma_start(out, X[:, :]).then_inc(sem("stored"), 16)
            sp.wait_ge(sem("stored"), 16)

        @block.gpsimd
        def _(pool):
            pool.memset(mean_w[:, :], 1.0 / D).then_inc(sem("consts"), 1)
            pool.memset(epsc[:, :], LN_EPS).then_inc(sem("consts"), 1)
            for L, c in LAYERS:
                if L in SELF:
                    self_pool(pool, SELF[L], c - 1)
                elif L in ("x0", "x3"):
                    cross_pool(pool, L, c - 1, L == "x0")
                elif L in ("f0", "f3"):
                    moe_pool(pool, L, c - 1)
                elif L in OTHER_POOL:
                    OTHER_POOL[L](pool)

        @block.scalar
        def _(act):
            act.wait_ge(sem("consts"), 2)
            for L, c in LAYERS:
                if L in SELF:
                    loaded(act, f"{L}_wq")
                    self_act(act, SELF[L], c - 1)
                elif L in ("x0", "x3"):
                    cross_act(act, L, c - 1, L == "x0")
                elif L in ("f0", "f3"):
                    moe_act(act, L, c - 1)
                else:
                    OTHER_ACT[L](act)

        @block.vector
        def _(dve):
            for L, c in LAYERS:
                if L in SELF:
                    x_ready(dve, c - 1, 1)
                    self_dve(dve, SELF[L], c - 1)
                elif L in ("x0", "x3"):
                    cross_dve(dve, L, c - 1, L == "x0")
                elif L in ("f0", "f3"):
                    moe_dve(dve, L, c - 1)
                else:
                    OTHER_DVE[L](dve)

        @block.tensor
        def _(pe):
            for L, c in LAYERS:
                if L in SELF:
                    self_pe(pe, SELF[L], c - 1)
                elif L in ("x0", "x3"):
                    cross_pe(pe, L, c - 1, L == "x0")
                elif L in ("f0", "f3"):
                    moe_pe(pe, L, c - 1)
                else:
                    OTHER_PE[L](pe)


def constants():
    c = {"ident": np.eye(128), "headmask": np.zeros((128, H)), "selx": np.zeros((128, 128)),
         "parity": np.zeros((128, 2)),
         "window": np.zeros((S, S)), "blockdiag": np.zeros((128, 128)), "sel64": np.zeros((H, 8, 128)),
         "maskab": np.zeros((128, 2)), "m_sel": np.zeros((40, 16, 2, 128))}
    for p in range(128):
        c["headmask"][p, p // DH] = 1
        c["sel64"][:, :, p] = (np.arange(H)[:, None] == 2 * np.arange(8)[None, :] + p // 64)
        c["selx"][p // SLOT * SLOT + DH, p] = 1
        c["parity"][p, p // DH % 2] = 1
    c["blockdiag"][0:64, 0:64] = 1
    c["blockdiag"][64:, 64:] = 1
    i, j = np.arange(S)[:, None], np.arange(S)[None, :]
    c["window"][...] = np.where((abs(i - j) <= 32) | (i == 0) | (j == 0), 0.0, -BIG)
    c["maskab"][0:2, 0] = [-9984, -16]
    for n in range(16):
        c["m_sel"][8 + n, n, 0] = 1
        c["m_sel"][24 + n, n, 1] = 1
    inv = np.float32(1.0) / np.float32(10000.0) ** (np.arange(0, DH, 2, dtype=np.float32) / np.float32(DH))
    ang = np.outer(np.arange(S, dtype=np.float32), inv.astype(np.float32)).astype(np.float32)
    cos, sin = np.cos(ang).T, np.sin(ang).T
    rows = np.arange(128) % DH // 2
    sign = np.where(np.arange(128) % 2 == 0, -1.0, 1.0)[:, None]
    c["cosq"], c["sinq"] = cos[rows] * DH ** -0.5, sin[rows] * sign * DH ** -0.5
    c["cosk"], c["sink"] = cos[rows], sin[rows] * sign
    return c


def slotted(wo):
    a = np.zeros((4, SLOT, 4, wo.shape[1]), wo.dtype)
    a[:, 0:DH] = wo.reshape(4, 4, DH, -1).transpose(1, 2, 0, 3)
    return a.reshape(128, -1)


def packed(v):
    swap = np.arange(128) ^ 1
    col = lambda *a: np.stack(a, 1)
    tiles = lambda a: a.reshape(-1, 128, a.shape[1]).transpose(1, 0, 2).reshape(128, -1)
    row = lambda a: np.broadcast_to(a, (128, a.shape[0]))
    c = constants()
    for L, N in (("a0", "L0_attn_"), ("x0", "L0_xattn_"), ("a3", "L3_attn_")):
        c.update({f"{L}_wq": v[N + "Wq"], f"{L}_wk": v[N + "Wk"], f"{L}_wv": v[N + "Wv"], f"{L}_wo": slotted(v[N + "Wo"]),
                  f"{L}_bv": row(v[N + "bv"]), f"{L}_b": col(v[N + "bq"], v[N + "bk"], v[N + "bo"])})
    c.update({"f0_wg": v["L0_ffn_wg"], "f0_b2": v["L0_ffn_b2"]})
    M = "L1_attn_"
    dtw = np.zeros((40, 256), np.float32)
    dtw[0:8] = v[M + "dt_proj_w"].T
    conv = np.concatenate([v[M + "conv_w"], v[M + "conv_b"][:, None]], 1)
    c.update({"m_ln1": col(v[M + "ln1_w"], v[M + "ln1_b"]), "m_ln2": col(v[M + "ln2_w"], v[M + "ln2_b"]),
              "m_in": v[M + "in_proj_w"].T, "m_conv": tiles(conv), "m_xp": tiles(v[M + "x_proj_w"].T), "m_dtw": dtw,
              "m_dtb": v[M + "dt_proj_b"].reshape(2, 128).T, "m_alog": tiles(v[M + "A_log"]),
              "m_d": v[M + "D"].reshape(2, 128).T, "m_out": tiles(v[M + "out_proj_w"].T), "m_w1": v[M + "ffn_w1"].T,
              "m_b1": v[M + "ffn_b1"].reshape(2, 128).T, "m_w2": tiles(v[M + "ffn_w2"].T), "m_b2": v[M + "ffn_b2"][:, None]})
    c.update({"x1_wq": v["L1_xattn_wq"].T, "x1_wk": v["L1_xattn_wk"].T, "x1_wv": v["L1_xattn_wv"].T,
              "f1_wr": v["L1_ffn_W_r"].T, "f1_wk": v["L1_ffn_W_k"].T, "f1_wv": v["L1_ffn_W_v"].T,
              "f1_mu": col(v["L1_ffn_mu_r"], v["L1_ffn_mu_k"])})
    N = "L2_attn_"
    c.update({"a2_wq": v[N + "wq"].T, "a2_wk": v[N + "wk"].T, "a2_wqs": v[N + "wq"].T[:, swap],
              "a2_wks": v[N + "wk"].T[:, swap], "a2_wv": v[N + "wv"].T, "a2_wo": slotted(v[N + "wo"].T)})
    N = "L2_xattn_"
    twice = lambda a: np.concatenate([a, a])
    c.update({"x2_ln": col(v[N + "ln_x_g"], v[N + "ln_x_b"], v[N + "ln_l_g"], v[N + "ln_l_b"]),
              "x2_g": col(twice(v[N + "qn_g"]), twice(v[N + "kn_g"])), "x2_wq": v[N + "Wq"],
              "x2_wk": v[N + "Wkv"][:, 0:1024], "x2_wv": v[N + "Wkv"][:, 1024:], "x2_wo": tiles(v[N + "Wout"]),
              "x2_b": v[N + "bout"][:, None]})
    N = "L2_ffn_"
    c.update({"f2_we": v[N + "W_exp"], "f2_wc": v[N + "W_con"].T, "f2_be": row(v[N + "b_exp"]),
              "f2_ub": v[N + "up_bias"].reshape(4, 128).T, "f2_b": col(v[N + "b_con"], v[N + "down_bias"])})
    N = "L3_xattn_"
    c.update({"x3_wq": v[N + "Wq"], "x3_wk": v[N + "Wk"], "x3_wv": v[N + "Wv"], "x3_wo": slotted(v[N + "Wp"]),
              "x3_b": v[N + "bp"][:, None]})
    N = "L3_ffn_"
    c.update({"f3_scale": v[N + "scale"][:, None], "f3_wg": v[N + "gate_w"].T, "f3_bg": row(v[N + "gate_b"]),
              "f3_b2": v[N + "mlp2_b"]})
    a = np.zeros((128, PACKED), np.float32)
    for name, (at, n) in AT.items():
        piece = np.asarray(c[name])
        a[0:piece.shape[0], at:at + n] = piece.reshape(piece.shape[0], n)
    return a


def experts(w1, w2, b1, width):
    E, n = w1.shape[0], len(b1)
    a = np.zeros((E, 128, width), np.float32)
    halves = w1.shape[2] // 128
    a[:, :, 0:128 * halves] = w1
    a[:, :, 128 * halves:128 * halves + 128] = w2
    for e in range(E):
        a[e, e, 128 * halves + 128:128 * halves + 256] = 1
    for j, b in enumerate(b1):
        a[:, :, width - n + j] = b
    return a.transpose(1, 0, 2).reshape(128, -1)


def arrays_of(v):
    v = {k: np.asarray(a) for k, a in v.items()}
    w1, b1 = v["L3_ffn_mlp1_w"].transpose(0, 2, 1), v["L3_ffn_mlp1_b"]
    w1 = np.concatenate([w1[:, :, 0::2], w1[:, :, 1::2]], 2)
    spread = lambda a: a.reshape(9, 256 * 4)
    return {
        "x_in": v["x"].transpose(2, 0, 1).reshape(D, T), "ctx_in": v["ctx_1024"].transpose(2, 0, 1).reshape(D, NB * CTX),
        "mask0_in": v["mask_Bx1x1xS2_if1"].reshape(NB, CTX), "mask2_in": v["mask_BxS2_bf1"].view(np.uint8),
        "packed_in": packed(v),
        "expert0_in": experts(v["L0_ffn_w1"], v["L0_ffn_w2"], [v["L0_ffn_b1"]], EXPERT0),
        "expert3_in": experts(w1, v["L3_ffn_mlp2_w"].transpose(0, 2, 1), [b1[:, 0::2], b1[:, 1::2]], EXPERT3),
        "stages_in": np.concatenate([spread(v["L2_ffn_up_weights"]), spread(v["L2_ffn_down_weights"])[::-1]]),
    }


def kernel(**inputs):
    import concourse.bacc as bacc
    from concourse.bass_utils import run_bass_kernel_spmd
    nc = bacc.Bacc("TRN2", target_bir_lowering=False, num_devices=1)
    arrays = {n: np.ascontiguousarray(a) for n, a in arrays_of(inputs).items()}
    args = [nc.dram_tensor(n, a.shape, mybir.dt.from_np(a.dtype), kind="ExternalInput").ap() for n, a in arrays.items()]
    args.append(nc.dram_tensor("out", (D, T), F32, kind="ExternalOutput").ap())
    build(nc, *args)
    r = run_bass_kernel_spmd(nc, [arrays], core_ids=[0])
    return r.results[0]["out"].reshape(D, NB, S).transpose(1, 2, 0)
```
